# Optimizing a Trainium2 kernel written in Bass

```python
import numpy as np
import jax
import jax.numpy as jnp

def _softmax(x, axis=-1):
    return jax.nn.softmax(x, axis=axis)

def _gelu(x):
    return jax.nn.gelu(x, approximate=True)

def _silu(x):
    return jax.nn.silu(x)

def _sigmoid(x):
    return jax.nn.sigmoid(x)

def _layernorm(x, axis=-1, eps=1e-05):
    m = jnp.mean(x, axis=axis, keepdims=True)
    v = jnp.var(x, axis=axis, keepdims=True)
    return (x - m) / jnp.sqrt(v + eps)

def _scatter_add(tgt, idx, src, axis=0):
    return tgt.at[idx].add(src)

def _segment_sum(src, seg, n):
    return jax.ops.segment_sum(src, seg, n)
kernel_name = 'mk_gnn_resnorm_d4_gnn_r8_f7c183'

def setup_inputs(seed: int=0):
    np.random.seed(seed)
    _w = jnp.asarray

    def _rec_inputs():
        import jax
        import jax.numpy as jnp
        _gk = jax.random.key(seed)
        x = -0.0005121 + 1.001 * jax.random.normal(jax.random.fold_in(_gk, 1), (12500, 64), jnp.float32)
        src = jax.random.randint(jax.random.fold_in(_gk, 2), (400000,), 0, 12500, jnp.int32)
        dst = jnp.minimum((12500 * jax.random.uniform(jax.random.fold_in(_gk, 3), (400000,)) ** 2.0).astype(jnp.int32), 99999)
        _o = jnp.argsort(dst, stable=True)
        src = src[_o]
        dst = dst[_o]
        edge_attr_6 = 0.00011001 + 1.00018 * jax.random.normal(jax.random.fold_in(_gk, 12), (400000, 6), jnp.float32)
        edge_weight1 = 0.000614103 + 0.999867 * jax.random.normal(jax.random.fold_in(_gk, 14), (400000, 1), jnp.float32)
        return (x, src, dst, edge_attr_6, edge_weight1)
    x, src, dst, edge_attr_6, edge_weight1 = _rec_inputs()

    def _L0_gnn_setup():
        import jax, jax.numpy as jnp
        import numpy as np
        N_NODES = 6250
        N_EDGES = 100000
        DIM = 64
        N_HEADS = 4

        def _scatter_softmax(scores, dst, n_nodes):
            m = jax.ops.segment_max(scores, dst, num_segments=n_nodes)
            m = jnp.maximum(m, jnp.float32(-1000000000.0))
            ex = jnp.exp(scores - m[dst])
            denom = jax.ops.segment_sum(ex, dst, num_segments=n_nodes)
            return ex / (denom[dst] + 1e-09)
        key = jax.random.key(seed)
        ks = jax.random.split(key, 7)
        x = jax.random.normal(ks[0], (N_NODES, DIM), dtype=jnp.float32)
        Wq = jax.random.normal(ks[1], (DIM, DIM), dtype=jnp.float32) / np.sqrt(DIM)
        Wk = jax.random.normal(ks[2], (DIM, DIM), dtype=jnp.float32) / np.sqrt(DIM)
        Wv = jax.random.normal(ks[3], (DIM, DIM), dtype=jnp.float32) / np.sqrt(DIM)
        Wo = jax.random.normal(ks[4], (DIM, DIM), dtype=jnp.float32) / np.sqrt(DIM)
        src = jax.random.randint(ks[5], (N_EDGES,), 0, N_NODES, dtype=jnp.int32)
        dst = jax.random.randint(ks[6], (N_EDGES,), 0, N_NODES, dtype=jnp.int32)
        return {'x': x, 'Wq': Wq, 'Wk': Wk, 'Wv': Wv, 'Wo': Wo, 'src': src, 'dst': dst}
    _L0_gnn_all = _L0_gnn_setup()
    _L0_gnn_in = {k: v for k, v in _L0_gnn_all.items() if k in ('Wq', 'Wk', 'Wv', 'Wo')}
    del _L0_gnn_all

    def _L1_gnn_setup():
        import jax, jax.numpy as jnp
        import numpy as np
        N_NODES = 6250
        DEG = 16
        N_EDGES = N_NODES * DEG
        C_IN = 64
        C_OUT = 64
        key = jax.random.key(seed)
        k_x, k_src, k_ea, k_w, k_b = jax.random.split(key, 5)
        x = jax.random.normal(k_x, (N_NODES, C_IN), dtype=jnp.float32)
        dst = jnp.repeat(jnp.arange(N_NODES, dtype=jnp.int32), DEG)
        src = jax.random.randint(k_src, (N_EDGES,), 0, N_NODES, dtype=jnp.int32)
        edge_index = jnp.stack([src, dst], axis=0)
        edge_attr = jax.random.normal(k_ea, (N_EDGES, 1), dtype=jnp.float32)
        W = jax.random.normal(k_w, (C_OUT, 2 * C_IN), dtype=jnp.float32) * (1.0 / np.sqrt(2 * C_IN))
        b = jax.random.normal(k_b, (C_OUT,), dtype=jnp.float32) * 0.01
        return {'x': x, 'edge_index': edge_index, 'edge_attr': edge_attr, 'W': W, 'b': b}
    _L1_gnn_all = _L1_gnn_setup()
    _L1_gnn_in = {k: v for k, v in _L1_gnn_all.items() if k in ('W', 'b')}
    del _L1_gnn_all

    def _L2_gnn_setup():
        import jax, jax.numpy as jnp
        import numpy as np
        N_NODES = 6250
        N_EDGES = 100000
        D_NODE = 64
        D_EDGE = 6
        HID = 128
        D_OUT = 64
        D_IN = 2 * D_NODE + D_EDGE

        def _linear_init(key, fan_in, fan_out):
            kw, kb = jax.random.split(key)
            bound = 1.0 / np.sqrt(fan_in)
            w = jax.random.uniform(kw, (fan_in, fan_out), jnp.float32, -bound, bound)
            b = jax.random.uniform(kb, (fan_out,), jnp.float32, -bound, bound)
            return (w, b)
        key = jax.random.key(seed)
        ks = jax.random.split(key, 8)
        x = jax.random.normal(ks[0], (N_NODES, D_NODE), jnp.float32)
        edge_index = jax.random.randint(ks[1], (2, N_EDGES), 0, N_NODES, jnp.int64)
        edge_attr = jax.random.normal(ks[2], (N_EDGES, D_EDGE), jnp.float32)
        phi_w1, phi_b1 = _linear_init(ks[3], D_IN, HID)
        phi_w2, phi_b2 = _linear_init(ks[4], HID, D_OUT)
        g_w1, g_b1 = _linear_init(ks[5], 2 * D_OUT, HID)
        g_w2, g_b2 = _linear_init(ks[6], HID, D_OUT)
        return {'x': x, 'edge_index': edge_index, 'edge_attr': edge_attr, 'phi_w1': phi_w1, 'phi_b1': phi_b1, 'phi_w2': phi_w2, 'phi_b2': phi_b2, 'g_w1': g_w1, 'g_b1': g_b1, 'g_w2': g_w2, 'g_b2': g_b2}
    _L2_gnn_all = _L2_gnn_setup()
    _L2_gnn_in = {k: v for k, v in _L2_gnn_all.items() if k in ('phi_w1', 'phi_b1', 'phi_w2', 'phi_b2', 'g_w1', 'g_b1', 'g_w2', 'g_b2')}
    del _L2_gnn_all

    def _L3_gnn_setup():
        import jax, jax.numpy as jnp
        import numpy as np
        N_NODES = 12500
        key = jax.random.key(seed)
        k1, k2, k3, k4 = jax.random.split(key, 4)
        x = jax.random.normal(k1, (N_NODES, 64), dtype=jnp.float32)
        W = jax.random.normal(k2, (64, 64), dtype=jnp.float32) * (1.0 / np.sqrt(64.0))
        src = jax.random.randint(k3, (200000,), 0, N_NODES, dtype=jnp.int32)
        dst = jax.random.randint(k4, (200000,), 0, N_NODES, dtype=jnp.int32)
        return {'x': x, 'W': W, 'src': src, 'dst': dst}
    _L3_gnn_all = _L3_gnn_setup()
    _L3_gnn_in = {k: v for k, v in _L3_gnn_all.items() if k in ('W',)}
    del _L3_gnn_all
    return {'x': x, 'src': src, 'dst': dst, 'edge_attr_6': edge_attr_6, 'edge_weight1': edge_weight1, 'L0_gnn_Wq': _L0_gnn_in['Wq'], 'L0_gnn_Wk': _L0_gnn_in['Wk'], 'L0_gnn_Wv': _L0_gnn_in['Wv'], 'L0_gnn_Wo': _L0_gnn_in['Wo'], 'L1_gnn_W': _L1_gnn_in['W'], 'L1_gnn_b': _L1_gnn_in['b'], 'L2_gnn_phi_w1': _L2_gnn_in['phi_w1'], 'L2_gnn_phi_b1': _L2_gnn_in['phi_b1'], 'L2_gnn_phi_w2': _L2_gnn_in['phi_w2'], 'L2_gnn_phi_b2': _L2_gnn_in['phi_b2'], 'L2_gnn_g_w1': _L2_gnn_in['g_w1'], 'L2_gnn_g_b1': _L2_gnn_in['g_b1'], 'L2_gnn_g_w2': _L2_gnn_in['g_w2'], 'L2_gnn_g_b2': _L2_gnn_in['g_b2'], 'L3_gnn_W': _L3_gnn_in['W']}

def reference(x, src, dst, edge_attr_6, edge_weight1, L0_gnn_Wq, L0_gnn_Wk, L0_gnn_Wv, L0_gnn_Wo, L1_gnn_W, L1_gnn_b, L2_gnn_phi_w1, L2_gnn_phi_b1, L2_gnn_phi_w2, L2_gnn_phi_b2, L2_gnn_g_w1, L2_gnn_g_b1, L2_gnn_g_w2, L2_gnn_g_b2, L3_gnn_W):
    import jax
    import jax.numpy as jnp

    def _L0_gnn_ref(x, Wq, Wk, Wv, Wo, src, dst):
        import jax, jax.numpy as jnp
        import numpy as np
        N_NODES = 6250
        N_EDGES = 100000
        DIM = 64
        N_HEADS = 4

        def _scatter_softmax(scores, dst, n_nodes):
            m = jax.ops.segment_max(scores, dst, num_segments=n_nodes)
            m = jnp.maximum(m, jnp.float32(-1000000000.0))
            ex = jnp.exp(scores - m[dst])
            denom = jax.ops.segment_sum(ex, dst, num_segments=n_nodes)
            return ex / (denom[dst] + 1e-09)
        N, D = x.shape
        H = N_HEADS
        Dh = D // H
        q = (x @ Wq).reshape(N, H, Dh)
        k = (x @ Wk).reshape(N, H, Dh)
        v = (x @ Wv).reshape(N, H, Dh)
        scores = jnp.einsum('ehd,ehd->eh', q[dst], k[src]) / jnp.sqrt(jnp.float32(Dh))
        alpha = _scatter_softmax(scores, dst, N)
        agg = jax.ops.segment_sum(alpha[:, :, None] * v[src], dst, num_segments=N)
        return agg.reshape(N, D) @ Wo

    def _L1_gnn_ref(x, edge_index, edge_attr, W, b):
        import jax, jax.numpy as jnp
        import numpy as np
        N_NODES = 6250
        DEG = 16
        N_EDGES = N_NODES * DEG
        C_IN = 64
        C_OUT = 64
        src = edge_index[0]
        dst = edge_index[1]
        x_i = x[dst]
        x_j = x[src]
        feat = jnp.concatenate([x_i, x_j - x_i], axis=-1)
        msg = jax.nn.relu(feat @ W.T + b)
        out = jax.ops.segment_max(msg, dst, num_segments=x.shape[0])
        return jnp.where(jnp.isneginf(out), 0.0, out)

    def _L2_gnn_ref(x, edge_index, edge_attr, phi_w1, phi_b1, phi_w2, phi_b2, g_w1, g_b1, g_w2, g_b2):
        import jax, jax.numpy as jnp
        import numpy as np
        N_NODES = 6250
        N_EDGES = 100000
        D_NODE = 64
        D_EDGE = 6
        HID = 128
        D_OUT = 64
        D_IN = 2 * D_NODE + D_EDGE

        def _linear_init(key, fan_in, fan_out):
            kw, kb = jax.random.split(key)
            bound = 1.0 / np.sqrt(fan_in)
            w = jax.random.uniform(kw, (fan_in, fan_out), jnp.float32, -bound, bound)
            b = jax.random.uniform(kb, (fan_out,), jnp.float32, -bound, bound)
            return (w, b)
        n = x.shape[0]
        src = edge_index[0]
        dst = edge_index[1]
        x_i = x[dst]
        x_j = x[src]
        m_in = jnp.concatenate([x_i, x_j, edge_attr], axis=1)
        h = jax.nn.elu(m_in @ phi_w1 + phi_b1)
        msg = h @ phi_w2 + phi_b2
        sums = jax.ops.segment_sum(msg, dst, num_segments=n)
        cnts = jax.ops.segment_sum(jnp.ones((msg.shape[0], 1), msg.dtype), dst, num_segments=n)
        aggr = sums / jnp.maximum(cnts, 1.0)
        u_in = jnp.concatenate([x, aggr], axis=1)
        g = jax.nn.elu(u_in @ g_w1 + g_b1)
        return g @ g_w2 + g_b2

    def _L3_gnn_ref(x, W, src, dst):
        import jax, jax.numpy as jnp
        import numpy as np
        N_NODES = 12500
        n = x.shape[0]
        ones = jnp.ones(src.shape[0], dtype=x.dtype)
        out_deg = jax.ops.segment_sum(ones, src, num_segments=n)
        in_deg = jax.ops.segment_sum(ones, dst, num_segments=n)
        norm_src = jnp.power(jnp.clip(out_deg, 1.0, None), -0.5)
        norm_dst = jnp.power(jnp.clip(in_deg, 1.0, None), -0.5)
        feat = x * norm_src[:, None]
        msgs = feat[src]
        agg = jax.ops.segment_sum(msgs, dst, num_segments=n)
        agg = agg * norm_dst[:, None]
        return agg @ W
    edge_index = jnp.stack([src, dst])
    x = _layernorm(x + _L0_gnn_ref(x, L0_gnn_Wq, L0_gnn_Wk, L0_gnn_Wv, L0_gnn_Wo, src, dst), axis=-1)
    x = _layernorm(x + _L1_gnn_ref(x, edge_index, edge_weight1, L1_gnn_W, L1_gnn_b), axis=-1)
    x = _layernorm(x + _L2_gnn_ref(x, edge_index, edge_attr_6, L2_gnn_phi_w1, L2_gnn_phi_b1, L2_gnn_phi_w2, L2_gnn_phi_b2, L2_gnn_g_w1, L2_gnn_g_b1, L2_gnn_g_w2, L2_gnn_g_b2), axis=-1)
    x = _layernorm(x + _L3_gnn_ref(x, L3_gnn_W, src, dst), axis=-1)
    return x

_drawn_inputs = setup_inputs


def setup_inputs(seed=0):
    import zlib

    import numpy as np

    out = dict(_drawn_inputs(seed))
    spreads = {}
    factors = {'edge_attr_6': 24.336, 'L1_gnn_b': 5.937, 'L2_gnn_phi_b1': 7.621, 'L2_gnn_phi_b2': 4.872}
    for name, (base, spread) in spreads.items():
        noise = np.random.default_rng([zlib.crc32(name.encode()), seed]).standard_normal(out[name].shape)
        drawn = base * np.exp(spread * noise) if base else spread * noise
        out[name] = jnp.asarray(drawn.astype(out[name].dtype))
    for name, factor in factors.items():
        out[name] = (out[name] * factor).astype(out[name].dtype)
    return out
```

```python
import concourse.bass as bass
from concourse import mybir
from contextlib import ExitStack, contextmanager

P = 128
D = 64
HEADS = 4
HID = 128
EA = 6
T = 50
G = 10
BLK = 10
BIG = 1.0e30
SKIP = 8.0e6
MAGIC = 12582912.0
EPS = 1e-5


def build(nc, x_in, src_in, dst_in, ea_in, wkvq_parts, wo_in, w1t_in, b1_in, pw1_in, pb1_in, pw2_in, pb2_in,
          gw1_in, gb1_in, gw2_in, gb2_in, w3_in, out):
    f32, bf16, i32 = mybir.dt.float32, mybir.dt.bfloat16, mybir.dt.int32
    ALU, ACT, AX = mybir.AluOpType, mybir.ActivationFunctionType, mybir.AxisListType
    ds = bass.ds

    N = x_in.shape[0]
    E = src_in.shape[0]
    TALL = E // P
    PAIRS = TALL // (2 * T)
    TAIL = TALL - 2 * PAIRS * T
    assert E == P * TALL and 0 < TAIL <= T and TAIL % 5 == 0
    J = -(-N // P)
    J = -(-J // (2 * G)) * 2 * G
    NPART = N // J
    assert N == NPART * J and NPART <= P
    NPAD = P * J
    GPAIRS = J // (2 * G)

    def dram(name, shape, dt=f32):
        return nc.dram_tensor(name, list(shape), dt, kind="Internal").ap()

    x_d = [dram(f"x_layer{n}", (NPAD, D)) for n in range(3)]
    kv_d = dram("kv_table", (NPAD, 2 * D))
    q_d = dram("q_table", (NPAD, D))
    own1_d = dram("edgeconv_own", (NPAD, D))
    nbr1_d = dram("edgeconv_neighbour_table", (NPAD, D))
    own2_d = dram("mlp_own_table", (NPAD, HID))
    nbr2_d = dram("mlp_neighbour_table", (NPAD, HID))
    feat_d = dram("gcn_table", (NPAD, D))
    qstart_d = dram("q_at_first_edges", (E, D))
    pstart_d = dram("mlp_own_at_first_edges", (E, HID))
    ROW0 = D + 2 * HEADS
    scan_d = [dram("scan_attention", (E, ROW0)), dram("scan_max", (E, D)), dram("scan_mlp", (E, HID)),
              dram("scan_gcn", (E, D))]
    last_d = dram("last_edge", (NPAD, 1), i32)
    first_d = dram("first_edge", (NPAD, 1), i32)

    def nodes(ap):
        return ap.rearrange("(p j) f -> p j f", p=P)

    def edges(ap):
        return ap.rearrange("(p t) f -> p t f", p=P)

    src_v = src_in.rearrange("(p t) -> p t", p=P)
    dst_v = dst_in.rearrange("(p t) -> p t", p=P)
    ea_v = edges(ea_in)

    ctx = ExitStack()
    ctx.enter_context(nc.allow_non_contiguous_dma(reason="columns of small tables"))

    def bc(ap, dim, n):
        wide = ap.unsqueeze(dim)
        shape = list(wide.shape)
        shape[dim] = n
        return wide.broadcast_to(shape)

    class Steps:

        def __init__(self, eng, sem, base=0):
            self.eng, self.sem, self.base, self.n = eng, sem, base, 0

        def step(self, ins):
            ins.then_inc(self.sem, 1)
            self.n += 1

        def wait(self):
            self.eng.wait_ge(self.sem, self.base + self.n)

        def link(self, ins):
            self.step(ins)
            self.wait()

    with ctx:
        phase_sems = []

        def sem(name):
            phase_sems.append(nc.alloc_semaphore(name=name))
            return phase_sems[-1]

        @contextmanager
        def phase(name):
            with ExitStack() as scope:
                with nc.Block(name) as block:
                    yield scope, block
            nc.clear_and_free_semaphores(phase_sems)
            phase_sems.clear()
            nc.all_engine_barrier()

        def maker(scope):
            def sb(name, shape, dt=f32):
                return scope.enter_context(nc.sbuf_tensor(name, list(shape), dt))

            def ps(name, shape, dt=f32):
                return scope.enter_context(nc.psum_tensor(name, list(shape), dt))
            return sb, ps

        sb, _ = maker(ctx)
        keep = sb("keep", [P, (2 * PAIRS + 1) * T])
        pen = sb("pen", [P, TALL])
        ident = sb("ident", [P, P])
        iota_row = sb("iota_row", [P, P], bf16)
        cnt_in = sb("cnt_in", [P, J])
        nonempty = sb("nonempty", [P, J])
        rcnt = sb("rcnt", [P, J])
        nsrc = sb("nsrc", [P, J])
        ndst = sb("ndst", [P, J])
        whole = sb("whole", [P, 1])
        fixidx = sb("fixidx", [P, 1], i32)
        qcarry = sb("qcarry", [P, D])
        pcarry = sb("pcarry", [P, HID])
        dfirst = sb("dfirst", [P, 1], i32)

        with phase("setup") as (scope, block):
            sb, ps = maker(scope)
            HG = 25
            HPAIRS = TALL // (2 * HG)
            HODD = TALL // HG - 2 * HPAIRS
            assert TALL % HG == 0
            dstx = sb("dstx", [P, TALL + 1], i32)
            hi32 = sb("hi32", [P, TALL])
            hi = sb("hi", [P, TALL], bf16)
            lo = sb("lo", [P, TALL], bf16)
            ohi = [sb(f"ohi{b}", [P, HG, P], bf16) for b in range(2)]
            olo = [sb(f"olo{b}", [P, HG, J], bf16) for b in range(2)]
            zrow = sb("zrow", [P, P], bf16)
            iota32 = sb("iota32", [P, P], i32)
            tri = sb("tri", [P, P])
            onesJ = sb("onesJ", [P, J])
            cum = sb("cum", [P, J])
            tmpJ = sb("tmpJ", [P, J])
            tmpK = sb("tmpK", [P, J])
            firsti = sb("firsti", [P, J], i32)
            lasti = sb("lasti", [P, J], i32)
            base = sb("base", [P, 1])
            zeros = sb("zeros", [P, T * D])
            xg = [sb(f"xg{b}", [P, G, D]) for b in range(2)]
            wkvq = sb("wkvq", [P, 2, 3 * D])
            xT = sb("xT", [P, G // 2, P])
            kv_s = sb("kv_s", [P, G, 2 * D])
            q_s = sb("q_s", [P, G, D])
            p_tr = ps("p_tr", [P, 1024])
            p_mm = ps("p_mm", [P, 5, 512])
            p_h = ps("p_h", [P, 512])

            s_w, s_dst, s_z, s_dmin, s_const, s_id = (sem(n) for n in ("su_w", "su_dst", "su_zero", "su_min", "su_const", "su_id"))
            s_x = [sem(f"su_x{b}") for b in range(2)]
            s_xz, s_tr, s_xt, s_mm, s_tab, s_st, s_oh, s_hm, s_v, s_tot, s_base, s_fl, s_fill, s_deg = (
                sem("su_" + n) for n in ("xz", "tr", "xt", "mm", "tab", "st", "oh", "hm", "v", "tot", "base", "fl", "fill", "deg"))

            @block.sync
            def _(sp):
                sp.dma_start(dstx[:, 1:TALL + 1], dst_v).then_inc(s_dst, 16)
                sp.wait_ge(s_dmin, 1)
                sp.dma_start(dstx[1:P, 0:1], dst_v[0:P - 1, TALL - 1:TALL]).then_inc(s_dst, 16)
                sp.wait_ge(s_xz, 1)
                for h in range(2):
                    for n, w in enumerate(wkvq_parts):
                        sp.dma_start(wkvq[h * D:(h + 1) * D, h, n * D:(n + 1) * D], w).then_inc(s_w, 16)
                xv = x_in.rearrange("(p j) f -> p j f", j=J)

                def load_x(g, b):
                    sp.dma_start(xg[b][0:NPART], xv[:, ds(g * G, G), :]).then_inc(s_x[b], 16)

                def store(g):
                    sp.wait_ge(s_tab, g * 2 + 2)
                    sp.dma_start(nodes(kv_d)[:, ds(g * G, G), :], kv_s[:]).then_inc(s_st, 16)
                    sp.dma_start(nodes(q_d)[:, ds(g * G, G), :], q_s[:]).then_inc(s_st, 16)
                load_x(0, 0)
                load_x(1, 1)
                if GPAIRS > 1:
                    with nc.Fori(0, GPAIRS - 1, engines=[nc.sync.engine]) as i:
                        for b in range(2):
                            store(i * 2 + b)
                            load_x(i * 2 + b + 2, b)
                for b in range(2):
                    store(2 * GPAIRS - 2 + b)
                sp.wait_ge(s_z, 1)
                with nc.Fori(0, 2 * PAIRS, engines=[nc.sync.engine]) as i:
                    sp.dma_start(edges(qstart_d)[:, ds(i * T, T), :], zeros[:].rearrange("p (t f) -> p t f", f=D)).then_inc(s_fill, 16)
                sp.dma_start(edges(qstart_d)[:, 2 * PAIRS * T:TALL, :],
                             zeros[:, 0:TAIL * D].rearrange("p (t f) -> p t f", f=D)).then_inc(s_fill, 16)
                sp.wait_ge(s_fl, 2)
                sp.dma_start(nodes(first_d)[:, :, 0], firsti[:]).then_inc(s_st, 16)
                sp.dma_start(nodes(last_d)[:, :, 0], lasti[:]).then_inc(s_st, 16)
                sp.wait_ge(s_fill, 16 * (2 * PAIRS + 1))
                sp.wait_ge(s_st, 16 * (4 * GPAIRS + 2))

            @block.gpsimd
            def _(pool):
                nc.gpsimd.iota(iota32[:], pattern=[[1, P]], base=0, channel_multiplier=0).then_inc(s_id, 1)
                nc.gpsimd.memset(ident[:], 0.0).then_inc(s_id, 1)
                nc.gpsimd.memset(tri[:], 1.0).then_inc(s_id, 1)
                pool.wait_ge(s_id, 3)
                nc.gpsimd.affine_select(out=ident[:], in_=ident[:], compare_op=ALU.not_equal, fill=1.0,
                                        base=0, pattern=[[-1, P]], channel_multiplier=1).then_inc(s_id, 1)
                nc.gpsimd.affine_select(out=tri[:], in_=tri[:], compare_op=ALU.is_gt, fill=0.0,
                                        base=0, pattern=[[1, P]], channel_multiplier=-1).then_inc(s_id, 1)

            @block.vector
            def _(dve):
                st = Steps(dve, s_v)
                nc.vector.memset(dstx[:, 0:1], -1).then_inc(s_dmin, 1)
                st.step(nc.vector.memset(xg[0][:], 0.0))
                st.step(nc.vector.memset(xg[1][:], 0.0))
                st.step(nc.vector.memset(wkvq[:], 0.0))
                st.wait()
                dve.sem_inc(s_xz, 1)
                nc.vector.memset(zeros[:], 0.0).then_inc(s_z, 1)
                st.step(nc.vector.memset(zrow[:], 0.0))
                st.step(nc.vector.memset(onesJ[:], 1.0))
                st.step(nc.vector.memset(keep[:], 0.0))
                dve.wait_ge(s_id, 1)
                st.step(nc.vector.tensor_copy(iota_row[:], iota32[:]))
                st.wait()
                dve.sem_inc(s_const, 1)
                dve.wait_ge(s_dst, 32)
                st.link(nc.vector.tensor_scalar(hi32[:], dstx[:, 1:TALL + 1], -(J - 1) / 2, 1.0 / J, ALU.add, ALU.mult))
                st.link(nc.vector.tensor_scalar(hi32[:], hi32[:], MAGIC, -MAGIC, ALU.add, ALU.add))
                st.step(nc.vector.tensor_copy(hi[:], hi32[:]))
                st.step(nc.vector.scalar_tensor_tensor(lo[:], hi32[:], -float(J), dstx[:, 1:TALL + 1], ALU.mult, ALU.add))
                st.step(nc.vector.tensor_copy(dfirst[:], dstx[:, 1:2]))
                st.link(nc.vector.tensor_tensor(keep[:, 0:TALL], dstx[:, 1:TALL + 1], dstx[:, 0:TALL], ALU.is_equal))
                st.link(nc.vector.tensor_scalar(pen[:], keep[:, 0:TALL], -1.0, BIG, ALU.add, ALU.mult))

                def onehots(c, b):
                    nc.vector.tensor_tensor(ohi[b][:], bc(hi[:, ds(c * HG, HG)], 2, P), bc(iota_row[:], 1, HG), ALU.is_equal)
                    nc.vector.tensor_tensor(olo[b][:], bc(lo[:, ds(c * HG, HG)], 2, J), bc(iota_row[:, 0:J], 1, HG),
                                            ALU.is_equal).then_inc(s_oh, 1)
                onehots(0, 0)
                onehots(1, 1)
                with nc.Fori(1, HPAIRS, engines=[nc.vector.engine]) as i:
                    for b in range(2):
                        dve.wait_ge(s_hm, i * 2 + b - 1)
                        onehots(i * 2 + b, b)
                if HODD:
                    dve.wait_ge(s_hm, 2 * HPAIRS - 1)
                    onehots(2 * HPAIRS, 0)
                dve.wait_ge(s_hm, 2 * HPAIRS + HODD)
                st.link(nc.vector.tensor_copy(cnt_in[:], p_h[:, 0:J]))
                nc.vector.tensor_tensor_scan(cum[:], onesJ[:], cnt_in[:], 0.0, ALU.mult, ALU.add).then_inc(s_tot, 1)
                st.step(nc.vector.tensor_scalar(nonempty[:], cnt_in[:], 0.0, None, ALU.is_gt))
                st.link(nc.vector.tensor_scalar(tmpJ[:], cnt_in[:], 1.0, None, ALU.max))
                dve.sem_inc(s_deg, 1)
                st.step(nc.vector.reciprocal(rcnt[:], tmpJ[:]))
                dve.wait_ge(s_base, 1)
                st.link(nc.vector.tensor_copy(base[:], p_h[:, 0:1]))
                st.link(nc.vector.tensor_scalar(cum[:], cum[:], base[:, 0:1], -1.0, ALU.add, ALU.add))
                st.step(nc.vector.tensor_tensor(tmpK[:], cum[:], cnt_in[:], ALU.subtract))
                nc.vector.tensor_scalar(lasti[:], cum[:], 0.0, None, ALU.max).then_inc(s_fl, 1)
                st.wait()
                st.link(nc.vector.tensor_scalar(tmpK[:], tmpK[:], 1.0 - SKIP, None, ALU.add))
                st.link(nc.vector.tensor_tensor(tmpK[:], tmpK[:], nonempty[:], ALU.mult))
                nc.vector.tensor_scalar(firsti[:], tmpK[:], SKIP, None, ALU.add).then_inc(s_fl, 1)

            @block.scalar
            def _(act):
                def evac(g):
                    act.wait_ge(s_tr, g + 1)
                    nc.scalar.activation(xT[:], p_tr[:, 0:G * D].rearrange("p (k n) -> p k n", n=P), ACT.Copy).then_inc(s_xt, 1)
                    act.wait_ge(s_mm, g + 1)
                    act.wait_ge(s_st, g * 32)
                    mm = p_mm[:, :, 0:6 * D].rearrange("p k (h f) -> p k h f", h=2)
                    nc.scalar.activation(kv_s[:].rearrange("p (k h) f -> p k h f", h=2), mm[:, :, :, 0:2 * D], ACT.Copy).then_inc(s_tab, 1)
                    nc.scalar.activation(q_s[:].rearrange("p (k h) f -> p k h f", h=2), mm[:, :, :, 2 * D:3 * D], ACT.Copy,
                                         scale=(D // HEADS) ** -0.5).then_inc(s_tab, 1)
                with nc.Fori(0, 2 * GPAIRS, engines=[nc.scalar.engine]) as g:
                    evac(g)
                act.wait_ge(s_deg, 1)
                nc.scalar.activation(ndst[:], tmpJ[:], ACT.Sqrt).then_inc(s_deg, 1)

            @block.tensor
            def _(pe):
                pe.wait_ge(s_id, 5)
                pe.wait_ge(s_w, 96)

                def tables(g, i, b):
                    pe.wait_ge(s_x[b], i * 16 + 16)
                    for k in range(G // 2):
                        tr = nc.tensor.transpose(p_tr[:, k * P:(k + 1) * P], xg[b][:, 2 * k:2 * k + 2, :].rearrange("p h f -> p (h f)"), ident[:])
                    tr.then_inc(s_tr, 1)
                    pe.wait_ge(s_tab, g * 2)
                    pe.wait_ge(s_xt, g + 1)
                    for k in range(G // 2):
                        mm = nc.tensor.matmul(p_mm[:, k, 0:6 * D], xT[:, k, :], wkvq[:].rearrange("p h f -> p (h f)"), start=True, stop=True)
                    mm.then_inc(s_mm, 1)
                with nc.Fori(0, GPAIRS, engines=[nc.tensor.engine]) as i:
                    for b in range(2):
                        tables(i * 2 + b, i, b)
                pe.wait_ge(s_const, 1)
                nc.tensor.matmul(p_h[:, 0:J], zrow[:], zrow[:, 0:J], start=True, stop=False)

                def count(c, b, last=False):
                    pe.wait_ge(s_oh, c + 1)
                    for t in range(HG):
                        mm = nc.tensor.matmul(p_h[:, 0:J], ohi[b][:, t, :], olo[b][:, t, :], start=False, stop=last and t == HG - 1)
                    mm.then_inc(s_hm, 1)
                with nc.Fori(0, HPAIRS - 1, engines=[nc.tensor.engine]) as i:
                    for b in range(2):
                        count(i * 2 + b, b)
                for b in range(2):
                    count(2 * HPAIRS - 2 + b, b, last=(not HODD and b == 1))
                if HODD:
                    count(2 * HPAIRS, 0, last=True)
                pe.wait_ge(s_tot, 1)
                nc.tensor.matmul(p_h[:, 0:1], tri[:], cum[:, J - 1:J], start=True, stop=True).then_inc(s_base, 1)

        def scatter_rows(name, rows_d, start_d, width, carry, with_bounds):
            with phase(name) as (scope, block):
                sb, ps = maker(scope)
                idx = [sb(f"{name}_idx{b}", [P, G], i32) for b in range(2)]
                row = [sb(f"{name}_row{b}", [P, G, width]) for b in range(2)]
                lastf = sb(f"{name}_last", [P, 1], i32)
                t = sb(f"{name}_t", [P, 4])
                pidx = sb(f"{name}_p", [P, 2], i32)
                s_in = [sem(f"{name}_in{b}") for b in range(2)]
                s_sc = [sem(f"{name}_sc{b}") for b in range(2)]
                s_g, s_v, s_io, s_turn = sem(f"{name}_g"), sem(f"{name}_v"), sem(f"{name}_io"), sem(f"{name}_turn")

                @block.sync
                def _(sp):
                    def load(g, b):
                        sp.dma_start(idx[b][:], nodes(first_d)[:, ds(g * G, G), 0]).then_inc(s_in[b], 16)
                        sp.dma_start(row[b][:], nodes(rows_d)[:, ds(g * G, G), :]).then_inc(s_in[b], 16)
                    load(0, 0)
                    load(1, 1)
                    if GPAIRS > 1:
                        with nc.Fori(1, GPAIRS, engines=[nc.sync.engine]) as i:
                            for b in range(2):
                                sp.wait_ge(s_sc[b], i * (16 * G))
                                load(i * 2 + b, b)

                @block.gpsimd
                def _(pool):
                    nc.gpsimd.indirect_dma_start(carry[:], None, rows_d, bass.IndirectOffsetOnAxis(ap=dfirst[:, 0:1], axis=0)).then_inc(s_g, 16)
                    if with_bounds:
                        nc.gpsimd.indirect_dma_start(lastf[:], None, last_d, bass.IndirectOffsetOnAxis(ap=dfirst[:, 0:1], axis=0)).then_inc(s_g, 16)
                        nc.gpsimd.iota(pidx[:, 0:1], pattern=[[1, 1]], base=0, channel_multiplier=TALL).then_inc(s_io, 1)
                    else:
                        pool.sem_inc(s_io, 1)
                    with nc.Fori(0, GPAIRS, engines=[nc.gpsimd.engine]) as i:
                        for b in range(2):
                            pool.wait_ge(s_in[b], i * 32 + 32)
                            pool.sem_inc(s_turn, 1)
                            for j in range(G):
                                nc.gpsimd.indirect_dma_start(start_d, bass.IndirectOffsetOnAxis(ap=idx[b][:, j:j + 1], axis=0),
                                                             row[b][:, j, :], None, bounds_check=E - 1, oob_is_err=False).then_inc(s_sc[b], 16)
                    pool.wait_ge(s_sc[0], GPAIRS * 16 * G)
                    pool.wait_ge(s_sc[1], GPAIRS * 16 * G)
                    pool.wait_ge(s_g, 32 if with_bounds else 16)

                if with_bounds:
                    @block.vector
                    def _(dve):
                        st = Steps(dve, s_v)
                        dve.wait_ge(s_g, 32)
                        dve.wait_ge(s_io, 1)
                        st.step(nc.vector.tensor_copy(t[:, 0:1], lastf[:]))
                        st.link(nc.vector.tensor_copy(t[:, 1:2], pidx[:, 0:1]))
                        st.link(nc.vector.tensor_tensor(t[:, 2:3], t[:, 0:1], t[:, 1:2], ALU.subtract))
                        st.link(nc.vector.tensor_scalar(whole[:], t[:, 2:3], float(TALL - 1), None, ALU.is_ge))
                        st.link(nc.vector.tensor_tensor(whole[:], whole[:], keep[:, 0:1], ALU.mult))
                        st.link(nc.vector.tensor_scalar(t[:, 3:4], t[:, 2:3], float(TALL - 1), None, ALU.is_le))
                        st.link(nc.vector.tensor_tensor(t[:, 3:4], t[:, 3:4], keep[:, 0:1], ALU.mult))
                        st.link(nc.vector.tensor_scalar(t[:, 0:1], t[:, 0:1], -SKIP, None, ALU.add))
                        st.link(nc.vector.tensor_tensor(t[:, 0:1], t[:, 0:1], t[:, 3:4], ALU.mult))
                        st.link(nc.vector.tensor_scalar(fixidx[:], t[:, 0:1], SKIP, None, ALU.add))
                        st.link(nc.vector.reciprocal(ndst[:], ndst[:]))

        scatter_rows("scatter_q", q_d, qstart_d, D, qcarry, True)

        def pool_gathers(pool, table, idx, rows, s_idx, s_free, s_rows, s_turn):
            def chunk(b, i, width):
                pool.wait_ge(s_idx[b], i * 16 + 16)
                pool.wait_ge(s_free[b], i + 1)
                pool.sem_inc(s_turn, 1)
                for t in range(width):
                    nc.gpsimd.indirect_dma_start(rows[b][:, t, :], None, table,
                                                 bass.IndirectOffsetOnAxis(ap=idx[b][:, t:t + 1], axis=0)).then_inc(s_rows[b], 16)
            with nc.Fori(0, PAIRS, engines=[nc.gpsimd.engine]) as i:
                for b in range(2):
                    chunk(b, i, T)
            chunk(0, PAIRS, TAIL)

        def boundary(name, last, scan_out, width, op, none):
            with phase(name) as (scope, block):
                sb, ps = maker(scope)
                gate = sb(f"{name}_gate", [P, width])
                carry = sb(f"{name}_carry", [P, width])
                rows = sb(f"{name}_rows", [P, width])
                gateT = sb(f"{name}_gateT", [width, P])
                runT = sb(f"{name}_runT", [width, P + 1])
                pa, pb, pc = ps(f"{name}_pa", [P, 512]), ps(f"{name}_pb", [P, 512]), ps(f"{name}_pc", [P, 512])
                s_v, s_t, s_g, s_s, s_m = (sem(f"{name}_{n}") for n in ("v", "t", "g", "s", "m"))
                first = ALU.mult if op == ALU.add else ALU.add

                @block.vector
                def _(dve):
                    st = Steps(dve, s_v)
                    nc.vector.memset(rows[:], 0.0).then_inc(s_m, 1)
                    st.step(nc.vector.memset(runT[:, 0:1], none))
                    if op == ALU.add:
                        st.step(nc.vector.tensor_copy(gate[:], bc(whole[:, 0], 1, width)))
                    else:
                        st.step(nc.vector.tensor_scalar(gate[:], bc(whole[:, 0], 1, width), -1.0, BIG, ALU.add, ALU.mult))
                    dve.wait_ge(s_t, 2)
                    st.link(nc.vector.tensor_copy(gateT[:], pa[0:width, 0:P]))
                    nc.vector.tensor_tensor_scan(runT[:, 1:P + 1], gateT[:], pb[0:width, 0:P], none, first, op).then_inc(s_v, 1)
                    dve.wait_ge(s_t, 3)
                    st.n += 1
                    st.link(nc.vector.tensor_copy(carry[:], pc[:, 0:width]))
                    dve.wait_ge(s_g, 16)
                    nc.vector.tensor_tensor(rows[:], rows[:], carry[:], op).then_inc(s_m, 1)

                @block.tensor
                def _(pe):
                    pe.wait_ge(s_v, 2)
                    nc.tensor.transpose(pa[0:width, 0:P], gate[:], ident[:]).then_inc(s_t, 1)
                    nc.tensor.transpose(pb[0:width, 0:P], last, ident[:]).then_inc(s_t, 1)
                    pe.wait_ge(s_v, 4)
                    nc.tensor.transpose(pc[:, 0:width], runT[:, 0:P], ident[0:width, 0:width]).then_inc(s_t, 1)

                @block.gpsimd
                def _(pool):
                    pool.wait_ge(s_m, 1)
                    nc.gpsimd.indirect_dma_start(rows[:], None, scan_out, bass.IndirectOffsetOnAxis(ap=fixidx[:, 0:1], axis=0),
                                                 bounds_check=E - 1, oob_is_err=False).then_inc(s_g, 16)
                    pool.wait_ge(s_m, 2)
                    nc.gpsimd.indirect_dma_start(scan_out, bass.IndirectOffsetOnAxis(ap=fixidx[:, 0:1], axis=0), rows[:], None,
                                                 bounds_check=E - 1, oob_is_err=False).then_inc(s_s, 16)
                    pool.wait_ge(s_s, 16)

        def node_block(name, layer, scan_out, width, x_prev, own_d=None):
            with phase(name) as (scope, block):
                sb, ps = maker(scope)
                def t(n, shape, dt=f32):
                    return sb(f"{name}_{n}", shape, dt)
                idx = [t(f"idx{b}", [P, G], i32) for b in range(2)]
                agg = [t(f"agg{b}", [P, G, width]) for b in range(2)]
                xg = [t(f"x{b}", [P, G, D]) for b in range(2)]
                own = [t(f"own{b}", [P, G, D]) for b in range(2)] if own_d is not None else None
                y = t("y", [P, G, D])
                sq = t("sq", [P, G, D])
                s1, s2 = t("s1", [P, G]), t("s2", [P, G])
                rt = t("rt", [P, G])
                xn = t("xn", [P, G, D])
                aT = t("aT", [P, G // 2, P])
                p_tr = ps(f"{name}_ptr", [P, 3, 512])
                p_mm = ps(f"{name}_pmm", [P, 5, 512])
                s_in = [sem(f"{name}_in{b}") for b in range(2)]
                s_ag = [sem(f"{name}_ag{b}") for b in range(2)]
                s_v, s_a, s_tr, s_ev, s_mm, s_xn, s_sq, s_rt, s_tab, s_st, s_w, s_open, s_used, s_turn = (
                    sem(f"{name}_{n}") for n in ("v", "a", "tr", "ev", "mm", "xn", "sq", "rt", "tab", "st", "w", "open", "used", "turn"))
                diagonal = []
                if layer == 0:
                    w_out, w_next, bias_next = t("wo", [P, 2, D]), t("wn", [P, 2, 2 * D]), t("bn", [P, D])
                    loads = [(w_out[h * D:(h + 1) * D, h, :], wo_in) for h in range(2)]
                    wa, wb = t("wa", [P, 2, D]), t("wb", [P, 2, D])
                    loads += [(wa[h * D:(h + 1) * D, h, :], w1t_in[0:D, :]) for h in range(2)]
                    loads += [(wb[h * D:(h + 1) * D, h, :], w1t_in[D:2 * D, :]) for h in range(2)]
                    diagonal = [w_out, wa, wb]
                    loads += [(bias_next[:], bc(b1_in, 0, P))]
                    NT, tabs = 2 * D, (own1_d, nbr1_d)
                    own_s, nbr_s = t("own_s", [P, G, D]), t("nbr_s", [P, G, D])
                    f4, g4, h4 = t("f4", [P, G, HEADS]), t("g4", [P, G, HEADS]), t("h4", [P, G, HEADS])
                    a = t("a", [P, G, D])
                elif layer == 1:
                    w_next, bias_next = t("wn", [P, 2, 2 * HID]), t("bn", [P, HID])
                    diagonal = [w_next]
                    loads = [(w_next[h * D:(h + 1) * D, h, n * HID:(n + 1) * HID], pw1_in[n * D:(n + 1) * D, :]) for h in range(2) for n in range(2)]
                    loads += [(bias_next[:], bc(pb1_in, 0, P))]
                    NT, tabs = 2 * HID, (own2_d, nbr2_d)
                    own_s, nbr_s = t("own_s", [P, G, HID]), t("nbr_s", [P, G, HID])
                    a = y
                elif layer == 2:
                    wp2, wg1, wg2 = t("wp2", [HID, D]), t("wg1", [P, HID]), t("wg2", [HID, D])
                    bp2, bg1, bg2 = t("bp2", [P, D]), t("bg1", [HID, 1]), t("bg2", [P, D])
                    loads = [(wp2[:], pw2_in), (wg1[:], gw1_in), (wg2[:], gw2_in), (bp2[:], bc(pb2_in, 0, P)),
                             (bg1[:], gb1_in.unsqueeze(1)), (bg2[:], bc(gb2_in, 0, P))]
                    a = t("a", [P, G, HID])
                    aTw = t("aTw", [P, G, P])
                    u = t("u", [P, G, 2 * D])
                    be, br = t("be", [P, G, P]), t("br", [P, G, P])
                    NT, tabs = 0, (feat_d,)
                    own_s = t("own_s", [P, G, D])
                else:
                    w_out = t("wo", [P, 2, D])
                    diagonal = [w_out]
                    loads = [(w_out[h * D:(h + 1) * D, h, :], w3_in) for h in range(2)]
                    a = t("a", [P, G, D])
                    NT, tabs = 0, ()
                PS_TAB = {0: (0, 1, 2, 3), 1: (0, 1, 2, 3, 4)}.get(layer)
                x_v = x_in.rearrange("(p j) f -> p j f", j=J) if layer == 0 else nodes(x_prev)
                out_v = out.rearrange("(p j) f -> p j f", j=J)
                NXP = NPART if layer == 0 else P
                n_in = 2 + (own_d is not None)
                n_st = {0: 3, 1: 3, 2: 2, 3: 1}[layer]
                n_ev = {0: 1, 1: 0, 2: 2, 3: 1}[layer] + (1 if layer < 2 else 0)

                @block.sync
                def _(sp):
                    sp.wait_ge(s_open, 1)
                    for o, w in loads:
                        sp.dma_start(o, w).then_inc(s_w, 16)

                    def load(g, b):
                        sp.dma_start(idx[b][:], nodes(last_d)[:, ds(g * G, G), 0]).then_inc(s_in[b], 16)
                        sp.dma_start(xg[b][0:NXP], x_v[:, ds(g * G, G), :]).then_inc(s_in[b], 16)
                        if own_d is not None:
                            sp.dma_start(own[b][:], nodes(own_d)[:, ds(g * G, G), :]).then_inc(s_in[b], 16)

                    def store(g):
                        sp.wait_ge(s_xn, g + 1)
                        if layer == 3:
                            sp.dma_start(out_v[:, ds(g * G, G), :], xn[0:NPART]).then_inc(s_st, 16)
                        else:
                            sp.dma_start(nodes(x_d[layer])[:, ds(g * G, G), :], xn[:]).then_inc(s_st, 16)
                        if layer < 2:
                            sp.wait_ge(s_tab, g * 2 + 2)
                            sp.dma_start(nodes(tabs[0])[:, ds(g * G, G), :], own_s[:]).then_inc(s_st, 16)
                            sp.dma_start(nodes(tabs[1])[:, ds(g * G, G), :], nbr_s[:]).then_inc(s_st, 16)
                        if layer == 2:
                            sp.wait_ge(s_tab, g + 1)
                            sp.dma_start(nodes(tabs[0])[:, ds(g * G, G), :], own_s[:]).then_inc(s_st, 16)
                    load(0, 0)
                    load(1, 1)
                    if GPAIRS > 1:
                        with nc.Fori(0, GPAIRS - 1, engines=[nc.sync.engine]) as i:
                            for b in range(2):
                                store(i * 2 + b)
                                load(i * 2 + b + 2, b)
                    for b in range(2):
                        store(2 * GPAIRS - 2 + b)
                    sp.wait_ge(s_st, 16 * n_st * 2 * GPAIRS)

                @block.gpsimd
                def _(pool):
                    with nc.Fori(0, GPAIRS, engines=[nc.gpsimd.engine]) as i:
                        for b in range(2):
                            pool.wait_ge(s_in[b], i * (16 * n_in) + 16 * n_in)
                            pool.wait_ge(s_used, i * 2 + b + 1)
                            pool.sem_inc(s_turn, 1)
                            for j in range(G):
                                nc.gpsimd.indirect_dma_start(agg[b][:, j, :], None, scan_out,
                                                             bass.IndirectOffsetOnAxis(ap=idx[b][:, j:j + 1], axis=0)).then_inc(s_ag[b], 16)

                @block.vector
                def _(dve):
                    st = Steps(dve, s_v)
                    st.step(nc.vector.memset(xg[0][:], 0.0))
                    st.step(nc.vector.memset(xg[1][:], 0.0))
                    for w in diagonal:
                        st.step(nc.vector.memset(w[:], 0.0))
                    st.wait()
                    dve.sem_inc(s_open, 1)
                    dve.sem_inc(s_used, 2)
                    dve.wait_ge(s_w, 16 * len(loads))
                    if layer == 0:
                        st.step(nc.vector.tensor_tensor(w_next[:, :, 0:D], wa[:], wb[:], ALU.subtract))
                        st.step(nc.vector.tensor_copy(w_next[:, :, D:2 * D], wb[:]))
                        st.wait()
                    dve.sem_inc(s_w, 16)
                    setup = st.n
                    K = {0: 18, 1: 12, 2: 19, 3: 10}[layer]

                    def group(g, i, b):
                        st = Steps(dve, s_v, g * K + setup)
                        slots = ds(g * G, G)
                        dve.wait_ge(s_ag[b], i * (16 * G) + 16 * G)
                        R = agg[b]
                        ne = nonempty[:, slots]
                        if layer == 0:
                            M = R[:, :, D + HEADS:D + 2 * HEADS]
                            st.link(nc.vector.tensor_scalar(f4[:], M, -1e9, None, ALU.max))
                            nc.vector.tensor_tensor(g4[:], M, f4[:], ALU.subtract).then_inc(s_sq, 1)
                            dve.wait_ge(s_rt, g * 2 + 1)
                            st.link(nc.vector.tensor_tensor(f4[:], R[:, :, D:D + HEADS], h4[:], ALU.mult))
                            st.link(nc.vector.tensor_scalar(f4[:], f4[:], 1e-9, None, ALU.add))
                            st.link(nc.vector.tensor_scalar(f4[:], f4[:], 1e-30, None, ALU.max))
                            st.link(nc.vector.reciprocal(g4[:], f4[:]))
                            st.link(nc.vector.tensor_tensor(g4[:], g4[:], h4[:], ALU.mult))
                            st.link(nc.vector.tensor_tensor(g4[:], g4[:], bc(ne, 2, HEADS), ALU.mult))
                            nc.vector.tensor_tensor(a[:].rearrange("p g (h e) -> p g h e", h=HEADS),
                                                    R[:, :, 0:D].rearrange("p g (h e) -> p g h e", h=HEADS),
                                                    bc(g4[:], 3, D // HEADS), ALU.mult).then_inc(s_a, 1)
                            dve.wait_ge(s_mm, g * 2 + 1)
                            st.link(nc.vector.tensor_tensor(y[:], xg[b][:], p_mm[:, 0:2, :].rearrange("p k n -> p (k n)")[:, 0:G * D].rearrange("p (g f) -> p g f", f=D), ALU.add))
                        elif layer == 1:
                            st.link(nc.vector.tensor_tensor(sq[:], R[:], own[b][:], ALU.add))
                            st.link(nc.vector.tensor_scalar(sq[:], sq[:], 0.0, None, ALU.max))
                            st.link(nc.vector.tensor_tensor(sq[:], sq[:], bc(ne, 2, D), ALU.mult))
                            st.link(nc.vector.tensor_tensor(y[:], sq[:], xg[b][:], ALU.add))
                        elif layer == 2:
                            nc.vector.tensor_tensor(a[:], R[:], bc(rcnt[:, slots], 2, HID), ALU.mult).then_inc(s_a, 1)
                            st.step(nc.vector.tensor_copy(u[:, :, 0:D], xg[b][:]))
                            st.step(nc.vector.tensor_copy(sq[:], bc(bp2[:], 1, G)))
                            st.wait()
                            dve.wait_ge(s_mm, g * 3 + 1)
                            st.link(nc.vector.tensor_tensor(sq[:], sq[:], p_mm[:, 0:2, :].rearrange("p k n -> p (k n)")[:, 0:G * D].rearrange("p (g f) -> p g f", f=D), ALU.add))
                            st.step(nc.vector.tensor_tensor(u[:, :, D:2 * D], sq[:], bc(ne, 2, D), ALU.mult))
                            st.wait()
                            dve.sem_inc(s_a, 1)
                            dve.wait_ge(s_rt, g * 2 + 1)
                            st.link(nc.vector.tensor_scalar(be[:], be[:], 1.0, -1.0, ALU.min, ALU.add))
                            nc.vector.tensor_tensor(be[:], be[:], br[:], ALU.add).then_inc(s_a, 1)
                            dve.wait_ge(s_mm, g * 3 + 3)
                            st.link(nc.vector.tensor_tensor(sq[:], xg[b][:], bc(bg2[:], 1, G), ALU.add))
                            st.link(nc.vector.tensor_tensor(y[:], sq[:], p_mm[:, 0:2, :].rearrange("p k n -> p (k n)")[:, 0:G * D].rearrange("p (g f) -> p g f", f=D), ALU.add))
                        else:
                            st.link(nc.vector.tensor_tensor(s1[:], ndst[:, slots], ne, ALU.mult))
                            nc.vector.tensor_tensor(a[:], R[:], bc(s1[:], 2, D), ALU.mult).then_inc(s_a, 1)
                            dve.wait_ge(s_mm, g + 1)
                            st.link(nc.vector.tensor_tensor(y[:], xg[b][:], p_mm[:, 0:2, :].rearrange("p k n -> p (k n)")[:, 0:G * D].rearrange("p (g f) -> p g f", f=D), ALU.add))
                        st.link(nc.vector.tensor_reduce(s1[:], y[:], AX.X, ALU.add))
                        nc.vector.sem_inc(s_used, 1)
                        st.link(nc.vector.tensor_scalar(s1[:], s1[:], 1.0 / D, None, ALU.mult))
                        st.link(nc.vector.tensor_tensor(y[:], y[:], bc(s1[:], 2, D), ALU.subtract))
                        st.link(nc.vector.tensor_tensor(sq[:], y[:], y[:], ALU.mult))
                        st.link(nc.vector.tensor_reduce(s2[:], sq[:], AX.X, ALU.add))
                        nc.vector.tensor_scalar(s2[:], s2[:], 1.0 / D, EPS, ALU.mult, ALU.add).then_inc(s_sq, 1)
                        dve.wait_ge(s_rt, (g + 1) * (2 if layer in (0, 2) else 1))
                        st.link(nc.vector.reciprocal(s2[:], rt[:]))
                        dve.wait_ge(s_st, g * (16 * n_st))
                        st.step(nc.vector.tensor_tensor(xn[:], y[:], bc(s2[:], 2, D), ALU.mult))
                        st.wait()
                        nc.vector.sem_inc(s_xn, 1)
                        if layer == 0:
                            dve.wait_ge(s_mm, g * 2 + 2)
                            tab = p_mm[:, 2:5, :].rearrange("p k n -> p (k n)")[:, 0:G * NT].rearrange("p (g f) -> p g f", f=NT)
                            st.step(nc.vector.tensor_tensor(own_s[:], tab[:, :, 0:D], bc(bias_next[:], 1, G), ALU.add))
                            st.wait()
                            nc.vector.sem_inc(s_tab, 1)
                        if layer == 1:
                            dve.wait_ge(s_mm, g + 1)
                            tab = p_mm[:].rearrange("p k (h f) -> p (k h) f", h=2)
                            st.step(nc.vector.tensor_tensor(own_s[:], tab[:, :, 0:HID], bc(bias_next[:], 1, G), ALU.add))
                            st.wait()
                            nc.vector.sem_inc(s_tab, 1)
                        if layer == 2:
                            st.step(nc.vector.tensor_tensor(own_s[:], xn[:], bc(nsrc[:, slots], 2, D), ALU.mult))
                            st.wait()
                            nc.vector.sem_inc(s_tab, 1)
                        assert st.n <= K, (layer, st.n)
                        for _ in range(K - st.n):
                            nc.vector.sem_inc(s_v, 1)
                    with nc.Fori(0, GPAIRS, engines=[nc.vector.engine]) as i:
                        for b in range(2):
                            group(i * 2 + b, i, b)

                @block.scalar
                def _(act):
                    act.wait_ge(s_w, 16 * len(loads) + 16)

                    def group(g):
                        if layer == 0:
                            act.wait_ge(s_sq, g * 2 + 1)
                            nc.scalar.activation(h4[:], g4[:], ACT.Exp).then_inc(s_rt, 1)
                        if layer in (0, 3):
                            n_tr = 2 if layer == 0 else 1
                            act.wait_ge(s_tr, g * n_tr + 1)
                            nc.scalar.activation(aT[:], p_tr[:, 0:2, :].rearrange("p k n -> p (k n)")[:, 0:G * D].rearrange("p (k n) -> p k n", n=P), ACT.Copy).then_inc(s_ev, 1)
                        if layer == 2:
                            for r in range(2):
                                act.wait_ge(s_tr, g * 2 + r + 1)
                                nc.scalar.activation(aTw[:], p_tr[:].rearrange("p k n -> p (k n)")[:, 0:G * P].rearrange("p (k n) -> p k n", n=P), ACT.Copy).then_inc(s_ev, 1)
                            act.wait_ge(s_mm, g * 3 + 2)
                            z = p_mm[:, 2:5, :].rearrange("p k n -> p (k n)")[:, 0:G * P].rearrange("p (k n) -> p k n", n=P)
                            nc.scalar.activation(be[:], z, ACT.Exp, bias=bg1[:, 0:1])
                            nc.scalar.activation(br[:], z, ACT.Relu, bias=bg1[:, 0:1]).then_inc(s_rt, 1)
                        act.wait_ge(s_sq, (g + 1) * (2 if layer == 0 else 1))
                        nc.scalar.activation(rt[:], s2[:], ACT.Sqrt).then_inc(s_rt, 1)
                        if layer < 2:
                            act.wait_ge(s_tr, g * (2 if layer == 0 else 1) + (2 if layer == 0 else 1))
                            nc.scalar.activation(aT[:], p_tr[:, 0:2, :].rearrange("p k n -> p (k n)")[:, 0:G * D].rearrange("p (k n) -> p k n", n=P), ACT.Copy).then_inc(s_ev, 1)
                            act.wait_ge(s_tab, g * 2 + 1)
                            act.wait_ge(s_st, g * (16 * n_st))
                            if layer == 0:
                                tab = p_mm[:, 2:5, :].rearrange("p k n -> p (k n)")[:, 0:G * NT].rearrange("p (g f) -> p g f", f=NT)
                                nc.scalar.activation(nbr_s[:], tab[:, :, D:2 * D], ACT.Copy).then_inc(s_tab, 1)
                            else:
                                tab = p_mm[:].rearrange("p k (h f) -> p (k h) f", h=2)
                                nc.scalar.activation(nbr_s[:], tab[:, :, HID:2 * HID], ACT.Copy).then_inc(s_tab, 1)
                    with nc.Fori(0, 2 * GPAIRS, engines=[nc.scalar.engine]) as g:
                        group(g)

                @block.tensor
                def _(pe):
                    pe.wait_ge(s_w, 16 * len(loads) + 16)

                    def transpose_pairs(rows):
                        for k in range(G // 2):
                            r = nc.tensor.transpose(p_tr[:, k // 4, (k % 4) * P:(k % 4 + 1) * P],
                                                    rows[:, 2 * k:2 * k + 2, :].rearrange("p h f -> p (h f)"), ident[:])
                        r.then_inc(s_tr, 1)

                    def times(w, n, bank0):
                        per_bank = 512 // (2 * n)
                        for k in range(G // 2):
                            r = nc.tensor.matmul(p_mm[:, bank0 + k // per_bank, (k % per_bank) * 2 * n:(k % per_bank + 1) * 2 * n],
                                                 aT[:, k, :], w[:].rearrange("p h f -> p (h f)"), start=True, stop=True)
                        r.then_inc(s_mm, 1)

                    def group(g):
                        if layer in (0, 3):
                            n_ev = 2 if layer == 0 else 1
                            pe.wait_ge(s_a, g + 1)
                            transpose_pairs(a)
                            pe.wait_ge(s_ev, g * n_ev + 1)
                            times(w_out, D, 0)
                        if layer == 2:
                            pe.wait_ge(s_a, g * 3 + 1)
                            for s in range(G):
                                r = nc.tensor.transpose(p_tr[:, s // 4, (s % 4) * P:(s % 4 + 1) * P], a[:, s, :], ident[:])
                            r.then_inc(s_tr, 1)
                            pe.wait_ge(s_ev, g * 2 + 1)
                            for s in range(G):
                                r = nc.tensor.matmul(p_mm[:, s // 8, (s % 8) * D:(s % 8 + 1) * D], aTw[:, s, :], wp2[:], start=True, stop=True)
                            r.then_inc(s_mm, 1)
                            pe.wait_ge(s_a, g * 3 + 2)
                            for s in range(G):
                                r = nc.tensor.transpose(p_tr[:, s // 4, (s % 4) * P:(s % 4 + 1) * P], u[:, s, :], ident[:])
                            r.then_inc(s_tr, 1)
                            pe.wait_ge(s_ev, g * 2 + 2)
                            for k in range(-(-G // 4)):
                                w = min(4, G - 4 * k)
                                r = nc.tensor.matmul(p_mm[:, 2 + k, 0:w * P], wg1[:], aTw[:, 4 * k:4 * k + w, :].rearrange("p k n -> p (k n)"),
                                                     start=True, stop=True)
                            r.then_inc(s_mm, 1)
                            pe.wait_ge(s_a, g * 3 + 3)
                            for s in range(G):
                                r = nc.tensor.matmul(p_mm[:, s // 8, (s % 8) * D:(s % 8 + 1) * D], be[:, s, :], wg2[:], start=True, stop=True)
                            r.then_inc(s_mm, 1)
                        if layer < 2:
                            pe.wait_ge(s_xn, g + 1)
                            transpose_pairs(xn)
                            pe.wait_ge(s_ev, (g + 1) * (2 if layer == 0 else 1))
                            pe.wait_ge(s_tab, g * 2)
                            times(w_next, NT, 2 if layer == 0 else 0)
                    with nc.Fori(0, 2 * GPAIRS, engines=[nc.tensor.engine]) as g:
                        group(g)

        last0 = sb_last0 = ctx.enter_context(nc.sbuf_tensor("last_state", [P, HID], f32))
        with phase("attention_edges") as (scope, block):
            sb, ps = maker(scope)
            idx = [sb(f"at_idx{b}", [P, T], i32) for b in range(2)]
            kv = [sb(f"at_kv{b}", [P, T, 2 * D]) for b in range(2)]
            q = [sb(f"at_q{b}", [P, T, D]) for b in range(2)]
            o = [sb(f"at_o{b}", [P, T, ROW0]) for b in range(2)]
            sc = sb("at_sc", [P, T, HEADS])
            mx = sb("at_mx", [P, T + 1, HEADS])
            dif = sb("at_dif", [P, 2, T, HEADS])
            ex = sb("at_ex", [P, 2, T, HEADS])
            s_idx = [sem(f"at_idx{b}") for b in range(2)]
            s_rows = [sem(f"at_rows{b}") for b in range(2)]
            s_free = [sem(f"at_free{b}") for b in range(2)]
            s_q = [sem(f"at_q{b}") for b in range(2)]
            s_out = [sem(f"at_out{b}") for b in range(2)]
            s_v, s_qf, s_dif, s_ex, s_o, s_turn, s_m = (sem("at_" + n) for n in ("v", "qf", "dif", "ex", "o", "turn", "m"))

            @block.sync
            def _(sp):
                def load(c, b, width=T):
                    sp.dma_start(idx[b][:, 0:width], src_v[:, ds(c * T, width)]).then_inc(s_idx[b], 16)
                    sp.dma_start(q[b][:, 0:width, :], edges(qstart_d)[:, ds(c * T, width), :]).then_inc(s_q[b], 16)

                def store(c, b, width=T):
                    sp.wait_ge(s_o, c * 2 + 2)
                    sp.dma_start(edges(scan_d[0])[:, ds(c * T, width), :], o[b][:, 0:width, :]).then_inc(s_out[b], 16)
                load(0, 0)
                load(1, 1)
                with nc.Fori(0, PAIRS - 1, engines=[nc.sync.engine]) as i:
                    for b in range(2):
                        sp.wait_ge(s_qf, i * 2 + b + 1)
                        load(i * 2 + b + 2, b)
                        store(i * 2 + b, b)
                sp.wait_ge(s_qf, 2 * PAIRS - 1)
                load(2 * PAIRS, 0, TAIL)
                store(2 * PAIRS - 2, 0)
                store(2 * PAIRS - 1, 1)
                store(2 * PAIRS, 0, TAIL)
                sp.wait_ge(s_out[0], 16 * (PAIRS + 1))
                sp.wait_ge(s_out[1], 16 * PAIRS)

            @block.gpsimd
            def _(pool):
                pool_gathers(pool, kv_d, idx, kv, s_idx, s_free, s_rows, s_turn)

            @block.vector
            def _(dve):
                st = Steps(dve, s_v)
                dve.sem_inc(s_free[0], 1)
                dve.sem_inc(s_free[1], 1)
                st.step(nc.vector.memset(mx[:, 0, :], -BIG))
                st.step(nc.vector.memset(o[1][:, T - 1, :], 0.0))
                setup = st.n
                st.wait()
                K = 11

                def chunk(c, i, b, width=T):
                    st = Steps(dve, s_v, c * K + setup)
                    kp = keep[:, ds(c * T, width)]
                    W = slice(0, width)
                    prev = o[1 - b][:, T - 1, :]
                    dve.wait_ge(s_q[b], i * 16 + 16)
                    for f in range(D):
                        r = nc.vector.tensor_tensor_scan(q[b][:, W, f], kp, q[b][:, W, f], qcarry[:, f:f + 1], ALU.mult, ALU.add)
                    st.link(r)
                    st.link(nc.vector.tensor_copy(qcarry[:], q[b][:, width - 1, :]))
                    dve.wait_ge(s_rows[b], i * (16 * T) + 16 * width)
                    st.link(nc.vector.tensor_tensor(q[b][:, W, :], q[b][:, W, :], kv[b][:, W, 0:D], ALU.mult))
                    st.link(nc.vector.tensor_reduce(sc[:, W, :], q[b][:, W, :].rearrange("p t (h e) -> p t h e", h=HEADS), AX.X, ALU.add))
                    nc.vector.sem_inc(s_qf, 1)
                    for h in range(HEADS):
                        r = nc.vector.tensor_tensor_scan(mx[:, 1:width + 1, h], pen[:, ds(c * T, width)], sc[:, W, h], mx[:, 0, h:h + 1], ALU.add, ALU.max)
                    st.link(r)
                    st.step(nc.vector.tensor_tensor(dif[:, 0, W, :], mx[:, 0:width, :], mx[:, 1:width + 1, :], ALU.subtract))
                    st.step(nc.vector.tensor_tensor(dif[:, 1, W, :], sc[:, W, :], mx[:, 1:width + 1, :], ALU.subtract))
                    st.wait()
                    nc.vector.tensor_scalar(dif[:, 0, W, :], dif[:, 0, W, :], 0.0, None, ALU.min).then_inc(s_dif, 1)
                    dve.wait_ge(s_ex, c * 2 + 1)
                    st.link(nc.vector.scalar_tensor_tensor(ex[:, 0, W, :], dif[:, 0, W, :], 0.0, ex[:, 0, W, :], ALU.is_ge, ALU.max))
                    st.step(nc.vector.tensor_tensor(ex[:, 0, W, :], ex[:, 0, W, :], bc(kp, 2, HEADS), ALU.mult))
                    v4 = kv[b][:, W, D:2 * D].rearrange("p t (h e) -> p t h e", h=HEADS)
                    st.step(nc.vector.tensor_tensor(v4, v4, bc(ex[:, 1, W, :], 3, D // HEADS), ALU.mult))
                    st.wait()
                    dve.wait_ge(s_out[b], i * 16)
                    for f in range(D):
                        h = f // (D // HEADS)
                        nc.vector.tensor_tensor_scan(o[b][:, W, f], ex[:, 0, W, h], kv[b][:, W, D + f], prev[:, f:f + 1], ALU.mult, ALU.add)
                    for h in range(HEADS):
                        r = nc.vector.tensor_tensor_scan(o[b][:, W, D + h], ex[:, 0, W, h], ex[:, 1, W, h], prev[:, D + h:D + h + 1], ALU.mult, ALU.add)
                    st.link(r)
                    nc.vector.sem_inc(s_o, 1)
                    nc.vector.sem_inc(s_free[b], 1)
                    dve.wait_ge(s_ex, c * 2 + 2)
                    st.n += 0
                    nc.vector.tensor_copy(mx[:, 0, :], mx[:, width, :]).then_inc(s_m, 1)
                    dve.wait_ge(s_m, c + 1)
                    assert st.n == K, st.n
                with nc.Fori(0, PAIRS, engines=[nc.vector.engine]) as i:
                    for b in range(2):
                        chunk(i * 2 + b, i, b)
                chunk(2 * PAIRS, PAIRS, 0, TAIL)
                st = Steps(dve, s_v, (2 * PAIRS + 1) * K + setup)
                st.step(nc.vector.tensor_copy(last0[:, 0:D + HEADS], o[0][:, TAIL - 1, 0:D + HEADS]))
                st.step(nc.vector.tensor_copy(last0[:, D + HEADS:ROW0], mx[:, 0, :]))

            @block.scalar
            def _(act):
                def chunk(c, i, b, width=T):
                    act.wait_ge(s_dif, c + 1)
                    nc.scalar.activation(ex[:, :, 0:width, :], dif[:, :, 0:width, :], ACT.Exp).then_inc(s_ex, 1)
                    act.wait_ge(s_out[b], i * 16)
                    nc.scalar.activation(o[b][:, 0:width, D + HEADS:ROW0], mx[:, 1:width + 1, :], ACT.Copy).then_inc(s_ex, 1)
                    act.wait_ge(s_ex, c * 2 + 2)
                    nc.scalar.sem_inc(s_o, 1)
                with nc.Fori(0, PAIRS, engines=[nc.scalar.engine]) as i:
                    for b in range(2):
                        chunk(i * 2 + b, i, b)
                chunk(2 * PAIRS, PAIRS, 0, TAIL)

        with phase("attention_boundary") as (scope, block):
            sb, ps = maker(scope)
            S = D + HEADS
            gm = sb("ab_gm", [P, HEADS])
            gmT = sb("ab_gmT", [HEADS, P])
            mT = sb("ab_mT", [HEADS, P + 1])
            mr = sb("ab_mr", [P, 2, HEADS])
            df = sb("ab_df", [P, 2, HEADS])
            ef = sb("ab_ef", [P, 2, HEADS])
            d0, d1 = sb("ab_d0", [P, S]), sb("ab_d1", [P, S])
            d0T, runT = sb("ab_d0T", [S, P]), sb("ab_runT", [S, P + 1])
            carry, rows, res = sb("ab_carry", [P, S]), sb("ab_rows", [P, ROW0]), sb("ab_res", [P, ROW0])
            pp = [ps(f"ab_p{n}", [P, 512]) for n in range(7)]
            s_v, s_t, s_e, s_g, s_s, s_m = (sem("ab_" + n) for n in ("v", "t", "e", "g", "s", "m"))
            waits = {}

            @block.vector
            def _(dve):
                st = Steps(dve, s_v)
                nc.vector.memset(rows[:], 0.0).then_inc(s_m, 1)
                st.step(nc.vector.memset(mT[:, 0:1], -BIG))
                st.step(nc.vector.memset(runT[:, 0:1], 0.0))
                st.link(nc.vector.tensor_scalar(gm[:], bc(whole[:, 0], 1, HEADS), -1.0, BIG, ALU.add, ALU.mult))
                waits["gates"] = st.n
                dve.wait_ge(s_t, 2)
                st.link(nc.vector.tensor_copy(gmT[:], pp[0][0:HEADS, 0:P]))
                st.link(nc.vector.tensor_tensor_scan(mT[:, 1:P + 1], gmT[:], pp[1][0:HEADS, 0:P], -BIG, ALU.add, ALU.max))
                waits["maxima"] = st.n
                dve.wait_ge(s_t, 4)
                st.step(nc.vector.tensor_copy(mr[:, 0, :], pp[2][:, 0:HEADS]))
                st.link(nc.vector.tensor_copy(mr[:, 1, :], pp[3][:, 0:HEADS]))
                st.step(nc.vector.tensor_tensor(df[:, 0, :], mr[:, 0, :], mr[:, 1, :], ALU.subtract))
                st.link(nc.vector.tensor_tensor(df[:, 1, :], last0[:, S:ROW0], mr[:, 1, :], ALU.subtract))
                st.link(nc.vector.tensor_scalar(df[:], df[:], 0.0, None, ALU.min))
                waits["factors"] = st.n
                dve.wait_ge(s_e, 1)
                st.link(nc.vector.tensor_scalar(ef[:, 0, :], ef[:, 0, :], whole[:, 0:1], None, ALU.mult))
                for dd, k in ((d0, 0), (d1, 1)):
                    st.step(nc.vector.tensor_copy(dd[:, 0:D].rearrange("p (h e) -> p h e", h=HEADS), bc(ef[:, k, :], 2, D // HEADS)))
                    st.step(nc.vector.tensor_copy(dd[:, D:S], ef[:, k, :]))
                st.wait()
                st.link(nc.vector.tensor_tensor(d1[:], d1[:], last0[:, 0:S], ALU.mult))
                waits["states"] = st.n
                dve.wait_ge(s_t, 6)
                st.link(nc.vector.tensor_copy(d0T[:], pp[4][0:S, 0:P]))
                st.link(nc.vector.tensor_tensor_scan(runT[:, 1:P + 1], d0T[:], pp[5][0:S, 0:P], 0.0, ALU.mult, ALU.add))
                waits["sums"] = st.n
                dve.wait_ge(s_t, 7)
                st.link(nc.vector.tensor_copy(carry[:], pp[6][:, 0:S]))
                dve.wait_ge(s_g, 16)
                st.link(nc.vector.tensor_tensor(res[:, S:ROW0], rows[:, S:ROW0], mr[:, 0, :], ALU.max))
                st.step(nc.vector.tensor_tensor(df[:, 0, :], mr[:, 0, :], res[:, S:ROW0], ALU.subtract))
                st.link(nc.vector.tensor_tensor(df[:, 1, :], rows[:, S:ROW0], res[:, S:ROW0], ALU.subtract))
                waits["merge"] = st.n
                dve.wait_ge(s_e, 2)
                for dd, k in ((d0, 0), (d1, 1)):
                    st.step(nc.vector.tensor_copy(dd[:, 0:D].rearrange("p (h e) -> p h e", h=HEADS), bc(ef[:, k, :], 2, D // HEADS)))
                    st.step(nc.vector.tensor_copy(dd[:, D:S], ef[:, k, :]))
                st.wait()
                st.step(nc.vector.tensor_tensor(d0[:], d0[:], carry[:], ALU.mult))
                st.link(nc.vector.tensor_tensor(d1[:], d1[:], rows[:, 0:S], ALU.mult))
                st.link(nc.vector.tensor_tensor(res[:, 0:S], d0[:], d1[:], ALU.add))
                nc.vector.sem_inc(s_m, 1)

            @block.tensor
            def _(pe):
                pe.wait_ge(s_v, waits["gates"])
                nc.tensor.transpose(pp[0][0:HEADS, 0:P], gm[:], ident[:]).then_inc(s_t, 1)
                nc.tensor.transpose(pp[1][0:HEADS, 0:P], last0[:, S:ROW0], ident[:]).then_inc(s_t, 1)
                pe.wait_ge(s_v, waits["maxima"])
                nc.tensor.transpose(pp[2][:, 0:HEADS], mT[:, 0:P], ident[0:HEADS, 0:HEADS]).then_inc(s_t, 1)
                nc.tensor.transpose(pp[3][:, 0:HEADS], mT[:, 1:P + 1], ident[0:HEADS, 0:HEADS]).then_inc(s_t, 1)
                pe.wait_ge(s_v, waits["states"])
                nc.tensor.transpose(pp[4][0:S, 0:P], d0[:], ident[:]).then_inc(s_t, 1)
                nc.tensor.transpose(pp[5][0:S, 0:P], d1[:], ident[:]).then_inc(s_t, 1)
                pe.wait_ge(s_v, waits["sums"])
                nc.tensor.transpose(pp[6][:, 0:S], runT[:, 0:P], ident[0:S, 0:S]).then_inc(s_t, 1)

            @block.scalar
            def _(act):
                act.wait_ge(s_v, waits["factors"])
                nc.scalar.activation(ef[:], df[:], ACT.Exp).then_inc(s_e, 1)
                act.wait_ge(s_v, waits["merge"])
                nc.scalar.activation(ef[:], df[:], ACT.Exp).then_inc(s_e, 1)

            @block.gpsimd
            def _(pool):
                pool.wait_ge(s_m, 1)
                nc.gpsimd.indirect_dma_start(rows[:], None, scan_d[0], bass.IndirectOffsetOnAxis(ap=fixidx[:, 0:1], axis=0),
                                             bounds_check=E - 1, oob_is_err=False).then_inc(s_g, 16)
                pool.wait_ge(s_m, 2)
                nc.gpsimd.indirect_dma_start(scan_d[0], bass.IndirectOffsetOnAxis(ap=fixidx[:, 0:1], axis=0), res[:], None,
                                             bounds_check=E - 1, oob_is_err=False).then_inc(s_s, 16)
                pool.wait_ge(s_s, 16)

        node_block("attention_nodes", 0, scan_d[0], ROW0, None)

        def plain_edges(name, table, scan_out, gate, op, none, degrees):
            first = ALU.mult if op == ALU.add else ALU.add
            with phase(name) as (scope, block):
                sb, ps = maker(scope)
                idx = [sb(f"{name}_idx{b}", [P, T], i32) for b in range(2)]
                rows = [sb(f"{name}_rows{b}", [P, T, D]) for b in range(2)]
                o = [sb(f"{name}_o{b}", [P, T, D]) for b in range(2)]
                s_idx = [sem(f"{name}_idx{b}") for b in range(2)]
                s_rows = [sem(f"{name}_rows{b}") for b in range(2)]
                s_free = [sem(f"{name}_free{b}") for b in range(2)]
                s_out = [sem(f"{name}_out{b}") for b in range(2)]
                s_v, s_o, s_open, s_turn = (sem(f"{name}_{n}") for n in ("v", "o", "open", "turn"))
                if degrees:
                    hi = sb("dg_hi", [P, T])
                    lo = sb("dg_lo", [P, T])
                    ohi, olo = sb("dg_ohi", [P, T, P], bf16), sb("dg_olo", [P, T, J], bf16)
                    zrow = sb("dg_zrow", [P, P], bf16)
                    zeros = sb("dg_zeros", [P, T, HID])
                    p_h = ps("dg_ph", [P, 512])
                    s_oh, s_hm, s_z, s_fill = (sem("dg_" + n) for n in ("oh", "hm", "z", "fill"))

                @block.sync
                def _(sp):
                    def load(c, b, width=T):
                        sp.dma_start(idx[b][:, 0:width], src_v[:, ds(c * T, width)]).then_inc(s_idx[b], 16)

                    def store(c, b, width=T):
                        sp.wait_ge(s_o, c + 1)
                        sp.dma_start(edges(scan_out)[:, ds(c * T, width), :], o[b][:, 0:width, :]).then_inc(s_out[b], 16)
                    load(0, 0)
                    load(1, 1)
                    with nc.Fori(0, PAIRS - 1, engines=[nc.sync.engine]) as i:
                        for b in range(2):
                            store(i * 2 + b, b)
                            load(i * 2 + b + 2, b)
                    store(2 * PAIRS - 2, 0)
                    load(2 * PAIRS, 0, TAIL)
                    store(2 * PAIRS - 1, 1)
                    store(2 * PAIRS, 0, TAIL)
                    sp.wait_ge(s_out[0], 16 * (PAIRS + 1))
                    sp.wait_ge(s_out[1], 16 * PAIRS)

                @block.gpsimd
                def _(pool):
                    pool_gathers(pool, table, idx, rows, s_idx, s_free, s_rows, s_turn)

                @block.vector
                def _(dve):
                    st = Steps(dve, s_v)
                    st.step(nc.vector.memset(o[1][:, T - 1, :], none))
                    if degrees:
                        st.step(nc.vector.memset(zrow[:], 0.0))
                        nc.vector.memset(zeros[:], 0.0).then_inc(s_z, 1)
                    st.wait()
                    setup = st.n
                    dve.sem_inc(s_open, 1)
                    dve.sem_inc(s_free[0], 1)
                    dve.sem_inc(s_free[1], 1)
                    K = 6 if degrees else 1

                    def chunk(c, i, b, width=T):
                        st = Steps(dve, s_v, c * K + setup)
                        W = slice(0, width)
                        if degrees:
                            dve.wait_ge(s_idx[b], i * 16 + 16)
                            st.link(nc.vector.tensor_scalar(hi[:, W], idx[b][:, W], -(J - 1) / 2, 1.0 / J, ALU.add, ALU.mult))
                            st.link(nc.vector.tensor_scalar(hi[:, W], hi[:, W], MAGIC, -MAGIC, ALU.add, ALU.add))
                            st.link(nc.vector.scalar_tensor_tensor(lo[:, W], hi[:, W], -float(J), idx[b][:, W], ALU.mult, ALU.add))
                            dve.wait_ge(s_hm, c + 1)
                            st.step(nc.vector.tensor_tensor(ohi[:, W, :], bc(hi[:, W], 2, P), bc(iota_row[:], 1, width), ALU.is_equal))
                            st.link(nc.vector.tensor_tensor(olo[:, W, :], bc(lo[:, W], 2, J), bc(iota_row[:, 0:J], 1, width), ALU.is_equal))
                            nc.vector.sem_inc(s_oh, 1)
                        dve.wait_ge(s_rows[b], i * (16 * T) + 16 * width)
                        dve.wait_ge(s_out[b], i * 16)
                        for f in range(D):
                            r = nc.vector.tensor_tensor_scan(o[b][:, W, f], gate[:, ds(c * T, width)], rows[b][:, W, f],
                                                             o[1 - b][:, T - 1, f:f + 1], first, op)
                        st.link(r)
                        nc.vector.sem_inc(s_o, 1)
                        nc.vector.sem_inc(s_free[b], 1)
                        assert st.n == K
                    with nc.Fori(0, PAIRS, engines=[nc.vector.engine]) as i:
                        for b in range(2):
                            chunk(i * 2 + b, i, b)
                    chunk(2 * PAIRS, PAIRS, 0, TAIL)
                    base = (2 * PAIRS + 1) * K + setup
                    st = Steps(dve, s_v, base)
                    st.step(nc.vector.tensor_copy(last0[:, 0:D], o[0][:, TAIL - 1, :]))
                    if degrees:
                        dve.wait_ge(s_hm, 2 * PAIRS + 2)
                        st.link(nc.vector.tensor_scalar(nsrc[:], p_h[:, 0:J], 1.0, None, ALU.max))
                        dve.wait_ge(s_hm, 2 * PAIRS + 3)
                        st.link(nc.vector.reciprocal(nsrc[:], nsrc[:]))

                if degrees:
                    @block.tensor
                    def _(pe):
                        pe.wait_ge(s_open, 1)
                        nc.tensor.matmul(p_h[:, 0:J], zrow[:], zrow[:, 0:J], start=True, stop=False).then_inc(s_hm, 1)

                        def count(c, width=T, last=False):
                            pe.wait_ge(s_oh, c + 1)
                            for t in range(width):
                                mm = nc.tensor.matmul(p_h[:, 0:J], ohi[:, t, :], olo[:, t, :], start=False, stop=last and t == width - 1)
                            mm.then_inc(s_hm, 1)
                        with nc.Fori(0, 2 * PAIRS, engines=[nc.tensor.engine]) as c:
                            count(c)
                        count(2 * PAIRS, TAIL, True)

                    @block.scalar
                    def _(act):
                        act.wait_ge(s_z, 1)
                        with nc.Fori(0, 2 * PAIRS, engines=[nc.scalar.engine]) as c:
                            act.wait_ge(s_o, c + 1)
                            act.dma_start(edges(pstart_d)[:, ds(c * T, T), :], zeros[:]).then_inc(s_fill, 16)
                        act.dma_start(edges(pstart_d)[:, 2 * PAIRS * T:TALL, :], zeros[:, 0:TAIL, :]).then_inc(s_fill, 16)
                        act.wait_ge(s_fill, 16 * (2 * PAIRS + 1))
                        act.wait_ge(s_v, (2 * PAIRS + 1) * 6 + 2 + 2)
                        nc.scalar.activation(nsrc[:], nsrc[:], ACT.Sqrt).then_inc(s_hm, 1)

        plain_edges("max_edges", nbr1_d, scan_d[1], pen, ALU.max, -BIG, True)
        boundary("max_boundary", last0[:, 0:D], scan_d[1], D, ALU.max, -BIG)
        node_block("max_nodes", 1, scan_d[1], D, x_d[0], own1_d)

        scatter_rows("scatter_p", own2_d, pstart_d, HID, pcarry, False)

        with phase("mlp_edges") as (scope, block):
            sb, ps = maker(scope)
            NB = T // BLK
            idx = [sb(f"ml_idx{b}", [P, T], i32) for b in range(2)]
            nbr = [sb(f"ml_nbr{b}", [P, T, HID]) for b in range(2)]
            own = [sb(f"ml_own{b}", [P, T, HID]) for b in range(2)]
            ea = [sb(f"ml_ea{b}", [P, T * EA]) for b in range(2)]
            eaT = sb("ml_eaT", [BLK * EA, NB, P])
            wea = sb("ml_wea", [BLK * EA, BLK, HID])
            hs = sb("ml_h", [P, T, HID])
            hcarry = sb("ml_hc", [P, HID])
            ee = [sb(f"ml_e{k}", [P, BLK, HID]) for k in range(2)]
            rr = [sb(f"ml_r{k}", [P, BLK, HID]) for k in range(2)]
            p_h = [ps(f"ml_ph{k}", [P, 3, 512]) for k in range(2)]
            p_e = ps("ml_pe", [P, 2, 512])
            s_idx = [sem(f"ml_idx{b}") for b in range(2)]
            s_rows = [sem(f"ml_rows{b}") for b in range(2)]
            s_free = [sem(f"ml_free{b}") for b in range(2)]
            s_in = [sem(f"ml_in{b}") for b in range(2)]
            s_v, s_w, s_w2, s_own, s_et, s_ev, s_ph, s_pf, s_er, s_ef, s_hd, s_o, s_out, s_done, s_turn = (
                sem("ml_" + n) for n in ("v", "w", "w2", "own", "et", "ev", "ph", "pf", "er", "ef", "hd", "o", "out", "done", "turn"))

            def blocks(width):
                return [(k, min(BLK, width - k)) for k in range(0, width, BLK)]

            @block.sync
            def _(sp):
                sp.wait_ge(s_w2, 1)
                for t in range(BLK):
                    sp.dma_start(wea[t * EA:(t + 1) * EA, t, :], pw1_in[2 * D:2 * D + EA, :]).then_inc(s_w, 16)

                def load(c, b, width=T):
                    sp.dma_start(idx[b][:, 0:width], src_v[:, ds(c * T, width)]).then_inc(s_idx[b], 16)
                    sp.dma_start(own[b][:, 0:width, :], edges(pstart_d)[:, ds(c * T, width), :]).then_inc(s_in[b], 16)
                    sp.dma_start(ea[b][:, 0:width * EA], ea_v[:, ds(c * T, width), :].rearrange("p t a -> p (t a)")).then_inc(s_in[b], 16)

                def store(c, width=T):
                    sp.wait_ge(s_o, c + 1)
                    sp.dma_start(edges(scan_d[2])[:, ds(c * T, width), :], hs[:, 0:width, :]).then_inc(s_out, 16)
                load(0, 0)
                load(1, 1)
                with nc.Fori(0, PAIRS - 1, engines=[nc.sync.engine]) as i:
                    for b in range(2):
                        sp.wait_ge(s_done, i * 2 + b + 1)
                        load(i * 2 + b + 2, b)
                        store(i * 2 + b)
                sp.wait_ge(s_done, 2 * PAIRS - 1)
                load(2 * PAIRS, 0, TAIL)
                store(2 * PAIRS - 2)
                store(2 * PAIRS - 1)
                store(2 * PAIRS, TAIL)
                sp.wait_ge(s_out, 16 * (2 * PAIRS + 1))

            @block.gpsimd
            def _(pool):
                pool_gathers(pool, nbr2_d, idx, nbr, s_idx, s_free, s_rows, s_turn)

            @block.tensor
            def _(pe):
                pe.wait_ge(s_w, 16 * BLK)

                def chunk(c, i, b, blk0, width=T):
                    bl = blocks(width)
                    pe.wait_ge(s_in[b], i * 32 + 32)
                    pe.sem_inc(s_turn, 1)
                    for n, (k, w) in enumerate(bl):
                        r = nc.tensor.transpose(p_e[0:w * EA, n // 4, (n % 4) * P:(n % 4 + 1) * P], ea[b][:, k * EA:(k + w) * EA], ident[:])
                    r.then_inc(s_et, 1)
                    pe.wait_ge(s_ev, c + 1)
                    pe.wait_ge(s_own, c + 1)
                    pe.wait_ge(s_rows[b], i * (16 * T) + 16 * width)
                    for n, (k, w) in enumerate(bl):
                        par = (b * NB + n) % 2
                        ph = p_h[par]
                        pe.wait_ge(s_pf, blk0 + n + 1)
                        for m in range(0, w, 4):
                            ww = min(4, w - m)
                            bank = ph[:, m // 4, 0:ww * HID]
                            nc.tensor.matmul(bank, ident[:], nbr[b][:, k + m:k + m + ww, :].rearrange("p t f -> p (t f)"), start=True, stop=False)
                            for t in range(m, m + ww):
                                nc.tensor.matmul(ph[:, m // 4, (t - m) * HID:(t - m + 1) * HID], eaT[0:w * EA, n, :], wea[0:w * EA, t, :], start=False, stop=False)
                            r = nc.tensor.matmul(bank, ident[:], own[b][:, k + m:k + m + ww, :].rearrange("p t f -> p (t f)"), start=False, stop=True)
                        r.then_inc(s_ph, 1)
                    pe.wait_ge(s_ph, blk0 + len(bl))
                    nc.tensor.sem_inc(s_done, 1)
                    nc.tensor.sem_inc(s_free[b], 1)
                with nc.Fori(0, PAIRS, engines=[nc.tensor.engine]) as i:
                    for b in range(2):
                        chunk(i * 2 + b, i, b, i * (2 * NB) + b * NB)
                chunk(2 * PAIRS, PAIRS, 0, 2 * PAIRS * NB, TAIL)

            @block.scalar
            def _(act):
                act.sem_inc(s_pf, 2)
                act.sem_inc(s_free[0], 1)
                act.sem_inc(s_free[1], 1)

                def chunk(c, b, blk0, width=T):
                    bl = blocks(width)
                    act.wait_ge(s_et, c + 1)
                    full = [n for n, (k, w) in enumerate(bl) if w == BLK]
                    flat = p_e[:].rearrange("p k n -> p (k n)")
                    r = nc.scalar.activation(eaT[:, 0:len(full), :], flat[0:BLK * EA, 0:len(full) * P].rearrange("p (k n) -> p k n", n=P), ACT.Copy)
                    if len(full) < len(bl):
                        w = bl[-1][1]
                        r = nc.scalar.activation(eaT[0:w * EA, len(full), :], flat[0:w * EA, len(full) * P:(len(full) + 1) * P], ACT.Copy)
                    r.then_inc(s_ev, 1)
                    for n, (k, w) in enumerate(bl):
                        par = (b * NB + n) % 2
                        z = p_h[par][:].rearrange("p k n -> p (k n)")[:, 0:w * HID].rearrange("p (t f) -> p t f", f=HID)
                        act.wait_ge(s_ph, blk0 + n + 1)
                        act.wait_ge(s_ef, blk0 + n + 1)
                        nc.scalar.activation(ee[par][:, 0:w, :], z, ACT.Exp)
                        nc.scalar.activation(rr[par][:, 0:w, :], z, ACT.Relu).then_inc(s_pf, 1)
                        act.wait_ge(s_pf, blk0 + n + 3)
                        nc.scalar.activation(rr[par][:, 0:w, :], rr[par][:, 0:w, :], ACT.Copy, bias=-1.0).then_inc(s_er, 1)
                with nc.Fori(0, PAIRS, engines=[nc.scalar.engine]) as i:
                    for b in range(2):
                        chunk(i * 2 + b, b, i * (2 * NB) + b * NB)
                chunk(2 * PAIRS, 0, 2 * PAIRS * NB, TAIL)

            @block.vector
            def _(dve):
                st = Steps(dve, s_v)
                nc.vector.memset(wea[:], 0.0).then_inc(s_w2, 1)
                st.step(nc.vector.memset(hcarry[:], 0.0))
                st.wait()
                dve.sem_inc(s_ef, 2)

                def spread(c, b, lo_f, hi_f):
                    for f in range(lo_f, hi_f):
                        r = nc.vector.tensor_tensor_scan(own[b][:, :, f], keep[:, ds(c * T, T)], own[b][:, :, f], pcarry[:, f:f + 1], ALU.mult, ALU.add)
                    return r

                K = 4
                FB = -(-HID // NB)
                dve.wait_ge(s_in[0], 32)
                st.link(spread(0, 0, 0, HID))
                st.link(nc.vector.tensor_copy(pcarry[:], own[0][:, T - 1, :]))
                dve.sem_inc(s_own, 1)
                setup = st.n

                def chunk(c, b, blk0, in_next, width=T):
                    st = Steps(dve, s_v, c * K + setup)
                    bl = blocks(width)
                    dve.wait_ge(s_out, c * 16)
                    if in_next is not None:
                        dve.wait_ge(s_in[1 - b], in_next)
                    for n, (k, w) in enumerate(bl):
                        par = (b * NB + n) % 2
                        if in_next is not None:
                            r = spread(c + 1, 1 - b, n * FB, min(HID, (n + 1) * FB))
                        dve.wait_ge(s_er, blk0 + n + 1)
                        nc.vector.scalar_tensor_tensor(hs[:, k:k + w, :], ee[par][:, 0:w, :], 1.0, rr[par][:, 0:w, :], ALU.min, ALU.add).then_inc(s_ef, 1)
                    if in_next is not None:
                        st.step(r)
                    else:
                        dve.sem_inc(s_v, 1)
                        st.n += 1
                    dve.wait_ge(s_ef, blk0 + len(bl) + 2)
                    st.wait()
                    if in_next is not None:
                        st.link(nc.vector.tensor_copy(pcarry[:], own[1 - b][:, T - 1, :]))
                        dve.sem_inc(s_own, 1)
                    else:
                        dve.sem_inc(s_v, 1)
                        st.n += 1
                    for f in range(HID):
                        r = nc.vector.tensor_tensor_scan(hs[:, 0:width, f], keep[:, ds(c * T, width)], hs[:, 0:width, f], hcarry[:, f:f + 1], ALU.mult, ALU.add)
                    st.link(r)
                    dve.sem_inc(s_o, 1)
                    st.link(nc.vector.tensor_copy(hcarry[:], hs[:, width - 1, :]))
                    assert st.n == K
                with nc.Fori(0, PAIRS, engines=[nc.vector.engine]) as i:
                    chunk(i * 2, 0, i * (2 * NB), i * 32 + 32)
                    chunk(i * 2 + 1, 1, i * (2 * NB) + NB, i * 32 + 64)
                chunk(2 * PAIRS, 0, 2 * PAIRS * NB, None, TAIL)
                nc.vector.tensor_copy(last0[:], hcarry[:]).then_inc(s_v, 1)

        boundary("mlp_boundary", last0[:], scan_d[2], HID, ALU.add, 0.0)
        node_block("mlp_nodes", 2, scan_d[2], HID, x_d[1])

        plain_edges("gcn_edges", feat_d, scan_d[3], keep, ALU.add, 0.0, False)
        boundary("gcn_boundary", last0[:, 0:D], scan_d[3], D, ALU.add, 0.0)
        node_block("gcn_nodes", 3, scan_d[3], D, x_d[2])


_INS = ['x', 'src', 'dst', 'edge_attr_6', 'L0_gnn_Wq', 'L0_gnn_Wk', 'L0_gnn_Wv', 'L0_gnn_Wo', 'L1_gnn_W', 'L1_gnn_b',
        'L2_gnn_phi_w1', 'L2_gnn_phi_b1', 'L2_gnn_phi_w2', 'L2_gnn_phi_b2', 'L2_gnn_g_w1', 'L2_gnn_g_b1',
        'L2_gnn_g_w2', 'L2_gnn_g_b2', 'L3_gnn_W']


def kernel(**inputs):
    import numpy as _np
    import concourse.bacc as _bacc
    from concourse import mybir as _mybir
    from concourse.bass_utils import run_bass_kernel_spmd as _run

    nc = _bacc.Bacc("TRN2", target_bir_lowering=False, num_devices=1)
    arrays, ap = {}, {}
    for name in _INS:
        a = _np.asarray(inputs[name])
        if name == 'L1_gnn_W':
            a = a.T
        a = _np.ascontiguousarray(a)
        arrays["in_" + name] = a
        ap[name] = nc.dram_tensor("in_" + name, a.shape, _mybir.dt.from_np(a.dtype), kind="ExternalInput").ap()
    out = nc.dram_tensor("out_0", inputs['x'].shape, _mybir.dt.from_np(_np.dtype('float32')), kind="ExternalOutput").ap()
    build(nc, ap['x'], ap['src'], ap['dst'], ap['edge_attr_6'], (ap['L0_gnn_Wk'], ap['L0_gnn_Wv'], ap['L0_gnn_Wq']),
          ap['L0_gnn_Wo'], ap['L1_gnn_W'], ap['L1_gnn_b'], ap['L2_gnn_phi_w1'], ap['L2_gnn_phi_b1'], ap['L2_gnn_phi_w2'],
          ap['L2_gnn_phi_b2'], ap['L2_gnn_g_w1'], ap['L2_gnn_g_b1'], ap['L2_gnn_g_w2'], ap['L2_gnn_g_b2'], ap['L3_gnn_W'], out)
    r = _run(nc, [arrays], core_ids=[0])
    return r.results[0]["out_0"]
```

```python
import concourse.bass as bass
from concourse import mybir
from contextlib import ExitStack, contextmanager

P = 128
D = 64
HEADS = 4
HID = 128
EA = 6
T = 50
G = 10
BIG = 1.0e30
SKIP = 8.0e6
MAGIC = 12582912.0
EPS = 1e-5


def build(nc, x_in, src_in, dst_in, ea_in, wkvq_parts, wo_in, w1t_in, b1_in, pw1_in, pb1_in, pw2_in, pb2_in,
          gw1_in, gb1_in, gw2_in, gb2_in, w3_in, out):
    f32, bf16, i32 = mybir.dt.float32, mybir.dt.bfloat16, mybir.dt.int32
    ALU, ACT, AX = mybir.AluOpType, mybir.ActivationFunctionType, mybir.AxisListType
    ds = bass.ds

    N = x_in.shape[0]
    E = src_in.shape[0]
    TALL = E // P
    PAIRS = TALL // (2 * T)
    TAIL = TALL - 2 * PAIRS * T
    assert E == P * TALL and 0 < TAIL <= T and TAIL % 5 == 0
    J = -(-N // P)
    J = -(-J // (2 * G)) * 2 * G
    NPART = N // J
    assert N == NPART * J and NPART <= P
    NPAD = P * J
    GPAIRS = J // (2 * G)

    def dram(name, shape, dt=f32):
        return nc.dram_tensor(name, list(shape), dt, kind="Internal").ap()

    x_d = [dram(f"x_layer{n}", (NPAD, D)) for n in range(3)]
    kv_d = dram("kv_table", (NPAD, 2 * D))
    q_d = dram("q_table", (NPAD, D))
    own1_d = dram("edgeconv_own", (NPAD, D))
    nbr1_d = dram("edgeconv_neighbour_table", (NPAD, D))
    feat_d = dram("gcn_table", (NPAD, D))
    start_d = dram("rows_at_first_edges", (E, D))
    ROW0 = D + 2 * HEADS
    scan_d = [dram("scan_attention", (E, ROW0)), dram("scan_max", (E, D)), dram("scan_mlp", (E, HID)),
              dram("scan_gcn", (E, D))]
    last_d = dram("last_edge", (NPAD, 1), i32)
    first_d = dram("first_edge", (NPAD, 1), i32)

    def nodes(ap):
        return ap.rearrange("(p j) f -> p j f", p=P)

    def edges(ap):
        return ap.rearrange("(p t) f -> p t f", p=P)

    src_v = src_in.rearrange("(p t) -> p t", p=P)
    dst_v = dst_in.rearrange("(p t) -> p t", p=P)
    ea_v = edges(ea_in)

    ctx = ExitStack()
    ctx.enter_context(nc.allow_non_contiguous_dma(reason="columns of small tables"))

    def bc(ap, dim, n):
        wide = ap.unsqueeze(dim)
        shape = list(wide.shape)
        shape[dim] = n
        return wide.broadcast_to(shape)

    class Steps:

        def __init__(self, eng, sem, base=0):
            self.eng, self.sem, self.base, self.n = eng, sem, base, 0

        def step(self, ins):
            ins.then_inc(self.sem, 1)
            self.n += 1

        def wait(self):
            self.eng.wait_ge(self.sem, self.base + self.n)

        def link(self, ins):
            self.step(ins)
            self.wait()

    with ctx:
        phase_sems = []

        def sem(name):
            phase_sems.append(nc.alloc_semaphore(name=name))
            return phase_sems[-1]

        @contextmanager
        def phase(name):
            with ExitStack() as scope:
                with nc.Block(name) as block:
                    yield scope, block
            nc.clear_and_free_semaphores(phase_sems)
            phase_sems.clear()
            nc.all_engine_barrier()

        def maker(scope):
            def sb(name, shape, dt=f32):
                return scope.enter_context(nc.sbuf_tensor(name, list(shape), dt))

            def ps(name, shape, dt=f32):
                return scope.enter_context(nc.psum_tensor(name, list(shape), dt))
            return sb, ps

        sb, _ = maker(ctx)
        keep = sb("keep", [P, (2 * PAIRS + 1) * T])
        pen = sb("pen", [P, TALL])
        ident = sb("ident", [P, P])
        iota_row = sb("iota_row", [P, P], bf16)
        cnt_in = sb("cnt_in", [P, J])
        nonempty = sb("nonempty", [P, J])
        rcnt = sb("rcnt", [P, J])
        nsrc = sb("nsrc", [P, J])
        ndst = sb("ndst", [P, J])
        whole = sb("whole", [P, 1])
        fixidx = sb("fixidx", [P, 1], i32)
        qcarry = sb("qcarry", [P, D])
        dfirst = sb("dfirst", [P, 1], i32)

        with phase("setup") as (scope, block):
            sb, ps = maker(scope)
            HG = 25
            HPAIRS = TALL // (2 * HG)
            HODD = TALL // HG - 2 * HPAIRS
            assert TALL % HG == 0
            dstx = sb("dstx", [P, TALL + 1], i32)
            hi32 = sb("hi32", [P, TALL])
            hi = sb("hi", [P, TALL], bf16)
            lo = sb("lo", [P, TALL], bf16)
            ohi = [sb(f"ohi{b}", [P, HG, P], bf16) for b in range(2)]
            olo = [sb(f"olo{b}", [P, HG, J], bf16) for b in range(2)]
            zrow = sb("zrow", [P, P], bf16)
            iota32 = sb("iota32", [P, P], i32)
            tri = sb("tri", [P, P])
            onesJ = sb("onesJ", [P, J])
            cum = sb("cum", [P, J])
            tmpJ = sb("tmpJ", [P, J])
            tmpK = sb("tmpK", [P, J])
            firsti = sb("firsti", [P, J], i32)
            lasti = sb("lasti", [P, J], i32)
            base = sb("base", [P, 1])
            zeros = sb("zeros", [P, T * D])
            xg = [sb(f"xg{b}", [P, G, D]) for b in range(2)]
            wkvq = sb("wkvq", [P, 2, 3 * D])
            xT = sb("xT", [P, G // 2, P])
            kv_s = sb("kv_s", [P, G, 2 * D])
            q_s = sb("q_s", [P, G, D])
            p_tr = ps("p_tr", [P, 1024])
            p_mm = ps("p_mm", [P, 5, 512])
            p_h = ps("p_h", [P, 512])

            s_w, s_dst, s_z, s_dmin, s_const, s_id = (sem(n) for n in ("su_w", "su_dst", "su_zero", "su_min", "su_const", "su_id"))
            s_x = [sem(f"su_x{b}") for b in range(2)]
            s_xz, s_tr, s_xt, s_mm, s_tab, s_st, s_oh, s_hm, s_v, s_tot, s_base, s_fl, s_fill, s_deg = (
                sem("su_" + n) for n in ("xz", "tr", "xt", "mm", "tab", "st", "oh", "hm", "v", "tot", "base", "fl", "fill", "deg"))

            @block.sync
            def _(sp):
                sp.dma_start(dstx[:, 1:TALL + 1], dst_v).then_inc(s_dst, 16)
                sp.wait_ge(s_dmin, 1)
                sp.dma_start(dstx[1:P, 0:1], dst_v[0:P - 1, TALL - 1:TALL]).then_inc(s_dst, 16)
                sp.wait_ge(s_xz, 1)
                for h in range(2):
                    for n, w in enumerate(wkvq_parts):
                        sp.dma_start(wkvq[h * D:(h + 1) * D, h, n * D:(n + 1) * D], w).then_inc(s_w, 16)
                xv = x_in.rearrange("(p j) f -> p j f", j=J)

                def load_x(g, b):
                    sp.dma_start(xg[b][0:NPART], xv[:, ds(g * G, G), :]).then_inc(s_x[b], 16)

                def store(g):
                    sp.wait_ge(s_tab, g * 2 + 2)
                    sp.dma_start(nodes(kv_d)[:, ds(g * G, G), :], kv_s[:]).then_inc(s_st, 16)
                    sp.dma_start(nodes(q_d)[:, ds(g * G, G), :], q_s[:]).then_inc(s_st, 16)
                load_x(0, 0)
                load_x(1, 1)
                if GPAIRS > 1:
                    with nc.Fori(0, GPAIRS - 1, engines=[nc.sync.engine]) as i:
                        for b in range(2):
                            store(i * 2 + b)
                            load_x(i * 2 + b + 2, b)
                for b in range(2):
                    store(2 * GPAIRS - 2 + b)
                sp.wait_ge(s_z, 1)
                with nc.Fori(0, 2 * PAIRS, engines=[nc.sync.engine]) as i:
                    sp.dma_start(edges(start_d)[:, ds(i * T, T), :], zeros[:].rearrange("p (t f) -> p t f", f=D)).then_inc(s_fill, 16)
                sp.dma_start(edges(start_d)[:, 2 * PAIRS * T:TALL, :],
                             zeros[:, 0:TAIL * D].rearrange("p (t f) -> p t f", f=D)).then_inc(s_fill, 16)
                sp.wait_ge(s_fl, 2)
                sp.dma_start(nodes(first_d)[:, :, 0], firsti[:]).then_inc(s_st, 16)
                sp.dma_start(nodes(last_d)[:, :, 0], lasti[:]).then_inc(s_st, 16)
                sp.wait_ge(s_fill, 16 * (2 * PAIRS + 1))
                sp.wait_ge(s_st, 16 * (4 * GPAIRS + 2))

            @block.gpsimd
            def _(pool):
                nc.gpsimd.iota(iota32[:], pattern=[[1, P]], base=0, channel_multiplier=0).then_inc(s_id, 1)
                nc.gpsimd.memset(ident[:], 0.0).then_inc(s_id, 1)
                nc.gpsimd.memset(tri[:], 1.0).then_inc(s_id, 1)
                pool.wait_ge(s_id, 3)
                nc.gpsimd.affine_select(out=ident[:], in_=ident[:], compare_op=ALU.not_equal, fill=1.0,
                                        base=0, pattern=[[-1, P]], channel_multiplier=1).then_inc(s_id, 1)
                nc.gpsimd.affine_select(out=tri[:], in_=tri[:], compare_op=ALU.is_gt, fill=0.0,
                                        base=0, pattern=[[1, P]], channel_multiplier=-1).then_inc(s_id, 1)

            @block.vector
            def _(dve):
                st = Steps(dve, s_v)
                nc.vector.memset(dstx[:, 0:1], -1).then_inc(s_dmin, 1)
                st.step(nc.vector.memset(xg[0][:], 0.0))
                st.step(nc.vector.memset(xg[1][:], 0.0))
                st.step(nc.vector.memset(wkvq[:], 0.0))
                st.wait()
                dve.sem_inc(s_xz, 1)
                nc.vector.memset(zeros[:], 0.0).then_inc(s_z, 1)
                st.step(nc.vector.memset(zrow[:], 0.0))
                st.step(nc.vector.memset(onesJ[:], 1.0))
                st.step(nc.vector.memset(keep[:], 0.0))
                dve.wait_ge(s_id, 1)
                st.step(nc.vector.tensor_copy(iota_row[:], iota32[:]))
                st.wait()
                dve.sem_inc(s_const, 1)
                dve.wait_ge(s_dst, 32)
                st.link(nc.vector.tensor_scalar(hi32[:], dstx[:, 1:TALL + 1], -(J - 1) / 2, 1.0 / J, ALU.add, ALU.mult))
                st.link(nc.vector.tensor_scalar(hi32[:], hi32[:], MAGIC, -MAGIC, ALU.add, ALU.add))
                st.step(nc.vector.tensor_copy(hi[:], hi32[:]))
                st.step(nc.vector.scalar_tensor_tensor(lo[:], hi32[:], -float(J), dstx[:, 1:TALL + 1], ALU.mult, ALU.add))
                st.step(nc.vector.tensor_copy(dfirst[:], dstx[:, 1:2]))
                st.link(nc.vector.tensor_tensor(keep[:, 0:TALL], dstx[:, 1:TALL + 1], dstx[:, 0:TALL], ALU.is_equal))
                st.link(nc.vector.tensor_scalar(pen[:], keep[:, 0:TALL], -1.0, BIG, ALU.add, ALU.mult))

                def onehots(c, b):
                    nc.vector.tensor_tensor(ohi[b][:], bc(hi[:, ds(c * HG, HG)], 2, P), bc(iota_row[:], 1, HG), ALU.is_equal)
                    nc.vector.tensor_tensor(olo[b][:], bc(lo[:, ds(c * HG, HG)], 2, J), bc(iota_row[:, 0:J], 1, HG),
                                            ALU.is_equal).then_inc(s_oh, 1)
                onehots(0, 0)
                onehots(1, 1)
                with nc.Fori(1, HPAIRS, engines=[nc.vector.engine]) as i:
                    for b in range(2):
                        dve.wait_ge(s_hm, i * 2 + b - 1)
                        onehots(i * 2 + b, b)
                if HODD:
                    dve.wait_ge(s_hm, 2 * HPAIRS - 1)
                    onehots(2 * HPAIRS, 0)
                dve.wait_ge(s_hm, 2 * HPAIRS + HODD)
                st.link(nc.vector.tensor_copy(cnt_in[:], p_h[:, 0:J]))
                nc.vector.tensor_tensor_scan(cum[:], onesJ[:], cnt_in[:], 0.0, ALU.mult, ALU.add).then_inc(s_tot, 1)
                st.step(nc.vector.tensor_scalar(nonempty[:], cnt_in[:], 0.0, None, ALU.is_gt))
                st.link(nc.vector.tensor_scalar(tmpJ[:], cnt_in[:], 1.0, None, ALU.max))
                dve.sem_inc(s_deg, 1)
                st.step(nc.vector.reciprocal(rcnt[:], tmpJ[:]))
                dve.wait_ge(s_base, 1)
                st.link(nc.vector.tensor_copy(base[:], p_h[:, 0:1]))
                st.link(nc.vector.tensor_scalar(cum[:], cum[:], base[:, 0:1], -1.0, ALU.add, ALU.add))
                st.step(nc.vector.tensor_tensor(tmpK[:], cum[:], cnt_in[:], ALU.subtract))
                nc.vector.tensor_scalar(lasti[:], cum[:], 0.0, None, ALU.max).then_inc(s_fl, 1)
                st.wait()
                st.link(nc.vector.tensor_scalar(tmpK[:], tmpK[:], 1.0 - SKIP, None, ALU.add))
                st.link(nc.vector.tensor_tensor(tmpK[:], tmpK[:], nonempty[:], ALU.mult))
                nc.vector.tensor_scalar(firsti[:], tmpK[:], SKIP, None, ALU.add).then_inc(s_fl, 1)

            @block.scalar
            def _(act):
                def evac(g):
                    act.wait_ge(s_tr, g + 1)
                    nc.scalar.activation(xT[:], p_tr[:, 0:G * D].rearrange("p (k n) -> p k n", n=P), ACT.Copy).then_inc(s_xt, 1)
                    act.wait_ge(s_mm, g + 1)
                    act.wait_ge(s_st, g * 32)
                    mm = p_mm[:, :, 0:6 * D].rearrange("p k (h f) -> p k h f", h=2)
                    nc.scalar.activation(kv_s[:].rearrange("p (k h) f -> p k h f", h=2), mm[:, :, :, 0:2 * D], ACT.Copy).then_inc(s_tab, 1)
                    nc.scalar.activation(q_s[:].rearrange("p (k h) f -> p k h f", h=2), mm[:, :, :, 2 * D:3 * D], ACT.Copy,
                                         scale=(D // HEADS) ** -0.5).then_inc(s_tab, 1)
                with nc.Fori(0, 2 * GPAIRS, engines=[nc.scalar.engine]) as g:
                    evac(g)
                act.wait_ge(s_deg, 1)
                nc.scalar.activation(ndst[:], tmpJ[:], ACT.Sqrt).then_inc(s_deg, 1)

            @block.tensor
            def _(pe):
                pe.wait_ge(s_id, 5)
                pe.wait_ge(s_w, 96)

                def tables(g, i, b):
                    pe.wait_ge(s_x[b], i * 16 + 16)
                    for k in range(G // 2):
                        tr = nc.tensor.transpose(p_tr[:, k * P:(k + 1) * P], xg[b][:, 2 * k:2 * k + 2, :].rearrange("p h f -> p (h f)"), ident[:])
                    tr.then_inc(s_tr, 1)
                    pe.wait_ge(s_tab, g * 2)
                    pe.wait_ge(s_xt, g + 1)
                    for k in range(G // 2):
                        mm = nc.tensor.matmul(p_mm[:, k, 0:6 * D], xT[:, k, :], wkvq[:].rearrange("p h f -> p (h f)"), start=True, stop=True)
                    mm.then_inc(s_mm, 1)
                with nc.Fori(0, GPAIRS, engines=[nc.tensor.engine]) as i:
                    for b in range(2):
                        tables(i * 2 + b, i, b)
                pe.wait_ge(s_const, 1)
                nc.tensor.matmul(p_h[:, 0:J], zrow[:], zrow[:, 0:J], start=True, stop=False)

                def count(c, b, last=False):
                    pe.wait_ge(s_oh, c + 1)
                    for t in range(HG):
                        mm = nc.tensor.matmul(p_h[:, 0:J], ohi[b][:, t, :], olo[b][:, t, :], start=False, stop=last and t == HG - 1)
                    mm.then_inc(s_hm, 1)
                with nc.Fori(0, HPAIRS - 1, engines=[nc.tensor.engine]) as i:
                    for b in range(2):
                        count(i * 2 + b, b)
                for b in range(2):
                    count(2 * HPAIRS - 2 + b, b, last=(not HODD and b == 1))
                if HODD:
                    count(2 * HPAIRS, 0, last=True)
                pe.wait_ge(s_tot, 1)
                nc.tensor.matmul(p_h[:, 0:1], tri[:], cum[:, J - 1:J], start=True, stop=True).then_inc(s_base, 1)

        def scatter_rows(name, rows_d, width, carry, with_bounds):
            with phase(name) as (scope, block):
                sb, ps = maker(scope)
                idx = [sb(f"{name}_idx{b}", [P, G], i32) for b in range(2)]
                row = [sb(f"{name}_row{b}", [P, G, width]) for b in range(2)]
                lastf = sb(f"{name}_last", [P, 1], i32)
                t = sb(f"{name}_t", [P, 4])
                pidx = sb(f"{name}_p", [P, 2], i32)
                s_in = [sem(f"{name}_in{b}") for b in range(2)]
                s_sc = [sem(f"{name}_sc{b}") for b in range(2)]
                s_g, s_v, s_io, s_turn = sem(f"{name}_g"), sem(f"{name}_v"), sem(f"{name}_io"), sem(f"{name}_turn")

                @block.sync
                def _(sp):
                    def load(g, b):
                        sp.dma_start(idx[b][:], nodes(first_d)[:, ds(g * G, G), 0]).then_inc(s_in[b], 16)
                        sp.dma_start(row[b][:], nodes(rows_d)[:, ds(g * G, G), :]).then_inc(s_in[b], 16)
                    load(0, 0)
                    load(1, 1)
                    if GPAIRS > 1:
                        with nc.Fori(1, GPAIRS, engines=[nc.sync.engine]) as i:
                            for b in range(2):
                                sp.wait_ge(s_sc[b], i * (16 * G))
                                load(i * 2 + b, b)

                @block.gpsimd
                def _(pool):
                    nc.gpsimd.indirect_dma_start(carry[:], None, rows_d, bass.IndirectOffsetOnAxis(ap=dfirst[:, 0:1], axis=0)).then_inc(s_g, 16)
                    if with_bounds:
                        nc.gpsimd.indirect_dma_start(lastf[:], None, last_d, bass.IndirectOffsetOnAxis(ap=dfirst[:, 0:1], axis=0)).then_inc(s_g, 16)
                        nc.gpsimd.iota(pidx[:, 0:1], pattern=[[1, 1]], base=0, channel_multiplier=TALL).then_inc(s_io, 1)
                    else:
                        pool.sem_inc(s_io, 1)
                    with nc.Fori(0, GPAIRS, engines=[nc.gpsimd.engine]) as i:
                        for b in range(2):
                            pool.wait_ge(s_in[b], i * 32 + 32)
                            pool.sem_inc(s_turn, 1)
                            for j in range(G):
                                nc.gpsimd.indirect_dma_start(start_d, bass.IndirectOffsetOnAxis(ap=idx[b][:, j:j + 1], axis=0),
                                                             row[b][:, j, :], None, bounds_check=E - 1, oob_is_err=False).then_inc(s_sc[b], 16)
                    pool.wait_ge(s_sc[0], GPAIRS * 16 * G)
                    pool.wait_ge(s_sc[1], GPAIRS * 16 * G)
                    pool.wait_ge(s_g, 32 if with_bounds else 16)

                if with_bounds:
                    @block.vector
                    def _(dve):
                        st = Steps(dve, s_v)
                        dve.wait_ge(s_g, 32)
                        dve.wait_ge(s_io, 1)
                        st.step(nc.vector.tensor_copy(t[:, 0:1], lastf[:]))
                        st.link(nc.vector.tensor_copy(t[:, 1:2], pidx[:, 0:1]))
                        st.link(nc.vector.tensor_tensor(t[:, 2:3], t[:, 0:1], t[:, 1:2], ALU.subtract))
                        st.link(nc.vector.tensor_scalar(whole[:], t[:, 2:3], float(TALL - 1), None, ALU.is_ge))
                        st.link(nc.vector.tensor_tensor(whole[:], whole[:], keep[:, 0:1], ALU.mult))
                        st.link(nc.vector.tensor_scalar(t[:, 3:4], t[:, 2:3], float(TALL - 1), None, ALU.is_le))
                        st.link(nc.vector.tensor_tensor(t[:, 3:4], t[:, 3:4], keep[:, 0:1], ALU.mult))
                        st.link(nc.vector.tensor_scalar(t[:, 0:1], t[:, 0:1], -SKIP, None, ALU.add))
                        st.link(nc.vector.tensor_tensor(t[:, 0:1], t[:, 0:1], t[:, 3:4], ALU.mult))
                        st.link(nc.vector.tensor_scalar(fixidx[:], t[:, 0:1], SKIP, None, ALU.add))
                        st.link(nc.vector.reciprocal(ndst[:], ndst[:]))
                        st.link(nc.vector.tensor_tensor(ndst[:], ndst[:], nonempty[:], ALU.mult))

        scatter_rows("scatter_q", q_d, D, qcarry, True)

        def pool_gathers(pool, table, idx, rows, s_idx, s_free, s_rows, s_turn, at=0):
            def chunk(b, i, width):
                pool.wait_ge(s_idx[b], i * 16 + 16)
                pool.wait_ge(s_free[b], i + 1)
                pool.sem_inc(s_turn, 1)
                for t in range(width):
                    nc.gpsimd.indirect_dma_start(rows[b][:, t, at:], None, table,
                                                 bass.IndirectOffsetOnAxis(ap=idx[b][:, t:t + 1], axis=0)).then_inc(s_rows[b], 16)
            with nc.Fori(0, PAIRS, engines=[nc.gpsimd.engine]) as i:
                for b in range(2):
                    chunk(b, i, T)
            chunk(0, PAIRS, TAIL)

        def boundary(name, last, scan_out, width, op, none):
            with phase(name) as (scope, block):
                sb, ps = maker(scope)
                gate = sb(f"{name}_gate", [P, width])
                carry = sb(f"{name}_carry", [P, width])
                rows = sb(f"{name}_rows", [P, width])
                gateT = sb(f"{name}_gateT", [width, P])
                runT = sb(f"{name}_runT", [width, P + 1])
                pa, pb, pc = ps(f"{name}_pa", [P, 512]), ps(f"{name}_pb", [P, 512]), ps(f"{name}_pc", [P, 512])
                s_v, s_t, s_g, s_s, s_m = (sem(f"{name}_{n}") for n in ("v", "t", "g", "s", "m"))
                first = ALU.mult if op == ALU.add else ALU.add

                @block.vector
                def _(dve):
                    st = Steps(dve, s_v)
                    nc.vector.memset(rows[:], 0.0).then_inc(s_m, 1)
                    st.step(nc.vector.memset(runT[:, 0:1], none))
                    if op == ALU.add:
                        st.step(nc.vector.tensor_copy(gate[:], bc(whole[:, 0], 1, width)))
                    else:
                        st.step(nc.vector.tensor_scalar(gate[:], bc(whole[:, 0], 1, width), -1.0, BIG, ALU.add, ALU.mult))
                    dve.wait_ge(s_t, 2)
                    st.link(nc.vector.tensor_copy(gateT[:], pa[0:width, 0:P]))
                    nc.vector.tensor_tensor_scan(runT[:, 1:P + 1], gateT[:], pb[0:width, 0:P], none, first, op).then_inc(s_v, 1)
                    dve.wait_ge(s_t, 3)
                    st.n += 1
                    st.link(nc.vector.tensor_copy(carry[:], pc[:, 0:width]))
                    dve.wait_ge(s_g, 16)
                    nc.vector.tensor_tensor(rows[:], rows[:], carry[:], op).then_inc(s_m, 1)

                @block.tensor
                def _(pe):
                    pe.wait_ge(s_v, 2)
                    nc.tensor.transpose(pa[0:width, 0:P], gate[:], ident[:]).then_inc(s_t, 1)
                    nc.tensor.transpose(pb[0:width, 0:P], last, ident[:]).then_inc(s_t, 1)
                    pe.wait_ge(s_v, 4)
                    nc.tensor.transpose(pc[:, 0:width], runT[:, 0:P], ident[0:width, 0:width]).then_inc(s_t, 1)

                @block.gpsimd
                def _(pool):
                    pool.wait_ge(s_m, 1)
                    nc.gpsimd.indirect_dma_start(rows[:], None, scan_out, bass.IndirectOffsetOnAxis(ap=fixidx[:, 0:1], axis=0),
                                                 bounds_check=E - 1, oob_is_err=False).then_inc(s_g, 16)
                    pool.wait_ge(s_m, 2)
                    nc.gpsimd.indirect_dma_start(scan_out, bass.IndirectOffsetOnAxis(ap=fixidx[:, 0:1], axis=0), rows[:], None,
                                                 bounds_check=E - 1, oob_is_err=False).then_inc(s_s, 16)
                    pool.wait_ge(s_s, 16)

        def node_block(name, layer, scan_out, width, x_prev, own_d=None):
            with phase(name) as (scope, block):
                sb, ps = maker(scope)

                def t(n, shape, dt=f32):
                    return sb(f"{name}_{n}", shape, dt)
                NG = 2 * GPAIRS
                XW = D + 1 if layer == 2 else D
                idx = [t(f"idx{b}", [P, G], i32) for b in range(2)]
                agg = [t(f"agg{b}", [P, G, width]) for b in range(2)]
                x_all = t("x", [P, J, XW])
                own_all = t("own", [P, J, D]) if own_d is not None else None
                last_all = t("last", [P, J], i32)
                first_all = t("first", [P, J], i32) if layer == 1 else None
                fidx = [t(f"fidx{b}", [P, G], i32) for b in range(2)] if layer == 1 else None
                y = t("y", [P, G, D])
                sq = t("sq", [P, G, D])
                s1, s2, rt = t("s1", [P, G]), t("s2", [P, G]), t("rt", [P, G])
                xn = [t(f"xn{b}", [P, G, D]) for b in range(2)]
                s_rows, s_ix, s_copy, s_fcopy = (sem(f"{name}_{n}") for n in ("rows", "ix", "copy", "fcopy"))
                s_ag = [sem(f"{name}_ag{b}") for b in range(2)]
                s_st = [sem(f"{name}_st{b}") for b in range(2)]
                s_sc = [sem(f"{name}_sc{b}") for b in range(2)] if layer == 1 else None
                s_vf, s_vb, s_vm, s_w, s_wz, s_w2, s_aggf, s_a, s_tr, s_evf, s_of, s_y, s_var, s_rt, s_xn, s_turn = (
                    sem(f"{name}_{n}") for n in ("vf", "vb", "vm", "w", "wz", "w2", "aggf", "a", "tr", "evf", "of", "y", "var", "rt", "xn", "turn"))
                if layer != 1:
                    p_o = ps(f"{name}_po", [P, 2, 512])
                diagonal = []
                if layer == 0:
                    w_out, w_next = t("wo", [P, 2, D]), t("wn", [P, 2, 2 * D])
                    wa, wb = t("wa", [P, 2, D]), t("wb", [P, 2, D])
                    bias = t("bias", [1, 4, 2, D])
                    ones = t("ones", [1, P])
                    loads = [(w_out[h * D:(h + 1) * D, h, :], wo_in) for h in range(2)]
                    loads += [(wa[h * D:(h + 1) * D, h, :], w1t_in[0:D, :]) for h in range(2)]
                    loads += [(wb[h * D:(h + 1) * D, h, :], w1t_in[D:2 * D, :]) for h in range(2)]
                    loads += [(bias[:, k, 0, :], bc(b1_in, 0, 1)) for k in range(4)]
                    diagonal = [w_out, wa, wb, bias]
                    own_s, nbr_s = t("own_s", [P, G, D]), t("nbr_s", [P, G, D])
                    f4, g4, h4 = t("f4", [P, G, HEADS]), t("g4", [P, G, HEADS]), t("h4", [P, G, HEADS])
                    a = t("a", [P, G, D])
                    aT, xT = t("aT", [P, G // 2, P]), t("xT", [P, G // 2, P])
                    p_ta, p_tx = ps(f"{name}_pta", [P, 640]), None
                    p_tab = ps(f"{name}_ptab", [P, 3, 512])
                    s_dm, s_ex, s_trx, s_evx, s_tab, s_tabs, s_tt = (sem(f"{name}_{n}") for n in ("dm", "ex", "trx", "evx", "tab", "tabs", "tt"))
                elif layer == 1:
                    loads = []
                elif layer == 2:
                    wp2T = t("wp2T", [D, HID])
                    wp2, wg1b, wgx, wg2 = t("wp2", [HID, D]), t("wg1b", [D, HID]), t("wgx", [D + 1, HID]), t("wg2", [HID, D])
                    wga = t("wga", [HID, HID])
                    bp2 = t("bp2", [D, D + 1])
                    bg1 = t("bg1", [HID, 1])
                    bg2 = t("bg2", [1, 8, D])
                    xs = t("xs", [P, G, D + 1])
                    ones = t("ones", [1, P])
                    loads = [(wp2[:], pw2_in), (wg1b[:], gw1_in[D:2 * D, :]), (wgx[0:D, :], gw1_in[0:D, :]), (wg2[:], gw2_in),
                             (bp2[:, D:D + 1], pb2_in.unsqueeze(1)), (bg1[:], gb1_in.unsqueeze(1))]
                    loads += [(bg2[:, k, :], bc(gb2_in, 0, 1)) for k in range(8)]
                    diagonal = [bp2]
                    a = t("a", [P, G, HID])
                    aT, xT = t("aT", [P, G, P]), t("xT", [D + 1, G, P])
                    be, br = t("be", [P, G, P]), t("br", [P, G, P])
                    feat_s = t("feat_s", [P, G, D])
                    p_ta, p_z = ps(f"{name}_pta", [P, 3, 512]), ps(f"{name}_pz", [P, 3, 512])
                    s_z, s_el, s_elu, s_feat, s_tabs = (sem(f"{name}_{n}") for n in ("z", "el", "elu", "feat", "tabs"))
                else:
                    w_out = t("wo", [P, 2, D])
                    diagonal = [w_out]
                    loads = [(w_out[h * D:(h + 1) * D, h, :], w3_in) for h in range(2)]
                    a = t("a", [P, G, D])
                    aT = t("aT", [P, G // 2, P])
                    p_ta = ps(f"{name}_pta", [P, 640])
                x_v = x_in.rearrange("(p j) f -> p j f", j=J) if layer == 0 else nodes(x_prev)
                out_v = out.rearrange("(p j) f -> p j f", j=J)
                NXP = NPART if layer == 0 else P

                def slots_of(psum, n):
                    return psum[:].rearrange("p k n -> p (k n)")[:, 0:G * n].rearrange("p (g f) -> p g f", f=n)

                def skewed(eng, front, back, mid=None):
                    def both(g, i, b):
                        front(g + 1, i + b, 1 - b)
                        back(g, i, b)
                        if mid:
                            mid(g + 1, i + b, 1 - b)
                    front(0, 0, 0)
                    if mid:
                        mid(0, 0, 0)
                    if GPAIRS > 1:
                        with nc.Fori(0, GPAIRS - 1, engines=[eng]) as i:
                            for b in range(2):
                                both(i * 2 + b, i, b)
                    both(NG - 2, GPAIRS - 1, 0)
                    back(NG - 1, GPAIRS - 1, 1)

                @block.sync
                def _(sp):
                    sp.dma_start(last_all[:], nodes(last_d)[:, :, 0]).then_inc(s_ix, 16)
                    if layer == 1:
                        sp.dma_start(first_all[:], nodes(first_d)[:, :, 0]).then_inc(s_ix, 16)
                        sp.dma_start(own_all[:], nodes(own_d)).then_inc(s_rows, 16)
                    sp.wait_ge(s_wz, 1)
                    for o, w in loads:
                        sp.dma_start(o, w).then_inc(s_w, 16)
                    sp.dma_start(x_all[0:NXP, :, 0:D], x_v).then_inc(s_rows, 16)

                    def store(g, b):
                        sp.wait_ge(s_xn, g + 1)
                        if layer == 3:
                            sp.dma_start(out_v[:, ds(g * G, G), :], xn[b][0:NPART]).then_inc(s_st[b], 16)
                        else:
                            sp.dma_start(nodes(x_d[layer])[:, ds(g * G, G), :], xn[b][:]).then_inc(s_st[b], 16)
                        if layer == 0:
                            sp.wait_ge(s_tab, g + 1)
                            sp.dma_start(nodes(own1_d)[:, ds(g * G, G), :], own_s[:]).then_inc(s_tabs, 16)
                            sp.dma_start(nodes(nbr1_d)[:, ds(g * G, G), :], nbr_s[:]).then_inc(s_tabs, 16)
                        if layer == 2:
                            sp.wait_ge(s_feat, g + 1)
                            sp.dma_start(nodes(feat_d)[:, ds(g * G, G), :], feat_s[:]).then_inc(s_tabs, 16)
                    with nc.Fori(0, GPAIRS, engines=[nc.sync.engine]) as i:
                        for b in range(2):
                            store(i * 2 + b, b)
                    for b in range(2):
                        sp.wait_ge(s_st[b], 16 * GPAIRS)
                        if layer == 1:
                            sp.wait_ge(s_sc[b], 16 * G * GPAIRS)
                    if layer in (0, 2):
                        sp.wait_ge(s_tabs, 16 * NG * (2 if layer == 0 else 1))

                @block.gpsimd
                def _(pool):
                    pool.wait_ge(s_ix, 16 + 16 * (layer == 1))

                    def gather(g, i, b):
                        pool.wait_ge(s_ag[b], i * (16 * G))
                        nc.gpsimd.tensor_copy(idx[b][:], last_all[:, ds(g * G, G)]).then_inc(s_copy, 1)
                        pool.wait_ge(s_aggf, g + 1)
                        pool.wait_ge(s_copy, g + 1)
                        pool.sem_inc(s_turn, 1)
                        for j in range(G):
                            nc.gpsimd.indirect_dma_start(agg[b][:, j, :], None, scan_out,
                                                         bass.IndirectOffsetOnAxis(ap=idx[b][:, j:j + 1], axis=0)).then_inc(s_ag[b], 16)

                    def scatter(g, i, b):
                        if layer != 1:
                            return
                        pool.wait_ge(s_sc[b], i * (16 * G))
                        nc.gpsimd.tensor_copy(fidx[b][:], first_all[:, ds(g * G, G)]).then_inc(s_fcopy, 1)
                        pool.wait_ge(s_xn, g + 1)
                        pool.wait_ge(s_fcopy, g + 1)
                        pool.sem_inc(s_turn, 1)
                        for j in range(G):
                            nc.gpsimd.indirect_dma_start(start_d, bass.IndirectOffsetOnAxis(ap=fidx[b][:, j:j + 1], axis=0),
                                                         xn[b][:, j, :], None, bounds_check=E - 1, oob_is_err=False).then_inc(s_sc[b], 16)
                    skewed(nc.gpsimd.engine, gather, scatter)

                @block.vector
                def _(dve):
                    su = Steps(dve, s_vm)
                    for w in [x_all] + diagonal:
                        su.step(nc.vector.memset(w[:], 0.0))
                    if layer in (0, 2):
                        su.step(nc.vector.memset(ones[:], 1.0))
                    su.wait()
                    if layer == 2:
                        su.link(nc.vector.tensor_copy(x_all[:, :, D], nonempty[:]))
                    dve.sem_inc(s_wz, 1)
                    dve.sem_inc(s_aggf, 2)
                    if layer == 0:
                        dve.wait_ge(s_w, 16 * len(loads))
                        su.step(nc.vector.tensor_tensor(w_next[:, :, 0:D], wa[:], wb[:], ALU.subtract))
                        su.step(nc.vector.tensor_copy(w_next[:, :, D:2 * D], wb[:]))
                        su.wait()
                        dve.sem_inc(s_w2, 1)
                    if layer == 2:
                        dve.wait_ge(s_w2, 1)
                        su.link(nc.vector.tensor_copy(wp2T[:], p_z[0:D, 0, 0:HID]))
                        dve.sem_inc(s_w2, 1)
                        dve.wait_ge(s_w2, 3)
                        su.step(nc.vector.tensor_copy(wga[:], p_z[:, 1, 0:HID]))
                        su.step(nc.vector.tensor_copy(wgx[D:D + 1, :], p_z[D:D + 1, 2, 0:HID]))
                        su.wait()
                        dve.sem_inc(s_w2, 1)
                    KF = {0: 7, 1: 0, 2: 0, 3: 0}[layer]
                    KB = {0: 8, 1: 10, 2: 10, 3: 8}[layer]

                    def front(g, i, b):
                        st = Steps(dve, s_vf, g * KF)
                        slots = ds(g * G, G)
                        if layer == 1:
                            return
                        dve.wait_ge(s_ag[b], i * (16 * G) + 16 * G)
                        R = agg[b]
                        if layer == 0:
                            M = R[:, :, D + HEADS:D + 2 * HEADS]
                            st.link(nc.vector.tensor_scalar(f4[:], M, -1e9, None, ALU.max))
                            nc.vector.tensor_tensor(g4[:], M, f4[:], ALU.subtract).then_inc(s_dm, 1)
                            dve.wait_ge(s_ex, g + 1)
                            st.link(nc.vector.tensor_tensor(f4[:], R[:, :, D:D + HEADS], h4[:], ALU.mult))
                            st.link(nc.vector.tensor_scalar(f4[:], f4[:], 1e-9, None, ALU.add))
                            st.link(nc.vector.reciprocal(g4[:], f4[:]))
                            st.link(nc.vector.tensor_tensor(g4[:], g4[:], h4[:], ALU.mult))
                            st.link(nc.vector.tensor_tensor(g4[:], g4[:], bc(nonempty[:, slots], 2, HEADS), ALU.mult))
                            dve.wait_ge(s_tr, g)
                            nc.vector.tensor_tensor(a[:].rearrange("p g (h e) -> p g h e", h=HEADS),
                                                    R[:, :, 0:D].rearrange("p g (h e) -> p g h e", h=HEADS),
                                                    bc(g4[:], 3, D // HEADS), ALU.mult).then_inc(s_a, 1)
                            st.n += 1
                            dve.wait_ge(s_a, g + 1)
                            dve.sem_inc(s_vf, 1)
                        elif layer == 2:
                            dve.wait_ge(s_tr, g * 2)
                            nc.vector.tensor_copy(xs[:], x_all[:, slots, :]).then_inc(s_a, 1)
                            nc.vector.tensor_tensor(a[:], R[:], bc(rcnt[:, slots], 2, HID), ALU.mult).then_inc(s_a, 1)
                            dve.wait_ge(s_a, g * 2 + 2)
                        else:
                            dve.wait_ge(s_tr, g)
                            nc.vector.tensor_tensor(a[:], R[:], bc(ndst[:, slots], 2, D), ALU.mult).then_inc(s_a, 1)
                            dve.wait_ge(s_a, g + 1)
                        dve.sem_inc(s_aggf, 1)
                        assert st.n == KF, st.n

                    def mid(g, i, b):
                        dve.wait_ge(s_el, g * 2 + 2)
                        nc.vector.scalar_tensor_tensor(be[:], be[:], 1.0, br[:], ALU.min, ALU.add).then_inc(s_elu, 1)

                    def back(g, i, b):
                        st = Steps(dve, s_vb, g * KB)
                        slots = ds(g * G, G)
                        if layer == 1:
                            dve.wait_ge(s_ag[b], i * (16 * G) + 16 * G)
                            st.link(nc.vector.tensor_tensor(sq[:], agg[b][:], own_all[:, slots, :], ALU.add))
                            dve.sem_inc(s_aggf, 1)
                            st.link(nc.vector.scalar_tensor_tensor(sq[:], sq[:], 0.0, bc(nonempty[:, slots], 2, D), ALU.max, ALU.mult))
                            st.link(nc.vector.tensor_tensor(y[:], sq[:], x_all[:, slots, :], ALU.add))
                        else:
                            dve.wait_ge(s_of, g + 1)
                            st.link(nc.vector.tensor_tensor(y[:], x_all[:, slots, 0:D], slots_of(p_o, D), ALU.add))
                        dve.sem_inc(s_y, 1)
                        st.link(nc.vector.tensor_reduce(s1[:], y[:], AX.X, ALU.add))
                        st.link(nc.vector.scalar_tensor_tensor(y[:], bc(s1[:], 2, D), -1.0 / D, y[:], ALU.mult, ALU.add))
                        st.link(nc.vector.tensor_tensor(sq[:], y[:], y[:], ALU.mult))
                        st.link(nc.vector.tensor_reduce(s2[:], sq[:], AX.X, ALU.add))
                        nc.vector.tensor_scalar(s2[:], s2[:], 1.0 / D, EPS, ALU.mult, ALU.add).then_inc(s_var, 1)
                        dve.wait_ge(s_rt, g + 1)
                        st.link(nc.vector.reciprocal(s2[:], rt[:]))
                        dve.wait_ge(s_st[b], i * 16)
                        if layer == 1:
                            dve.wait_ge(s_sc[b], i * (16 * G))
                        st.link(nc.vector.tensor_tensor(xn[b][:], y[:], bc(s2[:], 2, D), ALU.mult))
                        dve.sem_inc(s_xn, 1)
                        if layer == 2:
                            dve.wait_ge(s_tabs, g * 16)
                            st.link(nc.vector.tensor_tensor(feat_s[:], xn[b][:], bc(nsrc[:, slots], 2, D), ALU.mult))
                            dve.sem_inc(s_feat, 1)
                        while st.n < KB:
                            dve.sem_inc(s_vb, 1)
                            st.n += 1
                        assert st.n == KB, st.n
                    dve.wait_ge(s_rows, 16 + 16 * (layer == 1))
                    skewed(nc.vector.engine, front, back, mid if layer == 2 else None)

                @block.scalar
                def _(act):
                    def front(g, i, b):
                        if layer == 0:
                            act.wait_ge(s_dm, g + 1)
                            nc.scalar.activation(h4[:], g4[:], ACT.Exp).then_inc(s_ex, 1)
                        if layer in (0, 3):
                            act.wait_ge(s_tr, g + 1)
                            nc.scalar.activation(aT[:], p_ta[:].rearrange("p (k n) -> p k n", n=P), ACT.Copy).then_inc(s_evf, 1)
                        if layer == 2:
                            act.wait_ge(s_tr, g * 2 + 1)
                            nc.scalar.activation(aT[:], slots_of(p_ta, P), ACT.Copy).then_inc(s_evf, 1)
                            act.wait_ge(s_tr, g * 2 + 2)
                            nc.scalar.activation(xT[:], slots_of(p_ta, P)[0:D + 1], ACT.Copy).then_inc(s_evf, 1)

                    def mid(g, i, b):
                        act.wait_ge(s_z, g + 1)
                        act.wait_ge(s_of, g)
                        nc.scalar.activation(be[:], slots_of(p_z, P), ACT.Exp, bias=bg1[:, 0:1])
                        nc.scalar.activation(br[:], slots_of(p_z, P), ACT.Relu, bias=bg1[:, 0:1]).then_inc(s_el, 1)
                        act.wait_ge(s_el, g * 2 + 1)
                        nc.scalar.activation(br[:], br[:], ACT.Copy, bias=-1.0).then_inc(s_el, 1)

                    def back(g, i, b):
                        act.wait_ge(s_var, g + 1)
                        nc.scalar.activation(rt[:], s2[:], ACT.Sqrt).then_inc(s_rt, 1)
                        if layer == 0:
                            act.wait_ge(s_trx, g + 1)
                            nc.scalar.activation(xT[:], p_ta[:].rearrange("p (k n) -> p k n", n=P), ACT.Copy).then_inc(s_evx, 1)
                            act.wait_ge(s_tt, g + 1)
                            act.wait_ge(s_tabs, g * 32)
                            tab = slots_of(p_tab, 2 * D)
                            nc.scalar.activation(own_s[:], tab[:, :, 0:D], ACT.Copy)
                            nc.scalar.activation(nbr_s[:], tab[:, :, D:2 * D], ACT.Copy).then_inc(s_tab, 1)
                    if layer == 2:
                        act.wait_ge(s_w2, 4)
                    skewed(nc.scalar.engine, front, back, mid if layer == 2 else None)

                @block.tensor
                def _(pe):
                    pe.wait_ge(s_w, 16 * len(loads))
                    if layer == 0:
                        pe.wait_ge(s_w2, 1)
                    if layer == 2:
                        nc.tensor.transpose(p_z[0:D, 0, 0:HID], wp2[:], ident[:]).then_inc(s_w2, 1)
                        pe.wait_ge(s_w2, 2)
                        nc.tensor.matmul(p_z[:, 1, 0:HID], wp2T[:], wg1b[:], start=True, stop=True)
                        nc.tensor.matmul(p_z[0:D + 1, 2, 0:HID], bp2[:], wg1b[:], start=True, stop=True).then_inc(s_w2, 1)
                        pe.wait_ge(s_w2, 4)

                    def pairs(rows):
                        for k in range(G // 2):
                            r = nc.tensor.transpose(p_ta[:, k * P:(k + 1) * P], rows[:, 2 * k:2 * k + 2, :].rearrange("p h f -> p (h f)"), ident[:])
                        return r

                    def front(g, i, b):
                        if layer in (0, 3):
                            pe.wait_ge(s_a, g + 1)
                            if layer == 3:
                                pe.wait_ge(s_evf, g)
                            pairs(a).then_inc(s_tr, 1)
                            pe.wait_ge(s_evf, g + 1)
                            pe.wait_ge(s_y, g)
                            w = w_out[:].rearrange("p h f -> p (h f)")
                            for k in range(G // 2):
                                r = nc.tensor.matmul(p_o[:, k // 4, (k % 4) * P:(k % 4 + 1) * P], aT[:, k, :], w, start=True, stop=True)
                            r.then_inc(s_of, 1)
                        if layer == 2:
                            pe.wait_ge(s_a, g * 2 + 2)
                            for s in range(G):
                                r = nc.tensor.transpose(p_ta[:, s // 4, (s % 4) * P:(s % 4 + 1) * P], a[:, s, :], ident[:])
                            r.then_inc(s_tr, 1)
                            pe.wait_ge(s_evf, g * 2 + 1)
                            for s in range(G):
                                r = nc.tensor.transpose(p_ta[0:D + 1, s // 4, (s % 4) * P:(s % 4 + 1) * P], xs[:, s, :], ident[:])
                            r.then_inc(s_tr, 1)
                            pe.wait_ge(s_evf, g * 2 + 2)
                            pe.wait_ge(s_el, g * 2)
                            for k in range(-(-G // 4)):
                                w = min(4, G - 4 * k)
                                nc.tensor.matmul(p_z[:, k, 0:w * P], wga[:], aT[:, 4 * k:4 * k + w, :].rearrange("p k n -> p (k n)"), start=True, stop=False)
                                r = nc.tensor.matmul(p_z[:, k, 0:w * P], wgx[:], xT[:, 4 * k:4 * k + w, :].rearrange("p k n -> p (k n)"), start=False, stop=True)
                            r.then_inc(s_z, 1)

                    def mid(g, i, b):
                        pe.wait_ge(s_elu, g + 1)
                        pe.wait_ge(s_y, g)
                        row = bg2[:].rearrange("o s f -> o (s f)")
                        for k in range(2):
                            n = min(8, G - 8 * k)
                            nc.tensor.matmul(p_o[:, k, 0:n * D], ones[:], row[:, 0:n * D], start=True, stop=False)
                        for s in range(G):
                            r = nc.tensor.matmul(p_o[:, s // 8, (s % 8) * D:(s % 8 + 1) * D], be[:, s, :], wg2[:], start=False,
                                                 stop=s % 8 == 7 or s == G - 1)
                        r.then_inc(s_of, 1)

                    def back(g, i, b):
                        if layer != 0:
                            return
                        pe.wait_ge(s_xn, g + 1)
                        pairs(xn[b]).then_inc(s_trx, 1)
                        pe.wait_ge(s_evx, g + 1)
                        pe.wait_ge(s_tab, g)
                        row = bias[:].rearrange("o s h f -> o (s h f)")
                        w = w_next[:].rearrange("p h f -> p (h f)")
                        for k in range(3):
                            n = min(4, G - 4 * k)
                            nc.tensor.matmul(p_tab[:, k, 0:n * 2 * D], ones[:], row[:, 0:n * 2 * D], start=True, stop=False)
                        for k in range(G // 2):
                            r = nc.tensor.matmul(p_tab[:, k // 2, (k % 2) * 4 * D:(k % 2 + 1) * 4 * D], xT[:, k, :], w, start=False,
                                                 stop=k % 2 == 1 or k == G // 2 - 1)
                        r.then_inc(s_tt, 1)
                    skewed(nc.tensor.engine, front, back, mid if layer == 2 else None)

        last0 = sb_last0 = ctx.enter_context(nc.sbuf_tensor("last_state", [P, HID], f32))
        with phase("attention_edges") as (scope, block):
            sb, ps = maker(scope)
            idx = [sb(f"at_idx{b}", [P, T], i32) for b in range(2)]
            kv = [sb(f"at_kv{b}", [P, T, 2 * D]) for b in range(2)]
            q = [sb(f"at_q{b}", [P, T, D]) for b in range(2)]
            o = [sb(f"at_o{b}", [P, T, ROW0]) for b in range(2)]
            sc = sb("at_sc", [P, T, HEADS])
            mx = sb("at_mx", [P, T + 1, HEADS])
            dif = sb("at_dif", [P, 2, T, HEADS])
            ex = sb("at_ex", [P, 2, T, HEADS])
            s_idx = [sem(f"at_idx{b}") for b in range(2)]
            s_rows = [sem(f"at_rows{b}") for b in range(2)]
            s_free = [sem(f"at_free{b}") for b in range(2)]
            s_q = [sem(f"at_q{b}") for b in range(2)]
            s_out = [sem(f"at_out{b}") for b in range(2)]
            s_v, s_qf, s_dif, s_ex, s_o, s_turn, s_m = (sem("at_" + n) for n in ("v", "qf", "dif", "ex", "o", "turn", "m"))

            @block.sync
            def _(sp):
                def load(c, b, width=T):
                    sp.dma_start(idx[b][:, 0:width], src_v[:, ds(c * T, width)]).then_inc(s_idx[b], 16)
                    sp.dma_start(q[b][:, 0:width, :], edges(start_d)[:, ds(c * T, width), :]).then_inc(s_q[b], 16)

                def store(c, b, width=T):
                    sp.wait_ge(s_o, c * 2 + 2)
                    sp.dma_start(edges(scan_d[0])[:, ds(c * T, width), :], o[b][:, 0:width, :]).then_inc(s_out[b], 16)
                load(0, 0)
                load(1, 1)
                with nc.Fori(0, PAIRS - 1, engines=[nc.sync.engine]) as i:
                    for b in range(2):
                        sp.wait_ge(s_qf, i * 2 + b + 1)
                        load(i * 2 + b + 2, b)
                        store(i * 2 + b, b)
                sp.wait_ge(s_qf, 2 * PAIRS - 1)
                load(2 * PAIRS, 0, TAIL)
                store(2 * PAIRS - 2, 0)
                store(2 * PAIRS - 1, 1)
                store(2 * PAIRS, 0, TAIL)
                sp.wait_ge(s_out[0], 16 * (PAIRS + 1))
                sp.wait_ge(s_out[1], 16 * PAIRS)

            @block.gpsimd
            def _(pool):
                pool_gathers(pool, kv_d, idx, kv, s_idx, s_free, s_rows, s_turn)

            @block.vector
            def _(dve):
                st = Steps(dve, s_v)
                dve.sem_inc(s_free[0], 1)
                dve.sem_inc(s_free[1], 1)
                st.step(nc.vector.memset(mx[:, 0, :], -BIG))
                st.step(nc.vector.memset(o[1][:, T - 1, :], 0.0))
                setup = st.n
                st.wait()
                K = 11

                def chunk(c, i, b, width=T):
                    st = Steps(dve, s_v, c * K + setup)
                    kp = keep[:, ds(c * T, width)]
                    W = slice(0, width)
                    prev = o[1 - b][:, T - 1, :]
                    dve.wait_ge(s_q[b], i * 16 + 16)
                    for f in range(D):
                        r = nc.vector.tensor_tensor_scan(q[b][:, W, f], kp, q[b][:, W, f], qcarry[:, f:f + 1], ALU.mult, ALU.add)
                    st.link(r)
                    st.link(nc.vector.tensor_copy(qcarry[:], q[b][:, width - 1, :]))
                    dve.wait_ge(s_rows[b], i * (16 * T) + 16 * width)
                    st.link(nc.vector.tensor_tensor(q[b][:, W, :], q[b][:, W, :], kv[b][:, W, 0:D], ALU.mult))
                    st.link(nc.vector.tensor_reduce(sc[:, W, :], q[b][:, W, :].rearrange("p t (h e) -> p t h e", h=HEADS), AX.X, ALU.add))
                    nc.vector.sem_inc(s_qf, 1)
                    for h in range(HEADS):
                        r = nc.vector.tensor_tensor_scan(mx[:, 1:width + 1, h], pen[:, ds(c * T, width)], sc[:, W, h], mx[:, 0, h:h + 1], ALU.add, ALU.max)
                    st.link(r)
                    st.step(nc.vector.tensor_tensor(dif[:, 0, W, :], mx[:, 0:width, :], mx[:, 1:width + 1, :], ALU.subtract))
                    st.step(nc.vector.tensor_tensor(dif[:, 1, W, :], sc[:, W, :], mx[:, 1:width + 1, :], ALU.subtract))
                    st.wait()
                    nc.vector.tensor_scalar(dif[:, 0, W, :], dif[:, 0, W, :], 0.0, None, ALU.min).then_inc(s_dif, 1)
                    dve.wait_ge(s_ex, c * 2 + 1)
                    st.link(nc.vector.scalar_tensor_tensor(ex[:, 0, W, :], dif[:, 0, W, :], 0.0, ex[:, 0, W, :], ALU.is_ge, ALU.max))
                    st.step(nc.vector.tensor_tensor(ex[:, 0, W, :], ex[:, 0, W, :], bc(kp, 2, HEADS), ALU.mult))
                    v4 = kv[b][:, W, D:2 * D].rearrange("p t (h e) -> p t h e", h=HEADS)
                    st.step(nc.vector.tensor_tensor(v4, v4, bc(ex[:, 1, W, :], 3, D // HEADS), ALU.mult))
                    st.wait()
                    dve.wait_ge(s_out[b], i * 16)
                    for f in range(D):
                        h = f // (D // HEADS)
                        nc.vector.tensor_tensor_scan(o[b][:, W, f], ex[:, 0, W, h], kv[b][:, W, D + f], prev[:, f:f + 1], ALU.mult, ALU.add)
                    for h in range(HEADS):
                        r = nc.vector.tensor_tensor_scan(o[b][:, W, D + h], ex[:, 0, W, h], ex[:, 1, W, h], prev[:, D + h:D + h + 1], ALU.mult, ALU.add)
                    st.link(r)
                    nc.vector.sem_inc(s_o, 1)
                    nc.vector.sem_inc(s_free[b], 1)
                    dve.wait_ge(s_ex, c * 2 + 2)
                    st.n += 0
                    nc.vector.tensor_copy(mx[:, 0, :], mx[:, width, :]).then_inc(s_m, 1)
                    dve.wait_ge(s_m, c + 1)
                    assert st.n == K, st.n
                with nc.Fori(0, PAIRS, engines=[nc.vector.engine]) as i:
                    for b in range(2):
                        chunk(i * 2 + b, i, b)
                chunk(2 * PAIRS, PAIRS, 0, TAIL)
                st = Steps(dve, s_v, (2 * PAIRS + 1) * K + setup)
                st.step(nc.vector.tensor_copy(last0[:, 0:D + HEADS], o[0][:, TAIL - 1, 0:D + HEADS]))
                st.step(nc.vector.tensor_copy(last0[:, D + HEADS:ROW0], mx[:, 0, :]))

            @block.scalar
            def _(act):
                def chunk(c, i, b, width=T):
                    act.wait_ge(s_dif, c + 1)
                    nc.scalar.activation(ex[:, :, 0:width, :], dif[:, :, 0:width, :], ACT.Exp).then_inc(s_ex, 1)
                    act.wait_ge(s_out[b], i * 16)
                    nc.scalar.activation(o[b][:, 0:width, D + HEADS:ROW0], mx[:, 1:width + 1, :], ACT.Copy).then_inc(s_ex, 1)
                    act.wait_ge(s_ex, c * 2 + 2)
                    nc.scalar.sem_inc(s_o, 1)
                with nc.Fori(0, PAIRS, engines=[nc.scalar.engine]) as i:
                    for b in range(2):
                        chunk(i * 2 + b, i, b)
                chunk(2 * PAIRS, PAIRS, 0, TAIL)

        with phase("attention_boundary") as (scope, block):
            sb, ps = maker(scope)
            S = D + HEADS
            gm = sb("ab_gm", [P, HEADS])
            gmT = sb("ab_gmT", [HEADS, P])
            mT = sb("ab_mT", [HEADS, P + 1])
            mr = sb("ab_mr", [P, 2, HEADS])
            df = sb("ab_df", [P, 2, HEADS])
            ef = sb("ab_ef", [P, 2, HEADS])
            d0, d1 = sb("ab_d0", [P, S]), sb("ab_d1", [P, S])
            d0T, runT = sb("ab_d0T", [S, P]), sb("ab_runT", [S, P + 1])
            carry, rows, res = sb("ab_carry", [P, S]), sb("ab_rows", [P, ROW0]), sb("ab_res", [P, ROW0])
            pp = [ps(f"ab_p{n}", [P, 512]) for n in range(7)]
            s_v, s_t, s_e, s_g, s_s, s_m = (sem("ab_" + n) for n in ("v", "t", "e", "g", "s", "m"))
            waits = {}

            @block.vector
            def _(dve):
                st = Steps(dve, s_v)
                nc.vector.memset(rows[:], 0.0).then_inc(s_m, 1)
                st.step(nc.vector.memset(mT[:, 0:1], -BIG))
                st.step(nc.vector.memset(runT[:, 0:1], 0.0))
                st.link(nc.vector.tensor_scalar(gm[:], bc(whole[:, 0], 1, HEADS), -1.0, BIG, ALU.add, ALU.mult))
                waits["gates"] = st.n
                dve.wait_ge(s_t, 2)
                st.link(nc.vector.tensor_copy(gmT[:], pp[0][0:HEADS, 0:P]))
                st.link(nc.vector.tensor_tensor_scan(mT[:, 1:P + 1], gmT[:], pp[1][0:HEADS, 0:P], -BIG, ALU.add, ALU.max))
                waits["maxima"] = st.n
                dve.wait_ge(s_t, 4)
                st.step(nc.vector.tensor_copy(mr[:, 0, :], pp[2][:, 0:HEADS]))
                st.link(nc.vector.tensor_copy(mr[:, 1, :], pp[3][:, 0:HEADS]))
                st.step(nc.vector.tensor_tensor(df[:, 0, :], mr[:, 0, :], mr[:, 1, :], ALU.subtract))
                st.link(nc.vector.tensor_tensor(df[:, 1, :], last0[:, S:ROW0], mr[:, 1, :], ALU.subtract))
                st.link(nc.vector.tensor_scalar(df[:], df[:], 0.0, None, ALU.min))
                waits["factors"] = st.n
                dve.wait_ge(s_e, 1)
                st.link(nc.vector.tensor_scalar(ef[:, 0, :], ef[:, 0, :], whole[:, 0:1], None, ALU.mult))
                for dd, k in ((d0, 0), (d1, 1)):
                    st.step(nc.vector.tensor_copy(dd[:, 0:D].rearrange("p (h e) -> p h e", h=HEADS), bc(ef[:, k, :], 2, D // HEADS)))
                    st.step(nc.vector.tensor_copy(dd[:, D:S], ef[:, k, :]))
                st.wait()
                st.link(nc.vector.tensor_tensor(d1[:], d1[:], last0[:, 0:S], ALU.mult))
                waits["states"] = st.n
                dve.wait_ge(s_t, 6)
                st.link(nc.vector.tensor_copy(d0T[:], pp[4][0:S, 0:P]))
                st.link(nc.vector.tensor_tensor_scan(runT[:, 1:P + 1], d0T[:], pp[5][0:S, 0:P], 0.0, ALU.mult, ALU.add))
                waits["sums"] = st.n
                dve.wait_ge(s_t, 7)
                st.link(nc.vector.tensor_copy(carry[:], pp[6][:, 0:S]))
                dve.wait_ge(s_g, 16)
                st.link(nc.vector.tensor_tensor(res[:, S:ROW0], rows[:, S:ROW0], mr[:, 0, :], ALU.max))
                st.step(nc.vector.tensor_tensor(df[:, 0, :], mr[:, 0, :], res[:, S:ROW0], ALU.subtract))
                st.link(nc.vector.tensor_tensor(df[:, 1, :], rows[:, S:ROW0], res[:, S:ROW0], ALU.subtract))
                waits["merge"] = st.n
                dve.wait_ge(s_e, 2)
                for dd, k in ((d0, 0), (d1, 1)):
                    st.step(nc.vector.tensor_copy(dd[:, 0:D].rearrange("p (h e) -> p h e", h=HEADS), bc(ef[:, k, :], 2, D // HEADS)))
                    st.step(nc.vector.tensor_copy(dd[:, D:S], ef[:, k, :]))
                st.wait()
                st.step(nc.vector.tensor_tensor(d0[:], d0[:], carry[:], ALU.mult))
                st.link(nc.vector.tensor_tensor(d1[:], d1[:], rows[:, 0:S], ALU.mult))
                st.link(nc.vector.tensor_tensor(res[:, 0:S], d0[:], d1[:], ALU.add))
                nc.vector.sem_inc(s_m, 1)

            @block.tensor
            def _(pe):
                pe.wait_ge(s_v, waits["gates"])
                nc.tensor.transpose(pp[0][0:HEADS, 0:P], gm[:], ident[:]).then_inc(s_t, 1)
                nc.tensor.transpose(pp[1][0:HEADS, 0:P], last0[:, S:ROW0], ident[:]).then_inc(s_t, 1)
                pe.wait_ge(s_v, waits["maxima"])
                nc.tensor.transpose(pp[2][:, 0:HEADS], mT[:, 0:P], ident[0:HEADS, 0:HEADS]).then_inc(s_t, 1)
                nc.tensor.transpose(pp[3][:, 0:HEADS], mT[:, 1:P + 1], ident[0:HEADS, 0:HEADS]).then_inc(s_t, 1)
                pe.wait_ge(s_v, waits["states"])
                nc.tensor.transpose(pp[4][0:S, 0:P], d0[:], ident[:]).then_inc(s_t, 1)
                nc.tensor.transpose(pp[5][0:S, 0:P], d1[:], ident[:]).then_inc(s_t, 1)
                pe.wait_ge(s_v, waits["sums"])
                nc.tensor.transpose(pp[6][:, 0:S], runT[:, 0:P], ident[0:S, 0:S]).then_inc(s_t, 1)

            @block.scalar
            def _(act):
                act.wait_ge(s_v, waits["factors"])
                nc.scalar.activation(ef[:], df[:], ACT.Exp).then_inc(s_e, 1)
                act.wait_ge(s_v, waits["merge"])
                nc.scalar.activation(ef[:], df[:], ACT.Exp).then_inc(s_e, 1)

            @block.gpsimd
            def _(pool):
                pool.wait_ge(s_m, 1)
                nc.gpsimd.indirect_dma_start(rows[:], None, scan_d[0], bass.IndirectOffsetOnAxis(ap=fixidx[:, 0:1], axis=0),
                                             bounds_check=E - 1, oob_is_err=False).then_inc(s_g, 16)
                pool.wait_ge(s_m, 2)
                nc.gpsimd.indirect_dma_start(scan_d[0], bass.IndirectOffsetOnAxis(ap=fixidx[:, 0:1], axis=0), res[:], None,
                                             bounds_check=E - 1, oob_is_err=False).then_inc(s_s, 16)
                pool.wait_ge(s_s, 16)

        node_block("attention_nodes", 0, scan_d[0], ROW0, None)

        def plain_edges(name, table, scan_out, gate, op, none, degrees):
            first = ALU.mult if op == ALU.add else ALU.add
            with phase(name) as (scope, block):
                sb, ps = maker(scope)
                idx = [sb(f"{name}_idx{b}", [P, T], i32) for b in range(2)]
                rows = [sb(f"{name}_rows{b}", [P, T, D]) for b in range(2)]
                o = [sb(f"{name}_o{b}", [P, T, D]) for b in range(2)]
                s_idx = [sem(f"{name}_idx{b}") for b in range(2)]
                s_rows = [sem(f"{name}_rows{b}") for b in range(2)]
                s_free = [sem(f"{name}_free{b}") for b in range(2)]
                s_out = [sem(f"{name}_out{b}") for b in range(2)]
                s_v, s_o, s_open, s_turn = (sem(f"{name}_{n}") for n in ("v", "o", "open", "turn"))
                if degrees:
                    hi = sb("dg_hi", [P, T])
                    lo = sb("dg_lo", [P, T])
                    ohi, olo = sb("dg_ohi", [P, T, P], bf16), sb("dg_olo", [P, T, J], bf16)
                    zrow = sb("dg_zrow", [P, P], bf16)
                    p_h = ps("dg_ph", [P, 512])
                    s_oh, s_hm = sem("dg_oh"), sem("dg_hm")

                @block.sync
                def _(sp):
                    def load(c, b, width=T):
                        sp.dma_start(idx[b][:, 0:width], src_v[:, ds(c * T, width)]).then_inc(s_idx[b], 16)

                    def store(c, b, width=T):
                        sp.wait_ge(s_o, c + 1)
                        sp.dma_start(edges(scan_out)[:, ds(c * T, width), :], o[b][:, 0:width, :]).then_inc(s_out[b], 16)
                    load(0, 0)
                    load(1, 1)
                    with nc.Fori(0, PAIRS - 1, engines=[nc.sync.engine]) as i:
                        for b in range(2):
                            store(i * 2 + b, b)
                            load(i * 2 + b + 2, b)
                    store(2 * PAIRS - 2, 0)
                    load(2 * PAIRS, 0, TAIL)
                    store(2 * PAIRS - 1, 1)
                    store(2 * PAIRS, 0, TAIL)
                    sp.wait_ge(s_out[0], 16 * (PAIRS + 1))
                    sp.wait_ge(s_out[1], 16 * PAIRS)

                @block.gpsimd
                def _(pool):
                    pool_gathers(pool, table, idx, rows, s_idx, s_free, s_rows, s_turn)

                @block.vector
                def _(dve):
                    st = Steps(dve, s_v)
                    st.step(nc.vector.memset(o[1][:, T - 1, :], none))
                    if degrees:
                        st.step(nc.vector.memset(zrow[:], 0.0))
                    st.wait()
                    setup = st.n
                    dve.sem_inc(s_open, 1)
                    dve.sem_inc(s_free[0], 1)
                    dve.sem_inc(s_free[1], 1)
                    K = 6 if degrees else 1

                    def chunk(c, i, b, width=T):
                        st = Steps(dve, s_v, c * K + setup)
                        W = slice(0, width)
                        if degrees:
                            dve.wait_ge(s_idx[b], i * 16 + 16)
                            st.link(nc.vector.tensor_scalar(hi[:, W], idx[b][:, W], -(J - 1) / 2, 1.0 / J, ALU.add, ALU.mult))
                            st.link(nc.vector.tensor_scalar(hi[:, W], hi[:, W], MAGIC, -MAGIC, ALU.add, ALU.add))
                            st.link(nc.vector.scalar_tensor_tensor(lo[:, W], hi[:, W], -float(J), idx[b][:, W], ALU.mult, ALU.add))
                            dve.wait_ge(s_hm, c + 1)
                            st.step(nc.vector.tensor_tensor(ohi[:, W, :], bc(hi[:, W], 2, P), bc(iota_row[:], 1, width), ALU.is_equal))
                            st.link(nc.vector.tensor_tensor(olo[:, W, :], bc(lo[:, W], 2, J), bc(iota_row[:, 0:J], 1, width), ALU.is_equal))
                            nc.vector.sem_inc(s_oh, 1)
                        dve.wait_ge(s_rows[b], i * (16 * T) + 16 * width)
                        dve.wait_ge(s_out[b], i * 16)
                        for f in range(D):
                            r = nc.vector.tensor_tensor_scan(o[b][:, W, f], gate[:, ds(c * T, width)], rows[b][:, W, f],
                                                             o[1 - b][:, T - 1, f:f + 1], first, op)
                        st.link(r)
                        nc.vector.sem_inc(s_o, 1)
                        nc.vector.sem_inc(s_free[b], 1)
                        assert st.n == K
                    with nc.Fori(0, PAIRS, engines=[nc.vector.engine]) as i:
                        for b in range(2):
                            chunk(i * 2 + b, i, b)
                    chunk(2 * PAIRS, PAIRS, 0, TAIL)
                    base = (2 * PAIRS + 1) * K + setup
                    st = Steps(dve, s_v, base)
                    st.step(nc.vector.tensor_copy(last0[:, 0:D], o[0][:, TAIL - 1, :]))
                    if degrees:
                        dve.wait_ge(s_hm, 2 * PAIRS + 2)
                        st.link(nc.vector.tensor_scalar(nsrc[:], p_h[:, 0:J], 1.0, None, ALU.max))
                        dve.wait_ge(s_hm, 2 * PAIRS + 3)
                        st.link(nc.vector.reciprocal(nsrc[:], nsrc[:]))

                if degrees:
                    @block.tensor
                    def _(pe):
                        pe.wait_ge(s_open, 1)
                        nc.tensor.matmul(p_h[:, 0:J], zrow[:], zrow[:, 0:J], start=True, stop=False).then_inc(s_hm, 1)

                        def count(c, width=T, last=False):
                            pe.wait_ge(s_oh, c + 1)
                            for t in range(width):
                                mm = nc.tensor.matmul(p_h[:, 0:J], ohi[:, t, :], olo[:, t, :], start=False, stop=last and t == width - 1)
                            mm.then_inc(s_hm, 1)
                        with nc.Fori(0, 2 * PAIRS, engines=[nc.tensor.engine]) as c:
                            count(c)
                        count(2 * PAIRS, TAIL, True)

                    @block.scalar
                    def _(act):
                        act.wait_ge(s_v, (2 * PAIRS + 1) * 6 + 2 + 2)
                        nc.scalar.activation(nsrc[:], nsrc[:], ACT.Sqrt).then_inc(s_hm, 1)

        plain_edges("max_edges", nbr1_d, scan_d[1], pen, ALU.max, -BIG, True)
        boundary("max_boundary", last0[:, 0:D], scan_d[1], D, ALU.max, -BIG)
        node_block("max_nodes", 1, scan_d[1], D, x_d[0], own1_d)

        with phase("mlp_edges") as (scope, block):
            sb, ps = maker(scope)
            BLK = 8
            NB = -(-T // BLK)
            EK = BLK * EA
            EK1 = 64 + 1
            idx = [sb(f"ml_idx{b}", [P, T], i32) for b in range(2)]
            own = [sb(f"ml_own{b}", [P, T, D]) for b in range(2)]
            xx = [sb(f"ml_xx{b}", [P, T, 2 * D]) for b in range(2)]
            ea = [sb(f"ml_ea{b}", [P, T * EA]) for b in range(2)]
            eaT = sb("ml_eaT", [EK1, NB, P])
            wxx = sb("ml_wxx", [2 * D, HID])
            wea = sb("ml_wea", [EK1, BLK, HID])
            xT = [sb(f"ml_xT{k}", [P, BLK, P]) for k in range(2)]
            hs = [sb(f"ml_h{b}", [P, T, HID]) for b in range(2)]
            rr = sb("ml_r", [P, T, HID])
            xcarry = sb("ml_xc", [P, D])
            hcarry = sb("ml_hc", [P, HID])
            p_h = [ps(f"ml_ph{k}", [P, 2, 512]) for k in range(2)]
            p_x = ps("ml_px", [P, 2, 512])
            p_e = ps("ml_pe", [P, 2, 512])
            s_idx = [sem(f"ml_idx{b}") for b in range(2)]
            s_rows = [sem(f"ml_rows{b}") for b in range(2)]
            s_free = [sem(f"ml_free{b}") for b in range(2)]
            s_own = [sem(f"ml_own{b}") for b in range(2)]
            s_ea = [sem(f"ml_ea{b}") for b in range(2)]
            s_out = [sem(f"ml_out{b}") for b in range(2)]
            s_v, s_w, s_w2, s_c, s_sp, s_et, s_ev, s_xt, s_xe, s_ph, s_pf, s_er, s_ef, s_o, s_done, s_turn, s_first = (
                sem("ml_" + n) for n in ("v", "w", "w2", "c", "sp", "et", "ev", "xt", "xe", "ph", "pf", "er", "ef", "o", "done", "turn", "first"))

            def blocks(width):
                return [(k, min(BLK, width - k)) for k in range(0, width, BLK)]

            @block.sync
            def _(sp):
                sp.wait_ge(s_w2, 1)
                for t in range(BLK):
                    sp.dma_start(wea[t * EA:(t + 1) * EA, t, :], pw1_in[2 * D:2 * D + EA, :]).then_inc(s_w, 16)
                    sp.dma_start(wea[64:65, t, :], bc(pb1_in, 0, 1)).then_inc(s_w, 16)
                sp.dma_start(wxx[:], pw1_in[0:2 * D, :]).then_inc(s_w, 16)

                def load(c, b, width=T):
                    sp.dma_start(idx[b][:, 0:width], src_v[:, ds(c * T, width)]).then_inc(s_idx[b], 16)
                    sp.dma_start(own[b][:, 0:width, :], edges(start_d)[:, ds(c * T, width), :]).then_inc(s_own[b], 16)
                    sp.dma_start(ea[b][:, 0:width * EA], ea_v[:, ds(c * T, width), :].rearrange("p t a -> p (t a)")).then_inc(s_ea[b], 16)

                def store(c, b, width=T):
                    sp.wait_ge(s_o, c + 1)
                    sp.dma_start(edges(scan_d[2])[:, ds(c * T, width), :], hs[b][:, 0:width, :]).then_inc(s_out[b], 16)
                load(0, 0)
                load(1, 1)
                with nc.Fori(0, PAIRS - 1, engines=[nc.sync.engine]) as i:
                    for b in range(2):
                        sp.wait_ge(s_done, i * 2 + b + 1)
                        load(i * 2 + b + 2, b)
                        store(i * 2 + b, b)
                sp.wait_ge(s_done, 2 * PAIRS - 1)
                load(2 * PAIRS, 0, TAIL)
                store(2 * PAIRS - 2, 0)
                store(2 * PAIRS - 1, 1)
                store(2 * PAIRS, 0, TAIL)
                sp.wait_ge(s_out[0], 16 * (PAIRS + 1))
                sp.wait_ge(s_out[1], 16 * PAIRS)

            @block.gpsimd
            def _(pool):
                nc.gpsimd.indirect_dma_start(xcarry[:], None, x_d[1], bass.IndirectOffsetOnAxis(ap=dfirst[:, 0:1], axis=0)).then_inc(s_c, 16)
                pool_gathers(pool, x_d[1], idx, xx, s_idx, s_free, s_rows, s_turn, D)

            @block.tensor
            def _(pe):
                pe.wait_ge(s_w, 16 * (2 * BLK + 1))

                def chunk(c, i, b, blk0, width=T):
                    bl = blocks(width)

                    def transposes(n):
                        k, w = bl[n]
                        pe.wait_ge(s_xe, blk0 + n)
                        for t in range(w):
                            r = nc.tensor.transpose(p_x[:, t // 4, (t % 4) * P:(t % 4 + 1) * P], xx[b][:, k + t, :], ident[:])
                        r.then_inc(s_xt, 1)
                    pe.wait_ge(s_ea[b], i * 16 + 16)
                    pe.wait_ge(s_ph, blk0)
                    pe.sem_inc(s_turn, 1)
                    for n, (k, w) in enumerate(bl):
                        r = nc.tensor.transpose(p_e[0:w * EA, n // 4, (n % 4) * P:(n % 4 + 1) * P], ea[b][:, k * EA:(k + w) * EA], ident[:])
                    r.then_inc(s_et, 1)
                    pe.wait_ge(s_sp, c + 1)
                    pe.wait_ge(s_rows[b], i * (16 * T) + 16 * width)
                    transposes(0)
                    pe.wait_ge(s_ev, c + 1)
                    for n, (k, w) in enumerate(bl):
                        if n + 1 < len(bl):
                            transposes(n + 1)
                        else:
                            pe.wait_ge(s_xt, blk0 + len(bl))
                            pe.sem_inc(s_done, 1)
                            pe.sem_inc(s_free[b], 1)
                        par = (b * NB + n) % 2
                        ph = p_h[par]
                        pe.wait_ge(s_xe, blk0 + n + 1)
                        pe.wait_ge(s_pf, blk0 + n + 1)
                        for m in range(0, w, 4):
                            ww = min(4, w - m)
                            nc.tensor.matmul(ph[:, m // 4, 0:ww * HID], eaT[:, n, :], wea[:, m:m + ww, :].rearrange("p t f -> p (t f)"), start=True, stop=False)
                            for t in range(m, m + ww):
                                r = nc.tensor.matmul(ph[:, m // 4, (t - m) * HID:(t - m + 1) * HID], xT[par][:, t, :], wxx[:], start=False,
                                                     stop=t == m + ww - 1)
                        r.then_inc(s_ph, 1)
                with nc.Fori(0, PAIRS, engines=[nc.tensor.engine]) as i:
                    for b in range(2):
                        chunk(i * 2 + b, i, b, i * (2 * NB) + b * NB)
                chunk(2 * PAIRS, PAIRS, 0, 2 * PAIRS * NB, TAIL)

            @block.scalar
            def _(act):
                act.sem_inc(s_pf, 2)
                act.sem_inc(s_free[0], 1)
                act.sem_inc(s_free[1], 1)
                act.wait_ge(s_w2, 1)

                def chunk(c, i, b, blk0, width=T):
                    bl = blocks(width)

                    def move_x(n):
                        k, w = bl[n]
                        act.wait_ge(s_xt, blk0 + n + 1)
                        nc.scalar.activation(xT[(b * NB + n) % 2][:, 0:w, :], p_x[:].rearrange("p k n -> p (k n)")[:, 0:w * P].rearrange("p (t n) -> p t n", n=P), ACT.Copy).then_inc(s_xe, 1)
                    act.wait_ge(s_et, c + 1)
                    full = sum(w == BLK for k, w in bl)
                    flat = p_e[:].rearrange("p k n -> p (k n)")
                    r = nc.scalar.activation(eaT[0:EK, 0:full, :], flat[0:EK, 0:full * P].rearrange("p (k n) -> p k n", n=P), ACT.Copy)
                    if full < len(bl):
                        w = bl[-1][1]
                        r = nc.scalar.activation(eaT[0:w * EA, full, :], flat[0:w * EA, full * P:(full + 1) * P], ACT.Copy)
                    r.then_inc(s_ev, 1)
                    move_x(0)
                    act.wait_ge(s_out[b], i * 16)
                    for n, (k, w) in enumerate(bl):
                        par = (b * NB + n) % 2
                        if n + 1 < len(bl):
                            move_x(n + 1)
                        z = p_h[par][:].rearrange("p k n -> p (k n)")[:, 0:w * HID].rearrange("p (t f) -> p t f", f=HID)
                        act.wait_ge(s_ph, blk0 + n + 1)
                        act.wait_ge(s_ef, blk0 + n + 1)
                        nc.scalar.activation(hs[b][:, k:k + w, :], z, ACT.Exp)
                        nc.scalar.activation(rr[:, k:k + w, :], z, ACT.Relu).then_inc(s_pf, 1)
                        act.wait_ge(s_pf, blk0 + n + 3)
                        nc.scalar.activation(rr[:, k:k + w, :], rr[:, k:k + w, :], ACT.Copy, bias=-1.0).then_inc(s_er, 1)
                with nc.Fori(0, PAIRS, engines=[nc.scalar.engine]) as i:
                    for b in range(2):
                        chunk(i * 2 + b, i, b, i * (2 * NB) + b * NB)
                chunk(2 * PAIRS, PAIRS, 0, 2 * PAIRS * NB, TAIL)

            @block.vector
            def _(dve):
                st = Steps(dve, s_v)
                st.step(nc.vector.memset(wea[:], 0.0))
                st.step(nc.vector.memset(eaT[0:64], 0.0))
                st.link(nc.vector.memset(eaT[64:65, :, :], 1.0))
                dve.sem_inc(s_w2, 1)
                st.step(nc.vector.memset(hcarry[:], 0.0))
                dve.sem_inc(s_ef, NB)

                def spread(c, b, lo_f, hi_f, init):
                    for f in range(lo_f, hi_f):
                        r = nc.vector.tensor_tensor_scan(xx[b][:, :, f], keep[:, ds(c * T, T)], own[b][:, :, f], init[:, f:f + 1], ALU.mult, ALU.add)
                    return r

                K = 3
                FB = -(-D // NB)
                dve.wait_ge(s_c, 16)
                dve.wait_ge(s_own[0], 16)
                st.link(spread(0, 0, 0, D, xcarry))
                dve.sem_inc(s_sp, 1)
                setup = st.n

                def chunk(c, i, b, blk0, in_next, width=T):
                    st = Steps(dve, s_v, c * K + setup)
                    bl = blocks(width)
                    if in_next is not None:
                        dve.wait_ge(s_own[1 - b], in_next)
                    for n, (k, w) in enumerate(bl):
                        if in_next is not None and n * FB < D:
                            r = spread(c + 1, 1 - b, n * FB, min(D, (n + 1) * FB), xx[b][:, T - 1, :])
                            if (n + 1) * FB >= D:
                                st.link(r)
                                dve.sem_inc(s_sp, 1)
                        dve.wait_ge(s_er, blk0 + n + 1)
                        nc.vector.scalar_tensor_tensor(hs[b][:, k:k + w, :], hs[b][:, k:k + w, :], 1.0, rr[:, k:k + w, :], ALU.min, ALU.add).then_inc(s_ef, 1)
                    if in_next is None:
                        dve.sem_inc(s_v, 1)
                        st.n += 1
                    dve.wait_ge(s_ef, blk0 + len(bl) + NB)
                    for f in range(HID):
                        r = nc.vector.tensor_tensor_scan(hs[b][:, 0:width, f], keep[:, ds(c * T, width)], hs[b][:, 0:width, f],
                                                         hcarry[:, f:f + 1], ALU.mult, ALU.add)
                    st.link(r)
                    st.link(nc.vector.tensor_copy(hcarry[:], hs[b][:, width - 1, :]))
                    dve.sem_inc(s_o, 1)
                    assert st.n == K, st.n
                with nc.Fori(0, PAIRS, engines=[nc.vector.engine]) as i:
                    chunk(i * 2, i, 0, i * (2 * NB), i * 16 + 16)
                    chunk(i * 2 + 1, i, 1, i * (2 * NB) + NB, i * 16 + 32)
                chunk(2 * PAIRS, PAIRS, 0, 2 * PAIRS * NB, None, TAIL)
                nc.vector.tensor_copy(last0[:], hcarry[:]).then_inc(s_v, 1)

        boundary("mlp_boundary", last0[:], scan_d[2], HID, ALU.add, 0.0)
        node_block("mlp_nodes", 2, scan_d[2], HID, x_d[1])

        plain_edges("gcn_edges", feat_d, scan_d[3], keep, ALU.add, 0.0, False)
        boundary("gcn_boundary", last0[:, 0:D], scan_d[3], D, ALU.add, 0.0)
        node_block("gcn_nodes", 3, scan_d[3], D, x_d[2])


_INS = ['x', 'src', 'dst', 'edge_attr_6', 'L0_gnn_Wq', 'L0_gnn_Wk', 'L0_gnn_Wv', 'L0_gnn_Wo', 'L1_gnn_W', 'L1_gnn_b',
        'L2_gnn_phi_w1', 'L2_gnn_phi_b1', 'L2_gnn_phi_w2', 'L2_gnn_phi_b2', 'L2_gnn_g_w1', 'L2_gnn_g_b1',
        'L2_gnn_g_w2', 'L2_gnn_g_b2', 'L3_gnn_W']


def kernel(**inputs):
    import numpy as _np
    import concourse.bacc as _bacc
    from concourse import mybir as _mybir
    from concourse.bass_utils import run_bass_kernel_spmd as _run

    nc = _bacc.Bacc("TRN2", target_bir_lowering=False, num_devices=1)
    arrays, ap = {}, {}
    for name in _INS:
        a = _np.asarray(inputs[name])
        if name == 'L1_gnn_W':
            a = a.T
        a = _np.ascontiguousarray(a)
        arrays["in_" + name] = a
        ap[name] = nc.dram_tensor("in_" + name, a.shape, _mybir.dt.from_np(a.dtype), kind="ExternalInput").ap()
    out = nc.dram_tensor("out_0", inputs['x'].shape, _mybir.dt.from_np(_np.dtype('float32')), kind="ExternalOutput").ap()
    build(nc, ap['x'], ap['src'], ap['dst'], ap['edge_attr_6'], (ap['L0_gnn_Wk'], ap['L0_gnn_Wv'], ap['L0_gnn_Wq']),
          ap['L0_gnn_Wo'], ap['L1_gnn_W'], ap['L1_gnn_b'], ap['L2_gnn_phi_w1'], ap['L2_gnn_phi_b1'], ap['L2_gnn_phi_w2'],
          ap['L2_gnn_phi_b2'], ap['L2_gnn_g_w1'], ap['L2_gnn_g_b1'], ap['L2_gnn_g_w2'], ap['L2_gnn_g_b2'], ap['L3_gnn_W'], out)
    r = _run(nc, [arrays], core_ids=[0])
    return r.results[0]["out_0"]
```

```python
import concourse.bass as bass
from concourse import mybir
from contextlib import ExitStack, contextmanager

P = 128
D = 64
HEADS = 4
HID = 128
EA = 6
T = 50
G = 10
R = 200
BIG = 1.0e30
SKIP = 8.0e6
MAGIC = 12582912.0
EPS = 1e-5


def build(nc, x_in, src_in, dst_in, ea_in, wkvq_parts, wo_in, w1t_in, b1_in, pw1_in, pb1_in, pw2_in, pb2_in,
          gw1_in, gb1_in, gw2_in, gb2_in, w3_in, out):
    f32, bf16, i32 = mybir.dt.float32, mybir.dt.bfloat16, mybir.dt.int32
    ALU, ACT, AX = mybir.AluOpType, mybir.ActivationFunctionType, mybir.AxisListType
    ds = bass.ds

    N = x_in.shape[0]
    E = src_in.shape[0]
    TALL = E // P
    PAIRS = TALL // (2 * T)
    TAIL = TALL - 2 * PAIRS * T
    assert E == P * TALL and 0 < TAIL <= T and TAIL % 5 == 0
    J = -(-N // P)
    J = -(-J // (2 * G)) * 2 * G
    NPART = N // J
    assert N == NPART * J and NPART < P
    assert E % R == 0 and G % 2 == 0
    NPAD = P * J
    GPAIRS = J // (2 * G)

    def dram(name, shape, dt=f32):
        return nc.dram_tensor(name, list(shape), dt, kind="Internal").ap()

    x_d = [dram(f"x_layer{n}", (NPAD, D)) for n in range(3)]
    kv_d = dram("kv_table", (NPAD, 2 * D))
    q_d = dram("q_table", (NPAD, D))
    own1_d = dram("edgeconv_own", (NPAD, D))
    nbr1_d = dram("edgeconv_neighbour_table", (NPAD, D))
    feat_d = dram("gcn_table", (NPAD, D))
    start_d = dram("rows_at_first_edges", (E, D))
    ROW0 = D + 2 * HEADS
    scan_d = [dram("scan_attention", (E, ROW0)), dram("scan_max", (E, D)), dram("scan_mlp", (E, HID)),
              dram("scan_gcn", (E, D))]
    row_d = dram("row_starts", (1, E // R), i32)
    last_d = dram("last_edge", (NPAD, 1), i32)
    first_d = dram("first_edge", (NPAD, 1), i32)

    def nodes(ap):
        return ap.rearrange("(p j) f -> p j f", p=P)

    def edges(ap):
        return ap.rearrange("(p t) f -> p t f", p=P)

    src_v = src_in.rearrange("(p t) -> p t", p=P)
    dst_v = dst_in.rearrange("(p t) -> p t", p=P)
    ea_v = edges(ea_in)

    ctx = ExitStack()
    ctx.enter_context(nc.allow_non_contiguous_dma(reason="columns of small tables"))

    def bc(ap, dim, n):
        wide = ap.unsqueeze(dim)
        shape = list(wide.shape)
        shape[dim] = n
        return wide.broadcast_to(shape)

    class Steps:

        def __init__(self, eng, sem, base=0):
            self.eng, self.sem, self.base, self.n = eng, sem, base, 0

        def step(self, ins):
            ins.then_inc(self.sem, 1)
            self.n += 1

        def wait(self):
            self.eng.wait_ge(self.sem, self.base + self.n)

        def link(self, ins):
            self.step(ins)
            self.wait()

    with ctx:
        phase_sems = []

        def sem(name):
            phase_sems.append(nc.alloc_semaphore(name=name))
            return phase_sems[-1]

        @contextmanager
        def phase(name):
            with ExitStack() as scope:
                with nc.Block(name) as block:
                    yield scope, block
            nc.clear_and_free_semaphores(phase_sems)
            phase_sems.clear()
            nc.all_engine_barrier()

        def maker(scope):
            def sb(name, shape, dt=f32):
                return scope.enter_context(nc.sbuf_tensor(name, list(shape), dt))

            def ps(name, shape, dt=f32):
                return scope.enter_context(nc.psum_tensor(name, list(shape), dt))
            return sb, ps

        sb, _ = maker(ctx)
        keep = sb("keep", [P, (2 * PAIRS + 1) * T])
        pen = sb("pen", [P, TALL])
        ident = sb("ident", [P, P])
        iota_row = sb("iota_row", [P, P], bf16)
        cnt_in = sb("cnt_in", [P, J])
        nonempty = sb("nonempty", [P, J])
        rcnt = sb("rcnt", [P, J])
        nsrc = sb("nsrc", [P, J])
        ndst = sb("ndst", [P, J])
        whole = sb("whole", [P, 1])
        fixidx = sb("fixidx", [P, 1], i32)
        qcarry = sb("qcarry", [P, D])
        dfirst = sb("dfirst", [P, 1], i32)

        with phase("setup") as (scope, block):
            sb, ps = maker(scope)
            NR = E // R
            dstx = sb("dstx", [P, TALL + 1], i32)
            starts = sb("starts", [P, NR], i32)
            less = [sb(f"less{b}", [P, NR]) for b in range(2)]
            sign = [sb(f"sign{b}", [P, R]) for b in range(2)]
            node32 = sb("node32", [P, J], i32)
            node = sb("node", [P, J])
            below = sb("below", [P, J])
            nrow = sb("nrow", [P, J])
            row = sb("row", [P, J])
            rowi = [sb(f"rowi{b}", [P, G], i32) for b in range(2)]
            found = [sb(f"found{b}", [P, G, R], i32) for b in range(2)]
            acc = sb("acc", [P, J])
            first = sb("first", [P, J])
            behind = sb("behind", [P, J])
            iota32 = sb("iota32", [P, P], i32)
            down = sb("down", [P, P])
            tmpJ = sb("tmpJ", [P, J])
            tmpK = sb("tmpK", [P, J])
            firsti = sb("firsti", [P, J], i32)
            lasti = sb("lasti", [P, J], i32)
            zeros = sb("zeros", [P, T * D])
            xg = [sb(f"xg{b}", [P, G, D]) for b in range(2)]
            wkvq = sb("wkvq", [P, 2, 3 * D])
            xT = sb("xT", [P, G // 2, P])
            kv_s = [sb(f"kv_s{b}", [P, G, 2 * D]) for b in range(2)]
            q_s = [sb(f"q_s{b}", [P, G, D]) for b in range(2)]
            p_tr = ps("p_tr", [P, 1024])
            p_mm = ps("p_mm", [P, 5, 512])
            p_h = ps("p_h", [P, 512])

            s_w, s_dst, s_z, s_dmin, s_const, s_id = (sem(n) for n in ("su_w", "su_dst", "su_zero", "su_min", "su_const", "su_id"))
            s_x = [sem(f"su_x{b}") for b in range(2)]
            s_tabs = [sem(f"su_tabs{b}") for b in range(2)]
            s_found = [sem(f"su_found{b}") for b in range(2)]
            s_xz, s_tr, s_xt, s_mm, s_tab, s_st, s_rd, s_starts, s_less, s_rowi, s_sign, s_foundf, s_v, s_first, s_next, s_fl, s_fill, s_deg, s_turn = (
                sem("su_" + n) for n in ("xz", "tr", "xt", "mm", "tab", "st", "rd", "starts", "less", "rowi", "sign", "foundf", "v", "first",
                                         "next", "fl", "fill", "deg", "turn"))

            @block.sync
            def _(sp):
                sp.dma_start(row_d, dst_in.rearrange("(o r k) -> o r k", o=1, k=R)[:, :, 0]).then_inc(s_rd, 16)
                sp.wait_ge(s_rd, 16)
                sp.dma_start(starts[:], row_d.broadcast_to([P, NR])).then_inc(s_starts, 16)
                sp.dma_start(dstx[:, 1:TALL + 1], dst_v).then_inc(s_dst, 16)
                sp.wait_ge(s_dmin, 1)
                sp.dma_start(dstx[1:P, 0:1], dst_v[0:P - 1, TALL - 1:TALL]).then_inc(s_dst, 16)
                sp.wait_ge(s_xz, 1)
                for h in range(2):
                    for n, w in enumerate(wkvq_parts):
                        sp.dma_start(wkvq[h * D:(h + 1) * D, h, n * D:(n + 1) * D], w).then_inc(s_w, 16)
                xv = x_in.rearrange("(p j) f -> p j f", j=J)

                def load_x(g, b):
                    sp.dma_start(xg[b][0:NPART], xv[:, ds(g * G, G), :]).then_inc(s_x[b], 16)

                def store(g, b):
                    sp.wait_ge(s_tab, g * 2 + 2)
                    sp.dma_start(nodes(kv_d)[:, ds(g * G, G), :], kv_s[b][:]).then_inc(s_tabs[b], 16)
                    sp.dma_start(nodes(q_d)[:, ds(g * G, G), :], q_s[b][:]).then_inc(s_tabs[b], 16)
                load_x(0, 0)
                load_x(1, 1)
                if GPAIRS > 1:
                    with nc.Fori(0, GPAIRS - 1, engines=[nc.sync.engine]) as i:
                        for b in range(2):
                            store(i * 2 + b, b)
                            load_x(i * 2 + b + 2, b)
                for b in range(2):
                    store(2 * GPAIRS - 2 + b, b)
                sp.wait_ge(s_fl, 2)
                sp.dma_start(nodes(first_d)[:, :, 0], firsti[:]).then_inc(s_st, 16)
                sp.dma_start(nodes(last_d)[:, :, 0], lasti[:]).then_inc(s_st, 16)
                sp.wait_ge(s_fill, 16 * (2 * PAIRS + 1))
                sp.wait_ge(s_st, 32)
                for b in range(2):
                    sp.wait_ge(s_tabs[b], 32 * GPAIRS)

            @block.gpsimd
            def _(pool):
                nc.gpsimd.iota(iota32[:], pattern=[[1, P]], base=0, channel_multiplier=0).then_inc(s_id, 1)
                nc.gpsimd.memset(ident[:], 0.0).then_inc(s_id, 1)
                nc.gpsimd.memset(down[:], 0.0).then_inc(s_id, 1)
                nc.gpsimd.iota(node32[:], pattern=[[1, J]], base=0, channel_multiplier=J).then_inc(s_id, 1)
                pool.wait_ge(s_id, 4)
                nc.gpsimd.affine_select(out=ident[:], in_=ident[:], compare_op=ALU.not_equal, fill=1.0,
                                        base=0, pattern=[[-1, P]], channel_multiplier=1).then_inc(s_id, 1)
                nc.gpsimd.affine_select(out=down[:], in_=down[:], compare_op=ALU.not_equal, fill=1.0,
                                        base=-1, pattern=[[-1, P]], channel_multiplier=1).then_inc(s_id, 1)
                rows_v = dst_in.rearrange("(r k) -> r k", k=R)
                with nc.Fori(0, GPAIRS, engines=[nc.gpsimd.engine]) as i:
                    for b in range(2):
                        pool.wait_ge(s_rowi, i * 2 + b + 1)
                        pool.wait_ge(s_foundf, i * 2 + b + 1)
                        pool.sem_inc(s_turn, 1)
                        for j in range(G):
                            nc.gpsimd.indirect_dma_start(found[b][:, j, :], None, rows_v,
                                                         bass.IndirectOffsetOnAxis(ap=rowi[b][:, j:j + 1], axis=0)).then_inc(s_found[b], 16)

            @block.vector
            def _(dve):
                st = Steps(dve, s_v)
                nc.vector.memset(zeros[:], 0.0).then_inc(s_z, 1)
                nc.vector.memset(dstx[:, 0:1], -1).then_inc(s_dmin, 1)
                st.step(nc.vector.memset(xg[0][:], 0.0))
                st.step(nc.vector.memset(xg[1][:], 0.0))
                st.step(nc.vector.memset(wkvq[:], 0.0))
                st.wait()
                dve.sem_inc(s_xz, 1)
                st.step(nc.vector.memset(keep[:], 0.0))
                dve.wait_ge(s_id, 4)
                st.step(nc.vector.tensor_copy(iota_row[:], iota32[:]))
                st.step(nc.vector.tensor_copy(node[:], node32[:]))
                st.link(nc.vector.tensor_scalar(below[:], node32[:], -0.5, None, ALU.add))
                dve.sem_inc(s_const, 1)
                dve.sem_inc(s_less, 2)
                dve.wait_ge(s_starts, 16)
                setup = st.n

                def rows_of(g, i, b):
                    st = Steps(dve, s_v, g * 1 + setup)
                    slots = ds(g * G, G)
                    for j in range(G):
                        dve.wait_ge(s_less, g * G + j + 1)
                        nc.vector.tensor_scalar(less[j % 2][:], starts[:], node[:, ds(g * G + j, 1)], None, ALU.is_lt, ALU.add,
                                                accum_out=nrow[:, ds(g * G + j, 1)]).then_inc(s_less, 1)
                    dve.wait_ge(s_less, g * G + G + 2)
                    st.step(nc.vector.tensor_scalar(row[:, slots], nrow[:, slots], -1.0, 0.0, ALU.add, ALU.max))
                    dve.wait_ge(s_found[b], i * (16 * G))
                    nc.vector.tensor_scalar(rowi[b][:], nrow[:, slots], -1.0, 0.0, ALU.add, ALU.max).then_inc(s_rowi, 1)
                with nc.Fori(0, GPAIRS, engines=[nc.vector.engine]) as i:
                    for b in range(2):
                        rows_of(i * 2 + b, i, b)
                st = Steps(dve, s_v, 2 * GPAIRS + setup)
                dve.wait_ge(s_dst, 32)
                st.step(nc.vector.tensor_copy(dfirst[:], dstx[:, 1:2]))
                st.link(nc.vector.tensor_tensor(keep[:, 0:TALL], dstx[:, 1:TALL + 1], dstx[:, 0:TALL], ALU.is_equal))
                st.link(nc.vector.tensor_scalar(pen[:], keep[:, 0:TALL], -1.0, BIG, ALU.add, ALU.mult))
                dve.wait_ge(s_sign, 2 * GPAIRS * G + 2)
                st.link(nc.vector.tensor_scalar(acc[:], acc[:], 0.5, R / 2, ALU.mult, ALU.add))
                st.link(nc.vector.scalar_tensor_tensor(first[:], row[:], float(R), acc[:], ALU.mult, ALU.add))
                dve.sem_inc(s_first, 1)
                st.step(nc.vector.tensor_copy(behind[:, 0:J - 1], first[:, 1:J]))
                dve.wait_ge(s_next, 1)
                st.step(nc.vector.tensor_tensor(behind[:, J - 1:J], p_h[:, 0:1], first[:, J - 1:J], ALU.max))
                st.wait()
                st.step(nc.vector.tensor_tensor(cnt_in[:], behind[:], first[:], ALU.subtract))
                nc.vector.tensor_scalar(lasti[:], behind[:], -1.0, 0.0, ALU.add, ALU.max).then_inc(s_fl, 1)
                st.step(nc.vector.tensor_scalar(tmpK[:], first[:], -SKIP, None, ALU.add))
                st.wait()
                st.step(nc.vector.tensor_scalar(nonempty[:], cnt_in[:], 0.0, None, ALU.is_gt))
                st.link(nc.vector.tensor_scalar(tmpJ[:], cnt_in[:], 1.0, None, ALU.max))
                dve.sem_inc(s_deg, 1)
                st.link(nc.vector.reciprocal(rcnt[:], tmpJ[:]))
                st.step(nc.vector.tensor_tensor(rcnt[:], rcnt[:], nonempty[:], ALU.mult))
                st.link(nc.vector.tensor_tensor(tmpK[:], tmpK[:], nonempty[:], ALU.mult))
                nc.vector.tensor_scalar(firsti[:], tmpK[:], SKIP, None, ALU.add).then_inc(s_fl, 1)

            @block.scalar
            def _(act):
                def tables(g, i, b):
                    act.wait_ge(s_tr, g + 1)
                    nc.scalar.activation(xT[:], p_tr[:, 0:G * D].rearrange("p (k n) -> p k n", n=P), ACT.Copy).then_inc(s_xt, 1)
                    act.wait_ge(s_mm, g + 1)
                    act.wait_ge(s_tabs[b], i * 32)
                    mm = p_mm[:, :, 0:6 * D].rearrange("p k (h f) -> p k h f", h=2)
                    nc.scalar.activation(kv_s[b][:].rearrange("p (k h) f -> p k h f", h=2), mm[:, :, :, 0:2 * D], ACT.Copy).then_inc(s_tab, 1)
                    nc.scalar.activation(q_s[b][:].rearrange("p (k h) f -> p k h f", h=2), mm[:, :, :, 2 * D:3 * D], ACT.Copy,
                                         scale=(D // HEADS) ** -0.5).then_inc(s_tab, 1)

                def count(g, i, b):
                    act.wait_ge(s_found[b], i * (16 * G) + 16 * G)
                    for j in range(G):
                        act.wait_ge(s_sign, g * G + j + 1)
                        nc.scalar.activation(sign[j % 2][:], found[b][:, j, :], ACT.Sign, bias=below[:, ds(g * G + j, 1)],
                                             scale=-1.0, accum_out=acc[:, ds(g * G + j, 1)]).then_inc(s_sign, 1)
                    act.wait_ge(s_sign, g * G + G + 2)
                    act.sem_inc(s_foundf, 1)

                def fill(c, width=T):
                    act.dma_start(edges(start_d)[:, ds(c * T, width), :],
                                  zeros[:, 0:width * D].rearrange("p (t f) -> p t f", f=D)).then_inc(s_fill, 16)
                FILLS = 2 * PAIRS // (2 * GPAIRS)
                act.sem_inc(s_sign, 2)
                act.sem_inc(s_foundf, 2)
                act.wait_ge(s_z, 1)
                act.wait_ge(s_const, 1)
                with nc.Fori(0, GPAIRS, engines=[nc.scalar.engine]) as i:
                    for b in range(2):
                        g = i * 2 + b
                        for k in range(FILLS):
                            fill(g * FILLS + k)
                        tables(g, i, b)
                        count(g, i, b)
                for c in range(2 * GPAIRS * FILLS, 2 * PAIRS):
                    fill(c)
                fill(2 * PAIRS, TAIL)
                act.wait_ge(s_fill, 16 * (2 * PAIRS + 1))
                act.wait_ge(s_deg, 1)
                nc.scalar.activation(ndst[:], tmpJ[:], ACT.Sqrt).then_inc(s_deg, 1)

            @block.tensor
            def _(pe):
                pe.wait_ge(s_id, 6)
                pe.wait_ge(s_w, 96)

                def tables(g, i, b):
                    pe.wait_ge(s_x[b], i * 16 + 16)
                    for k in range(G // 2):
                        tr = nc.tensor.transpose(p_tr[:, k * P:(k + 1) * P], xg[b][:, 2 * k:2 * k + 2, :].rearrange("p h f -> p (h f)"), ident[:])
                    tr.then_inc(s_tr, 1)
                    pe.wait_ge(s_tab, g * 2)
                    pe.wait_ge(s_xt, g + 1)
                    for k in range(G // 2):
                        mm = nc.tensor.matmul(p_mm[:, k, 0:6 * D], xT[:, k, :], wkvq[:].rearrange("p h f -> p (h f)"), start=True, stop=True)
                    mm.then_inc(s_mm, 1)
                with nc.Fori(0, GPAIRS, engines=[nc.tensor.engine]) as i:
                    for b in range(2):
                        tables(i * 2 + b, i, b)
                pe.wait_ge(s_first, 1)
                nc.tensor.matmul(p_h[:, 0:1], down[:], first[:, 0:1], start=True, stop=True).then_inc(s_next, 1)

        with phase("scatter_q") as (scope, block):
            sb, ps = maker(scope)
            idx = [sb(f"sq_idx{b}", [P, G], i32) for b in range(2)]
            row = [sb(f"sq_row{b}", [P, G, D]) for b in range(2)]
            lastf = sb("sq_last", [P, 1], i32)
            t = sb("sq_t", [P, 4])
            pidx = sb("sq_p", [P, 2], i32)
            s_in = [sem(f"sq_in{b}") for b in range(2)]
            s_sc = [sem(f"sq_sc{b}") for b in range(2)]
            s_g, s_v, s_io, s_turn = sem("sq_g"), sem("sq_v"), sem("sq_io"), sem("sq_turn")

            @block.sync
            def _(sp):
                def load(g, b):
                    sp.dma_start(idx[b][:], nodes(first_d)[:, ds(g * G, G), 0]).then_inc(s_in[b], 16)
                    sp.dma_start(row[b][:], nodes(q_d)[:, ds(g * G, G), :]).then_inc(s_in[b], 16)
                load(0, 0)
                load(1, 1)
                if GPAIRS > 1:
                    with nc.Fori(1, GPAIRS, engines=[nc.sync.engine]) as i:
                        for b in range(2):
                            sp.wait_ge(s_sc[b], i * (16 * G))
                            load(i * 2 + b, b)

            @block.gpsimd
            def _(pool):
                nc.gpsimd.indirect_dma_start(qcarry[:], None, q_d, bass.IndirectOffsetOnAxis(ap=dfirst[:, 0:1], axis=0)).then_inc(s_g, 16)
                nc.gpsimd.indirect_dma_start(lastf[:], None, last_d, bass.IndirectOffsetOnAxis(ap=dfirst[:, 0:1], axis=0)).then_inc(s_g, 16)
                nc.gpsimd.iota(pidx[:, 0:1], pattern=[[1, 1]], base=0, channel_multiplier=TALL).then_inc(s_io, 1)
                with nc.Fori(0, GPAIRS, engines=[nc.gpsimd.engine]) as i:
                    for b in range(2):
                        pool.wait_ge(s_in[b], i * 32 + 32)
                        pool.sem_inc(s_turn, 1)
                        for j in range(G):
                            nc.gpsimd.indirect_dma_start(start_d, bass.IndirectOffsetOnAxis(ap=idx[b][:, j:j + 1], axis=0),
                                                         row[b][:, j, :], None, bounds_check=E - 1, oob_is_err=False).then_inc(s_sc[b], 16)
                pool.wait_ge(s_sc[0], GPAIRS * 16 * G)
                pool.wait_ge(s_sc[1], GPAIRS * 16 * G)
                pool.wait_ge(s_g, 32)

            @block.vector
            def _(dve):
                st = Steps(dve, s_v)
                dve.wait_ge(s_g, 32)
                dve.wait_ge(s_io, 1)
                st.step(nc.vector.tensor_copy(t[:, 0:1], lastf[:]))
                st.link(nc.vector.tensor_copy(t[:, 1:2], pidx[:, 0:1]))
                st.link(nc.vector.tensor_tensor(t[:, 2:3], t[:, 0:1], t[:, 1:2], ALU.subtract))
                st.link(nc.vector.tensor_scalar(whole[:], t[:, 2:3], float(TALL - 1), None, ALU.is_ge))
                st.link(nc.vector.tensor_tensor(whole[:], whole[:], keep[:, 0:1], ALU.mult))
                st.link(nc.vector.tensor_scalar(t[:, 3:4], t[:, 2:3], float(TALL - 1), None, ALU.is_le))
                st.link(nc.vector.tensor_tensor(t[:, 3:4], t[:, 3:4], keep[:, 0:1], ALU.mult))
                st.link(nc.vector.tensor_scalar(t[:, 0:1], t[:, 0:1], -SKIP, None, ALU.add))
                st.link(nc.vector.tensor_tensor(t[:, 0:1], t[:, 0:1], t[:, 3:4], ALU.mult))
                st.link(nc.vector.tensor_scalar(fixidx[:], t[:, 0:1], SKIP, None, ALU.add))
                st.link(nc.vector.reciprocal(ndst[:], ndst[:]))
                st.link(nc.vector.tensor_tensor(ndst[:], ndst[:], nonempty[:], ALU.mult))

        def pool_gathers(pool, table, idx, rows, s_idx, s_free, s_rows, s_turn, at=0):
            def chunk(b, i, width):
                pool.wait_ge(s_idx[b], i * 16 + 16)
                pool.wait_ge(s_free[b], i + 1)
                pool.sem_inc(s_turn, 1)
                for t in range(width):
                    nc.gpsimd.indirect_dma_start(rows[b][:, t, at:], None, table,
                                                 bass.IndirectOffsetOnAxis(ap=idx[b][:, t:t + 1], axis=0)).then_inc(s_rows[b], 16)
            with nc.Fori(0, PAIRS, engines=[nc.gpsimd.engine]) as i:
                for b in range(2):
                    chunk(b, i, T)
            chunk(0, PAIRS, TAIL)

        def boundary(name, last, scan_out, width, op, none):
            with phase(name) as (scope, block):
                sb, ps = maker(scope)
                gate = sb(f"{name}_gate", [P, width])
                carry = sb(f"{name}_carry", [P, width])
                rows = sb(f"{name}_rows", [P, width])
                gateT = sb(f"{name}_gateT", [width, P])
                runT = sb(f"{name}_runT", [width, P + 1])
                pa, pb, pc = ps(f"{name}_pa", [P, 512]), ps(f"{name}_pb", [P, 512]), ps(f"{name}_pc", [P, 512])
                s_v, s_t, s_g, s_s, s_m = (sem(f"{name}_{n}") for n in ("v", "t", "g", "s", "m"))
                first = ALU.mult if op == ALU.add else ALU.add

                @block.vector
                def _(dve):
                    st = Steps(dve, s_v)
                    nc.vector.memset(rows[:], 0.0).then_inc(s_m, 1)
                    st.step(nc.vector.memset(runT[:, 0:1], none))
                    if op == ALU.add:
                        st.step(nc.vector.tensor_copy(gate[:], bc(whole[:, 0], 1, width)))
                    else:
                        st.step(nc.vector.tensor_scalar(gate[:], bc(whole[:, 0], 1, width), -1.0, BIG, ALU.add, ALU.mult))
                    dve.wait_ge(s_t, 2)
                    st.link(nc.vector.tensor_copy(gateT[:], pa[0:width, 0:P]))
                    nc.vector.tensor_tensor_scan(runT[:, 1:P + 1], gateT[:], pb[0:width, 0:P], none, first, op).then_inc(s_v, 1)
                    dve.wait_ge(s_t, 3)
                    st.n += 1
                    st.link(nc.vector.tensor_copy(carry[:], pc[:, 0:width]))
                    dve.wait_ge(s_g, 16)
                    nc.vector.tensor_tensor(rows[:], rows[:], carry[:], op).then_inc(s_m, 1)

                @block.tensor
                def _(pe):
                    pe.wait_ge(s_v, 2)
                    nc.tensor.transpose(pa[0:width, 0:P], gate[:], ident[:]).then_inc(s_t, 1)
                    nc.tensor.transpose(pb[0:width, 0:P], last, ident[:]).then_inc(s_t, 1)
                    pe.wait_ge(s_v, 4)
                    nc.tensor.transpose(pc[:, 0:width], runT[:, 0:P], ident[0:width, 0:width]).then_inc(s_t, 1)

                @block.gpsimd
                def _(pool):
                    pool.wait_ge(s_m, 1)
                    nc.gpsimd.indirect_dma_start(rows[:], None, scan_out, bass.IndirectOffsetOnAxis(ap=fixidx[:, 0:1], axis=0),
                                                 bounds_check=E - 1, oob_is_err=False).then_inc(s_g, 16)
                    pool.wait_ge(s_m, 2)
                    nc.gpsimd.indirect_dma_start(scan_out, bass.IndirectOffsetOnAxis(ap=fixidx[:, 0:1], axis=0), rows[:], None,
                                                 bounds_check=E - 1, oob_is_err=False).then_inc(s_s, 16)
                    pool.wait_ge(s_s, 16)

        def node_block(name, layer, scan_out, width, x_prev, own_d=None):
            with phase(name) as (scope, block):
                sb, ps = maker(scope)

                def t(n, shape, dt=f32):
                    return sb(f"{name}_{n}", shape, dt)
                NG = 2 * GPAIRS
                XW = D + 1 if layer == 2 else D
                idx = [t(f"idx{b}", [P, G], i32) for b in range(2)]
                agg = [t(f"agg{b}", [P, G, width]) for b in range(2)]
                x_all = t("x", [P, J, XW])
                own_all = t("own", [P, J, D]) if own_d is not None else None
                last_all = t("last", [P, J], i32)
                first_all = t("first", [P, J], i32) if layer == 1 else None
                fidx = [t(f"fidx{b}", [P, G], i32) for b in range(2)] if layer == 1 else None
                y = t("y", [P, G, D])
                sq = t("sq", [P, G, D])
                s1, s2, rt = t("s1", [P, G]), t("s2", [P, G]), t("rt", [P, G])
                xn = [t(f"xn{b}", [P, G, D]) for b in range(2)]
                s_rows, s_ix, s_copy, s_fcopy = (sem(f"{name}_{n}") for n in ("rows", "ix", "copy", "fcopy"))
                s_ag = [sem(f"{name}_ag{b}") for b in range(2)]
                s_st = [sem(f"{name}_st{b}") for b in range(2)]
                s_sc = [sem(f"{name}_sc{b}") for b in range(2)] if layer == 1 else None
                s_vf, s_vb, s_vm, s_w, s_wz, s_w2, s_aggf, s_a, s_tr, s_evf, s_of, s_y, s_var, s_rt, s_xn, s_turn = (
                    sem(f"{name}_{n}") for n in ("vf", "vb", "vm", "w", "wz", "w2", "aggf", "a", "tr", "evf", "of", "y", "var", "rt", "xn", "turn"))
                if layer != 1:
                    p_o = ps(f"{name}_po", [P, 2, 512])
                diagonal = []
                if layer == 0:
                    w_out, w_next = t("wo", [P, 2, D]), t("wn", [P, 2, 2 * D])
                    wa, wb = t("wa", [P, 2, D]), t("wb", [P, 2, D])
                    loads = [(w_out[h * D:(h + 1) * D, h, :], wo_in) for h in range(2)]
                    loads += [(wa[h * D:(h + 1) * D, h, :], w1t_in[0:D, :]) for h in range(2)]
                    loads += [(wb[h * D:(h + 1) * D, h, :], w1t_in[D:2 * D, :]) for h in range(2)]
                    diagonal = [w_out, wa, wb]
                    own_s, nbr_s = t("own_s", [P, G, D]), t("nbr_s", [P, G, D])
                    f4, g4, h4 = t("f4", [P, G, HEADS]), t("g4", [P, G, HEADS]), t("h4", [P, G, HEADS])
                    a = [t(f"a{b}", [P, G, D]) for b in range(2)]
                    aT, xT = t("aT", [P, G // 2, P]), t("xT", [P, G // 2, P])
                    p_ta = ps(f"{name}_pta", [P, 640])
                    p_tab = ps(f"{name}_ptab", [P, 3, 512])
                    s_dm, s_ex, s_trx, s_evx, s_tab, s_tabs, s_tt = (sem(f"{name}_{n}") for n in ("dm", "ex", "trx", "evx", "tab", "tabs", "tt"))
                elif layer == 1:
                    bias = t("bias", [P, D])
                    loads = [(bias[:], bc(b1_in, 0, P))]
                elif layer == 2:
                    wp2T = t("wp2T", [D, HID])
                    wp2, wg1b, wgx, wg2 = t("wp2", [HID, D]), t("wg1b", [D, HID]), t("wgx", [D + 1, HID]), t("wg2", [HID, D])
                    wga = t("wga", [HID, HID])
                    bp2 = t("bp2", [D, D + 1])
                    bg1 = t("bg1", [HID, 1])
                    bg2 = t("bg2", [1, 8, D])
                    xs = [t(f"xs{b}", [P, G, D + 1]) for b in range(2)]
                    ones = t("ones", [1, P])
                    loads = [(wp2[:], pw2_in), (wg1b[:], gw1_in[D:2 * D, :]), (wgx[0:D, :], gw1_in[0:D, :]), (wg2[:], gw2_in),
                             (bp2[:, D:D + 1], pb2_in.unsqueeze(1)), (bg1[:], gb1_in.unsqueeze(1))]
                    loads += [(bg2[:, k, :], bc(gb2_in, 0, 1)) for k in range(8)]
                    diagonal = [bp2]
                    a = [t(f"a{b}", [P, G, HID]) for b in range(2)]
                    aT, xT = t("aT", [P, G, P]), t("xT", [D + 1, G, P])
                    be, br = t("be", [P, G, P]), t("br", [P, G, P])
                    feat_s = t("feat_s", [P, G, D])
                    p_ta, p_z = ps(f"{name}_pta", [P, 3, 512]), ps(f"{name}_pz", [P, 3, 512])
                    s_z, s_el, s_elu, s_feat, s_tabs = (sem(f"{name}_{n}") for n in ("z", "el", "elu", "feat", "tabs"))
                else:
                    w_out = t("wo", [P, 2, D])
                    diagonal = [w_out]
                    loads = [(w_out[h * D:(h + 1) * D, h, :], w3_in) for h in range(2)]
                    a = t("a", [P, G, D])
                    aT = t("aT", [P, G // 2, P])
                    p_ta = ps(f"{name}_pta", [P, 640])
                x_v = x_in.rearrange("(p j) f -> p j f", j=J) if layer == 0 else nodes(x_prev)
                out_v = out.rearrange("(p j) f -> p j f", j=J)
                NXP = NPART if layer == 0 else P

                def slots_of(psum, n):
                    return psum[:].rearrange("p k n -> p (k n)")[:, 0:G * n].rearrange("p (g f) -> p g f", f=n)

                def skewed(eng, *steps):
                    def turn(g, i, b, left=2):
                        for step, ahead in steps:
                            if ahead <= left:
                                step(g + ahead, i + (b + ahead) // 2, (b + ahead) % 2)
                    for step, ahead in steps:
                        for g in range(ahead):
                            step(g, 0, g)
                    if GPAIRS > 1:
                        with nc.Fori(0, GPAIRS - 1, engines=[eng]) as i:
                            for b in range(2):
                                turn(i * 2 + b, i, b)
                    turn(NG - 2, GPAIRS - 1, 0, left=1)
                    turn(NG - 1, GPAIRS - 1, 1, left=0)

                @block.sync
                def _(sp):
                    sp.dma_start(last_all[:], nodes(last_d)[:, :, 0]).then_inc(s_ix, 16)
                    if layer == 1:
                        sp.dma_start(first_all[:], nodes(first_d)[:, :, 0]).then_inc(s_ix, 16)
                        sp.dma_start(own_all[:], nodes(own_d)).then_inc(s_rows, 16)
                    sp.wait_ge(s_wz, 1)
                    for o, w in loads:
                        sp.dma_start(o, w).then_inc(s_w, 16)
                    sp.dma_start(x_all[0:NXP, :, 0:D], x_v).then_inc(s_rows, 16)

                    def store(g, b):
                        sp.wait_ge(s_xn, g + 1)
                        if layer == 3:
                            sp.dma_start(out_v[:, ds(g * G, G), :], xn[b][0:NPART]).then_inc(s_st[b], 16)
                        else:
                            sp.dma_start(nodes(x_d[layer])[:, ds(g * G, G), :], xn[b][:]).then_inc(s_st[b], 16)
                        if layer == 0:
                            sp.wait_ge(s_tab, g + 1)
                            sp.dma_start(nodes(own1_d)[:, ds(g * G, G), :], own_s[:]).then_inc(s_tabs, 16)
                            sp.dma_start(nodes(nbr1_d)[:, ds(g * G, G), :], nbr_s[:]).then_inc(s_tabs, 16)
                        if layer == 2:
                            sp.wait_ge(s_feat, g + 1)
                            sp.dma_start(nodes(feat_d)[:, ds(g * G, G), :], feat_s[:]).then_inc(s_tabs, 16)
                    with nc.Fori(0, GPAIRS, engines=[nc.sync.engine]) as i:
                        for b in range(2):
                            store(i * 2 + b, b)
                    for b in range(2):
                        sp.wait_ge(s_st[b], 16 * GPAIRS)
                        if layer == 1:
                            sp.wait_ge(s_sc[b], 16 * G * GPAIRS)
                    if layer in (0, 2):
                        sp.wait_ge(s_tabs, 16 * NG * (2 if layer == 0 else 1))

                @block.gpsimd
                def _(pool):
                    pool.wait_ge(s_ix, 16 + 16 * (layer == 1))

                    def gather(g, i, b):
                        pool.wait_ge(s_ag[b], i * (16 * G))
                        nc.gpsimd.tensor_copy(idx[b][:], last_all[:, ds(g * G, G)]).then_inc(s_copy, 1)
                        pool.wait_ge(s_aggf, g + 1)
                        pool.wait_ge(s_copy, g + 1)
                        pool.sem_inc(s_turn, 1)
                        for j in range(G):
                            nc.gpsimd.indirect_dma_start(agg[b][:, j, :], None, scan_out,
                                                         bass.IndirectOffsetOnAxis(ap=idx[b][:, j:j + 1], axis=0)).then_inc(s_ag[b], 16)

                    def scatter(g, i, b):
                        if layer != 1:
                            return
                        pool.wait_ge(s_sc[b], i * (16 * G))
                        nc.gpsimd.tensor_copy(fidx[b][:], first_all[:, ds(g * G, G)]).then_inc(s_fcopy, 1)
                        pool.wait_ge(s_xn, g + 1)
                        pool.wait_ge(s_fcopy, g + 1)
                        pool.sem_inc(s_turn, 1)
                        for j in range(G):
                            nc.gpsimd.indirect_dma_start(start_d, bass.IndirectOffsetOnAxis(ap=fidx[b][:, j:j + 1], axis=0),
                                                         xn[b][:, j, :], None, bounds_check=E - 1, oob_is_err=False).then_inc(s_sc[b], 16)
                    skewed(nc.gpsimd.engine, (gather, 1), (scatter, 0))

                @block.vector
                def _(dve):
                    su = Steps(dve, s_vm)
                    for w in ([x_all] if layer == 0 else []) + diagonal:
                        su.step(nc.vector.memset(w[:], 0.0))
                    if layer == 2:
                        su.step(nc.vector.memset(ones[:], 1.0))
                    if layer != 1:
                        su.wait()
                    if layer == 2:
                        su.link(nc.vector.tensor_copy(x_all[:, :, D], nonempty[:]))
                    dve.sem_inc(s_wz, 1)
                    dve.sem_inc(s_aggf, 2)
                    if layer == 0:
                        dve.wait_ge(s_w, 16 * len(loads))
                        su.step(nc.vector.tensor_tensor(w_next[:, :, 0:D], wa[:], wb[:], ALU.subtract))
                        su.step(nc.vector.tensor_copy(w_next[:, :, D:2 * D], wb[:]))
                        su.wait()
                        dve.sem_inc(s_w2, 1)
                    if layer == 2:
                        dve.wait_ge(s_w2, 1)
                        su.link(nc.vector.tensor_copy(wp2T[:], p_z[0:D, 0, 0:HID]))
                        dve.sem_inc(s_w2, 1)
                        dve.wait_ge(s_w2, 3)
                        su.step(nc.vector.tensor_copy(wga[:], p_z[:, 1, 0:HID]))
                        su.step(nc.vector.tensor_copy(wgx[D:D + 1, :], p_z[D:D + 1, 2, 0:HID]))
                        su.wait()
                        dve.sem_inc(s_w2, 1)
                    KF = {0: 7, 1: 0, 2: 0, 3: 0}[layer]
                    KB = {0: 8, 1: 10, 2: 10, 3: 8}[layer]

                    def front(g, i, b):
                        st = Steps(dve, s_vf, g * KF)
                        slots = ds(g * G, G)
                        if layer == 1:
                            return
                        dve.wait_ge(s_ag[b], i * (16 * G) + 16 * G)
                        R = agg[b]
                        if layer == 0:
                            M = R[:, :, D + HEADS:D + 2 * HEADS]
                            st.link(nc.vector.tensor_scalar(f4[:], M, -1e9, None, ALU.max))
                            nc.vector.tensor_tensor(g4[:], M, f4[:], ALU.subtract).then_inc(s_dm, 1)
                            dve.wait_ge(s_ex, g + 1)
                            st.link(nc.vector.tensor_tensor(f4[:], R[:, :, D:D + HEADS], h4[:], ALU.mult))
                            st.link(nc.vector.tensor_scalar(f4[:], f4[:], 1e-9, None, ALU.add))
                            st.link(nc.vector.reciprocal(g4[:], f4[:]))
                            st.link(nc.vector.tensor_tensor(g4[:], g4[:], h4[:], ALU.mult))
                            st.link(nc.vector.tensor_tensor(g4[:], g4[:], bc(nonempty[:, slots], 2, HEADS), ALU.mult))
                            dve.wait_ge(s_tr, g)
                            nc.vector.tensor_tensor(a[b][:].rearrange("p g (h e) -> p g h e", h=HEADS),
                                                    R[:, :, 0:D].rearrange("p g (h e) -> p g h e", h=HEADS),
                                                    bc(g4[:], 3, D // HEADS), ALU.mult).then_inc(s_a, 1)
                            st.n += 1
                            dve.wait_ge(s_a, g + 1)
                            dve.sem_inc(s_vf, 1)
                        elif layer == 2:
                            dve.wait_ge(s_tr, g * 2)
                            nc.vector.tensor_copy(xs[b][:], x_all[:, slots, :]).then_inc(s_a, 1)
                            nc.vector.tensor_tensor(a[b][:], R[:], bc(rcnt[:, slots], 2, HID), ALU.mult).then_inc(s_a, 1)
                            dve.wait_ge(s_a, g * 2 + 2)
                        else:
                            dve.wait_ge(s_tr, g)
                            nc.vector.tensor_tensor(a[:], R[:], bc(ndst[:, slots], 2, D), ALU.mult).then_inc(s_a, 1)
                            dve.wait_ge(s_a, g + 1)
                        dve.sem_inc(s_aggf, 1)
                        assert st.n == KF, st.n

                    def mid(g, i, b):
                        dve.wait_ge(s_el, g * 2 + 2)
                        nc.vector.scalar_tensor_tensor(be[:], be[:], 1.0, br[:], ALU.min, ALU.add).then_inc(s_elu, 1)

                    def back(g, i, b):
                        st = Steps(dve, s_vb, g * KB)
                        slots = ds(g * G, G)
                        if layer == 1:
                            dve.wait_ge(s_ag[b], i * (16 * G) + 16 * G)
                            st.link(nc.vector.tensor_tensor(sq[:], agg[b][:], own_all[:, slots, :], ALU.add))
                            dve.sem_inc(s_aggf, 1)
                            st.link(nc.vector.scalar_tensor_tensor(sq[:], sq[:], 0.0, bc(nonempty[:, slots], 2, D), ALU.max, ALU.mult))
                            st.link(nc.vector.tensor_tensor(y[:], sq[:], x_all[:, slots, :], ALU.add))
                        else:
                            dve.wait_ge(s_of, g + 1)
                            st.link(nc.vector.tensor_tensor(y[:], x_all[:, slots, 0:D], slots_of(p_o, D), ALU.add))
                        dve.sem_inc(s_y, 1)
                        st.link(nc.vector.tensor_reduce(s1[:], y[:], AX.X, ALU.add))
                        st.link(nc.vector.scalar_tensor_tensor(y[:], bc(s1[:], 2, D), -1.0 / D, y[:], ALU.mult, ALU.add))
                        st.link(nc.vector.tensor_tensor(sq[:], y[:], y[:], ALU.mult))
                        st.link(nc.vector.tensor_reduce(s2[:], sq[:], AX.X, ALU.add))
                        nc.vector.tensor_scalar(s2[:], s2[:], 1.0 / D, EPS, ALU.mult, ALU.add).then_inc(s_var, 1)
                        dve.wait_ge(s_rt, g + 1)
                        st.link(nc.vector.reciprocal(s2[:], rt[:]))
                        dve.wait_ge(s_st[b], i * 16)
                        if layer == 1:
                            dve.wait_ge(s_sc[b], i * (16 * G))
                        st.link(nc.vector.tensor_tensor(xn[b][:], y[:], bc(s2[:], 2, D), ALU.mult))
                        dve.sem_inc(s_xn, 1)
                        if layer == 2:
                            dve.wait_ge(s_tabs, g * 16)
                            st.link(nc.vector.tensor_tensor(feat_s[:], xn[b][:], bc(nsrc[:, slots], 2, D), ALU.mult))
                            dve.sem_inc(s_feat, 1)
                        while st.n < KB:
                            dve.sem_inc(s_vb, 1)
                            st.n += 1
                        assert st.n == KB, st.n
                    dve.wait_ge(s_rows, 16 + 16 * (layer == 1))
                    if layer == 1:
                        dve.wait_ge(s_w, 16)
                        su.link(nc.vector.tensor_tensor(own_all[:], own_all[:], bc(bias[:], 1, J), ALU.add))
                    if layer in (0, 2):
                        skewed(nc.vector.engine, *([(front, 2), (back, 0), (mid, 1)] if layer == 2 else [(back, 0), (front, 2)]))
                    else:
                        skewed(nc.vector.engine, (front, 1), (back, 0))

                @block.scalar
                def _(act):
                    def guard(g, i, b):
                        act.wait_ge(s_dm, g + 1)
                        nc.scalar.activation(h4[:], g4[:], ACT.Exp).then_inc(s_ex, 1)

                    def front(g, i, b):
                        if layer in (0, 3):
                            act.wait_ge(s_tr, g + 1 + (layer == 0))
                            nc.scalar.activation(aT[:], p_ta[:].rearrange("p (k n) -> p k n", n=P), ACT.Copy).then_inc(s_evf, 1)
                        if layer == 2:
                            act.wait_ge(s_tr, g * 2 + 3)
                            nc.scalar.activation(aT[:], slots_of(p_ta, P), ACT.Copy).then_inc(s_evf, 1)
                            act.wait_ge(s_tr, g * 2 + 4)
                            nc.scalar.activation(xT[:], slots_of(p_ta, P)[0:D + 1], ACT.Copy).then_inc(s_evf, 1)

                    def mid(g, i, b):
                        act.wait_ge(s_z, g + 1)
                        act.wait_ge(s_of, g)
                        nc.scalar.activation(be[:], slots_of(p_z, P), ACT.Exp, bias=bg1[:, 0:1])
                        nc.scalar.activation(br[:], slots_of(p_z, P), ACT.Relu, bias=bg1[:, 0:1]).then_inc(s_el, 1)
                        act.wait_ge(s_el, g * 2 + 1)
                        nc.scalar.activation(br[:], br[:], ACT.Copy, bias=-1.0).then_inc(s_el, 1)

                    def root(g, i, b):
                        act.wait_ge(s_var, g + 1)
                        nc.scalar.activation(rt[:], s2[:], ACT.Sqrt).then_inc(s_rt, 1)

                    def back(g, i, b):
                        act.wait_ge(s_trx, g + 1)
                        nc.scalar.activation(xT[:], p_ta[:].rearrange("p (k n) -> p k n", n=P), ACT.Copy).then_inc(s_evx, 1)
                        act.wait_ge(s_tt, g + 1)
                        act.wait_ge(s_tabs, g * 32)
                        tab = slots_of(p_tab, 2 * D)
                        nc.scalar.activation(own_s[:], tab[:, :, 0:D], ACT.Copy)
                        nc.scalar.activation(nbr_s[:], tab[:, :, D:2 * D], ACT.Copy).then_inc(s_tab, 1)
                    if layer == 2:
                        act.wait_ge(s_w2, 4)
                    if layer == 0:
                        skewed(nc.scalar.engine, (root, 0), (guard, 2), (front, 1), (back, 0))
                    elif layer == 2:
                        skewed(nc.scalar.engine, (front, 1), (mid, 1), (root, 0))
                    elif layer == 1:
                        skewed(nc.scalar.engine, (root, 0))
                    else:
                        skewed(nc.scalar.engine, (front, 1), (root, 0))

                @block.tensor
                def _(pe):
                    pe.wait_ge(s_w, 16 * len(loads))
                    if layer == 0:
                        pe.wait_ge(s_w2, 1)
                        pe.sem_inc(s_tr, 1)
                    if layer == 2:
                        nc.tensor.transpose(p_z[0:D, 0, 0:HID], wp2[:], ident[:]).then_inc(s_w2, 1)
                        pe.wait_ge(s_w2, 2)
                        nc.tensor.matmul(p_z[:, 1, 0:HID], wp2T[:], wg1b[:], start=True, stop=True)
                        nc.tensor.matmul(p_z[0:D + 1, 2, 0:HID], bp2[:], wg1b[:], start=True, stop=True).then_inc(s_w2, 1)
                        pe.wait_ge(s_w2, 4)
                        pe.sem_inc(s_tr, 2)

                    def pairs(rows):
                        for k in range(G // 2):
                            r = nc.tensor.transpose(p_ta[:, k * P:(k + 1) * P], rows[:, 2 * k:2 * k + 2, :].rearrange("p h f -> p (h f)"), ident[:])
                        return r

                    def front(g, i, b):
                        if layer in (0, 3):
                            pe.wait_ge(s_a, g + 1)
                            if layer == 3:
                                pe.wait_ge(s_evf, g)
                            pairs(a[b] if layer == 0 else a).then_inc(s_tr, 1)
                            pe.wait_ge(s_evf, g + 1)
                            pe.wait_ge(s_y, g)
                            w = w_out[:].rearrange("p h f -> p (h f)")
                            for k in range(G // 2):
                                r = nc.tensor.matmul(p_o[:, k // 4, (k % 4) * P:(k % 4 + 1) * P], aT[:, k, :], w, start=True, stop=True)
                            r.then_inc(s_of, 1)
                        if layer == 2:
                            pe.wait_ge(s_a, g * 2 + 2)
                            for s in range(G):
                                r = nc.tensor.transpose(p_ta[:, s // 4, (s % 4) * P:(s % 4 + 1) * P], a[b][:, s, :], ident[:])
                            r.then_inc(s_tr, 1)
                            pe.wait_ge(s_evf, g * 2 + 1)
                            for s in range(G):
                                r = nc.tensor.transpose(p_ta[0:D + 1, s // 4, (s % 4) * P:(s % 4 + 1) * P], xs[b][:, s, :], ident[:])
                            r.then_inc(s_tr, 1)
                            pe.wait_ge(s_evf, g * 2 + 2)
                            pe.wait_ge(s_el, g * 2)
                            for k in range(-(-G // 4)):
                                w = min(4, G - 4 * k)
                                nc.tensor.matmul(p_z[:, k, 0:w * P], wga[:], aT[:, 4 * k:4 * k + w, :].rearrange("p k n -> p (k n)"), start=True, stop=False)
                                r = nc.tensor.matmul(p_z[:, k, 0:w * P], wgx[:], xT[:, 4 * k:4 * k + w, :].rearrange("p k n -> p (k n)"), start=False, stop=True)
                            r.then_inc(s_z, 1)

                    def mid(g, i, b):
                        pe.wait_ge(s_elu, g + 1)
                        pe.wait_ge(s_y, g)
                        row = bg2[:].rearrange("o s f -> o (s f)")
                        for k in range(2):
                            n = min(8, G - 8 * k)
                            nc.tensor.matmul(p_o[:, k, 0:n * D], ones[:], row[:, 0:n * D], start=True, stop=False)
                        for s in range(G):
                            r = nc.tensor.matmul(p_o[:, s // 8, (s % 8) * D:(s % 8 + 1) * D], be[:, s, :], wg2[:], start=False,
                                                 stop=s % 8 == 7 or s == G - 1)
                        r.then_inc(s_of, 1)

                    def back(g, i, b):
                        pe.wait_ge(s_xn, g + 1)
                        pairs(xn[b]).then_inc(s_trx, 1)
                        pe.wait_ge(s_evx, g + 1)
                        pe.wait_ge(s_tab, g)
                        w = w_next[:].rearrange("p h f -> p (h f)")
                        for k in range(G // 2):
                            r = nc.tensor.matmul(p_tab[:, k // 2, (k % 2) * 4 * D:(k % 2 + 1) * 4 * D], xT[:, k, :], w,
                                                 start=True, stop=True)
                        r.then_inc(s_tt, 1)
                    if layer != 1:
                        skewed(nc.tensor.engine, (front, 1), *([(mid, 0)] if layer == 2 else []), *([(back, 0)] if layer == 0 else []))

        last0 = ctx.enter_context(nc.sbuf_tensor("last_state", [P, HID], f32))
        with phase("attention_edges") as (scope, block):
            sb, ps = maker(scope)
            idx = [sb(f"at_idx{b}", [P, T], i32) for b in range(2)]
            kv = [sb(f"at_kv{b}", [P, T, 2 * D]) for b in range(2)]
            q = [sb(f"at_q{b}", [P, T, D]) for b in range(2)]
            o = [sb(f"at_o{b}", [P, T, ROW0]) for b in range(2)]
            sc = sb("at_sc", [P, T, HEADS])
            mx = sb("at_mx", [P, T + 1, HEADS])
            dif = sb("at_dif", [P, 2, T, HEADS])
            ex = sb("at_ex", [P, 2, T, HEADS])
            s_idx = [sem(f"at_idx{b}") for b in range(2)]
            s_rows = [sem(f"at_rows{b}") for b in range(2)]
            s_free = [sem(f"at_free{b}") for b in range(2)]
            s_q = [sem(f"at_q{b}") for b in range(2)]
            s_out = [sem(f"at_out{b}") for b in range(2)]
            s_v, s_qf, s_dif, s_ex, s_o, s_turn, s_m = (sem("at_" + n) for n in ("v", "qf", "dif", "ex", "o", "turn", "m"))

            @block.sync
            def _(sp):
                def load(c, b, width=T):
                    sp.dma_start(idx[b][:, 0:width], src_v[:, ds(c * T, width)]).then_inc(s_idx[b], 16)
                    sp.dma_start(q[b][:, 0:width, :], edges(start_d)[:, ds(c * T, width), :]).then_inc(s_q[b], 16)

                def store(c, b, width=T):
                    sp.wait_ge(s_o, c * 2 + 2)
                    sp.dma_start(edges(scan_d[0])[:, ds(c * T, width), :], o[b][:, 0:width, :]).then_inc(s_out[b], 16)
                load(0, 0)
                load(1, 1)
                with nc.Fori(0, PAIRS - 1, engines=[nc.sync.engine]) as i:
                    for b in range(2):
                        sp.wait_ge(s_qf, i * 2 + b + 1)
                        load(i * 2 + b + 2, b)
                        store(i * 2 + b, b)
                sp.wait_ge(s_qf, 2 * PAIRS - 1)
                load(2 * PAIRS, 0, TAIL)
                store(2 * PAIRS - 2, 0)
                store(2 * PAIRS - 1, 1)
                store(2 * PAIRS, 0, TAIL)
                sp.wait_ge(s_out[0], 16 * (PAIRS + 1))
                sp.wait_ge(s_out[1], 16 * PAIRS)

            @block.gpsimd
            def _(pool):
                pool_gathers(pool, kv_d, idx, kv, s_idx, s_free, s_rows, s_turn)

            @block.vector
            def _(dve):
                st = Steps(dve, s_v)
                dve.sem_inc(s_free[0], 1)
                dve.sem_inc(s_free[1], 1)
                st.step(nc.vector.memset(mx[:, 0, :], -BIG))
                st.step(nc.vector.memset(o[1][:, T - 1, :], 0.0))
                setup = st.n
                st.wait()
                K = 11

                def chunk(c, i, b, width=T):
                    st = Steps(dve, s_v, c * K + setup)
                    kp = keep[:, ds(c * T, width)]
                    W = slice(0, width)
                    prev = o[1 - b][:, T - 1, :]
                    dve.wait_ge(s_q[b], i * 16 + 16)
                    for f in range(D):
                        r = nc.vector.tensor_tensor_scan(q[b][:, W, f], kp, q[b][:, W, f], qcarry[:, f:f + 1], ALU.mult, ALU.add)
                    st.link(r)
                    st.link(nc.vector.tensor_copy(qcarry[:], q[b][:, width - 1, :]))
                    dve.wait_ge(s_rows[b], i * (16 * T) + 16 * width)
                    st.link(nc.vector.tensor_tensor(q[b][:, W, :], q[b][:, W, :], kv[b][:, W, 0:D], ALU.mult))
                    st.link(nc.vector.tensor_reduce(sc[:, W, :], q[b][:, W, :].rearrange("p t (h e) -> p t h e", h=HEADS), AX.X, ALU.add))
                    nc.vector.sem_inc(s_qf, 1)
                    for h in range(HEADS):
                        r = nc.vector.tensor_tensor_scan(mx[:, 1:width + 1, h], pen[:, ds(c * T, width)], sc[:, W, h], mx[:, 0, h:h + 1], ALU.add, ALU.max)
                    st.link(r)
                    st.step(nc.vector.tensor_tensor(dif[:, 0, W, :], mx[:, 0:width, :], mx[:, 1:width + 1, :], ALU.subtract))
                    st.step(nc.vector.tensor_tensor(dif[:, 1, W, :], sc[:, W, :], mx[:, 1:width + 1, :], ALU.subtract))
                    st.wait()
                    nc.vector.tensor_scalar(dif[:, 0, W, :], dif[:, 0, W, :], 0.0, None, ALU.min).then_inc(s_dif, 1)
                    dve.wait_ge(s_ex, c * 2 + 1)
                    st.link(nc.vector.scalar_tensor_tensor(ex[:, 0, W, :], dif[:, 0, W, :], 0.0, ex[:, 0, W, :], ALU.is_ge, ALU.max))
                    st.step(nc.vector.tensor_tensor(ex[:, 0, W, :], ex[:, 0, W, :], bc(kp, 2, HEADS), ALU.mult))
                    v4 = kv[b][:, W, D:2 * D].rearrange("p t (h e) -> p t h e", h=HEADS)
                    st.step(nc.vector.tensor_tensor(v4, v4, bc(ex[:, 1, W, :], 3, D // HEADS), ALU.mult))
                    st.wait()
                    dve.wait_ge(s_out[b], i * 16)
                    for f in range(D):
                        h = f // (D // HEADS)
                        nc.vector.tensor_tensor_scan(o[b][:, W, f], ex[:, 0, W, h], kv[b][:, W, D + f], prev[:, f:f + 1], ALU.mult, ALU.add)
                    for h in range(HEADS):
                        r = nc.vector.tensor_tensor_scan(o[b][:, W, D + h], ex[:, 0, W, h], ex[:, 1, W, h], prev[:, D + h:D + h + 1], ALU.mult, ALU.add)
                    st.link(r)
                    nc.vector.sem_inc(s_o, 1)
                    nc.vector.sem_inc(s_free[b], 1)
                    dve.wait_ge(s_ex, c * 2 + 2)
                    st.n += 0
                    nc.vector.tensor_copy(mx[:, 0, :], mx[:, width, :]).then_inc(s_m, 1)
                    dve.wait_ge(s_m, c + 1)
                    assert st.n == K, st.n
                with nc.Fori(0, PAIRS, engines=[nc.vector.engine]) as i:
                    for b in range(2):
                        chunk(i * 2 + b, i, b)
                chunk(2 * PAIRS, PAIRS, 0, TAIL)
                st = Steps(dve, s_v, (2 * PAIRS + 1) * K + setup)
                st.step(nc.vector.tensor_copy(last0[:, 0:D + HEADS], o[0][:, TAIL - 1, 0:D + HEADS]))
                st.step(nc.vector.tensor_copy(last0[:, D + HEADS:ROW0], mx[:, 0, :]))

            @block.scalar
            def _(act):
                def chunk(c, i, b, width=T):
                    act.wait_ge(s_dif, c + 1)
                    nc.scalar.activation(ex[:, :, 0:width, :], dif[:, :, 0:width, :], ACT.Exp).then_inc(s_ex, 1)
                    act.wait_ge(s_out[b], i * 16)
                    nc.scalar.activation(o[b][:, 0:width, D + HEADS:ROW0], mx[:, 1:width + 1, :], ACT.Copy).then_inc(s_ex, 1)
                    act.wait_ge(s_ex, c * 2 + 2)
                    nc.scalar.sem_inc(s_o, 1)
                with nc.Fori(0, PAIRS, engines=[nc.scalar.engine]) as i:
                    for b in range(2):
                        chunk(i * 2 + b, i, b)
                chunk(2 * PAIRS, PAIRS, 0, TAIL)

        with phase("attention_boundary") as (scope, block):
            sb, ps = maker(scope)
            S = D + HEADS
            gm = sb("ab_gm", [P, HEADS])
            gmT = sb("ab_gmT", [HEADS, P])
            mT = sb("ab_mT", [HEADS, P + 1])
            mr = sb("ab_mr", [P, 2, HEADS])
            df = sb("ab_df", [P, 2, HEADS])
            ef = sb("ab_ef", [P, 2, HEADS])
            d0, d1 = sb("ab_d0", [P, S]), sb("ab_d1", [P, S])
            d0T, runT = sb("ab_d0T", [S, P]), sb("ab_runT", [S, P + 1])
            carry, rows, res = sb("ab_carry", [P, S]), sb("ab_rows", [P, ROW0]), sb("ab_res", [P, ROW0])
            pp = [ps(f"ab_p{n}", [P, 512]) for n in range(7)]
            s_v, s_t, s_e, s_g, s_s, s_m = (sem("ab_" + n) for n in ("v", "t", "e", "g", "s", "m"))
            waits = {}

            @block.vector
            def _(dve):
                st = Steps(dve, s_v)
                nc.vector.memset(rows[:], 0.0).then_inc(s_m, 1)
                st.step(nc.vector.memset(mT[:, 0:1], -BIG))
                st.step(nc.vector.memset(runT[:, 0:1], 0.0))
                st.link(nc.vector.tensor_scalar(gm[:], bc(whole[:, 0], 1, HEADS), -1.0, BIG, ALU.add, ALU.mult))
                waits["gates"] = st.n
                dve.wait_ge(s_t, 2)
                st.link(nc.vector.tensor_copy(gmT[:], pp[0][0:HEADS, 0:P]))
                st.link(nc.vector.tensor_tensor_scan(mT[:, 1:P + 1], gmT[:], pp[1][0:HEADS, 0:P], -BIG, ALU.add, ALU.max))
                waits["maxima"] = st.n
                dve.wait_ge(s_t, 4)
                st.step(nc.vector.tensor_copy(mr[:, 0, :], pp[2][:, 0:HEADS]))
                st.link(nc.vector.tensor_copy(mr[:, 1, :], pp[3][:, 0:HEADS]))
                st.step(nc.vector.tensor_tensor(df[:, 0, :], mr[:, 0, :], mr[:, 1, :], ALU.subtract))
                st.link(nc.vector.tensor_tensor(df[:, 1, :], last0[:, S:ROW0], mr[:, 1, :], ALU.subtract))
                st.link(nc.vector.tensor_scalar(df[:], df[:], 0.0, None, ALU.min))
                waits["factors"] = st.n
                dve.wait_ge(s_e, 1)
                st.link(nc.vector.tensor_scalar(ef[:, 0, :], ef[:, 0, :], whole[:, 0:1], None, ALU.mult))
                for dd, k in ((d0, 0), (d1, 1)):
                    st.step(nc.vector.tensor_copy(dd[:, 0:D].rearrange("p (h e) -> p h e", h=HEADS), bc(ef[:, k, :], 2, D // HEADS)))
                    st.step(nc.vector.tensor_copy(dd[:, D:S], ef[:, k, :]))
                st.wait()
                st.link(nc.vector.tensor_tensor(d1[:], d1[:], last0[:, 0:S], ALU.mult))
                waits["states"] = st.n
                dve.wait_ge(s_t, 6)
                st.link(nc.vector.tensor_copy(d0T[:], pp[4][0:S, 0:P]))
                st.link(nc.vector.tensor_tensor_scan(runT[:, 1:P + 1], d0T[:], pp[5][0:S, 0:P], 0.0, ALU.mult, ALU.add))
                waits["sums"] = st.n
                dve.wait_ge(s_t, 7)
                st.link(nc.vector.tensor_copy(carry[:], pp[6][:, 0:S]))
                dve.wait_ge(s_g, 16)
                st.link(nc.vector.tensor_tensor(res[:, S:ROW0], rows[:, S:ROW0], mr[:, 0, :], ALU.max))
                st.step(nc.vector.tensor_tensor(df[:, 0, :], mr[:, 0, :], res[:, S:ROW0], ALU.subtract))
                st.link(nc.vector.tensor_tensor(df[:, 1, :], rows[:, S:ROW0], res[:, S:ROW0], ALU.subtract))
                waits["merge"] = st.n
                dve.wait_ge(s_e, 2)
                for dd, k in ((d0, 0), (d1, 1)):
                    st.step(nc.vector.tensor_copy(dd[:, 0:D].rearrange("p (h e) -> p h e", h=HEADS), bc(ef[:, k, :], 2, D // HEADS)))
                    st.step(nc.vector.tensor_copy(dd[:, D:S], ef[:, k, :]))
                st.wait()
                st.step(nc.vector.tensor_tensor(d0[:], d0[:], carry[:], ALU.mult))
                st.link(nc.vector.tensor_tensor(d1[:], d1[:], rows[:, 0:S], ALU.mult))
                st.link(nc.vector.tensor_tensor(res[:, 0:S], d0[:], d1[:], ALU.add))
                nc.vector.sem_inc(s_m, 1)

            @block.tensor
            def _(pe):
                pe.wait_ge(s_v, waits["gates"])
                nc.tensor.transpose(pp[0][0:HEADS, 0:P], gm[:], ident[:]).then_inc(s_t, 1)
                nc.tensor.transpose(pp[1][0:HEADS, 0:P], last0[:, S:ROW0], ident[:]).then_inc(s_t, 1)
                pe.wait_ge(s_v, waits["maxima"])
                nc.tensor.transpose(pp[2][:, 0:HEADS], mT[:, 0:P], ident[0:HEADS, 0:HEADS]).then_inc(s_t, 1)
                nc.tensor.transpose(pp[3][:, 0:HEADS], mT[:, 1:P + 1], ident[0:HEADS, 0:HEADS]).then_inc(s_t, 1)
                pe.wait_ge(s_v, waits["states"])
                nc.tensor.transpose(pp[4][0:S, 0:P], d0[:], ident[:]).then_inc(s_t, 1)
                nc.tensor.transpose(pp[5][0:S, 0:P], d1[:], ident[:]).then_inc(s_t, 1)
                pe.wait_ge(s_v, waits["sums"])
                nc.tensor.transpose(pp[6][:, 0:S], runT[:, 0:P], ident[0:S, 0:S]).then_inc(s_t, 1)

            @block.scalar
            def _(act):
                act.wait_ge(s_v, waits["factors"])
                nc.scalar.activation(ef[:], df[:], ACT.Exp).then_inc(s_e, 1)
                act.wait_ge(s_v, waits["merge"])
                nc.scalar.activation(ef[:], df[:], ACT.Exp).then_inc(s_e, 1)

            @block.gpsimd
            def _(pool):
                pool.wait_ge(s_m, 1)
                nc.gpsimd.indirect_dma_start(rows[:], None, scan_d[0], bass.IndirectOffsetOnAxis(ap=fixidx[:, 0:1], axis=0),
                                             bounds_check=E - 1, oob_is_err=False).then_inc(s_g, 16)
                pool.wait_ge(s_m, 2)
                nc.gpsimd.indirect_dma_start(scan_d[0], bass.IndirectOffsetOnAxis(ap=fixidx[:, 0:1], axis=0), res[:], None,
                                             bounds_check=E - 1, oob_is_err=False).then_inc(s_s, 16)
                pool.wait_ge(s_s, 16)

        node_block("attention_nodes", 0, scan_d[0], ROW0, None)

        def plain_edges(name, table, scan_out, gate, op, none, degrees):
            first = ALU.mult if op == ALU.add else ALU.add
            with phase(name) as (scope, block):
                sb, ps = maker(scope)
                idx = [sb(f"{name}_idx{b}", [P, T], i32) for b in range(2)]
                rows = [sb(f"{name}_rows{b}", [P, T, D]) for b in range(2)]
                o = [sb(f"{name}_o{b}", [P, T, D]) for b in range(2)]
                s_idx = [sem(f"{name}_idx{b}") for b in range(2)]
                s_rows = [sem(f"{name}_rows{b}") for b in range(2)]
                s_free = [sem(f"{name}_free{b}") for b in range(2)]
                s_out = [sem(f"{name}_out{b}") for b in range(2)]
                s_v, s_o, s_open, s_turn = (sem(f"{name}_{n}") for n in ("v", "o", "open", "turn"))
                if degrees:
                    hi = sb("dg_hi", [P, T])
                    lo = sb("dg_lo", [P, T])
                    ohi, olo = sb("dg_ohi", [P, T, P], bf16), sb("dg_olo", [P, T, J], bf16)
                    zrow = sb("dg_zrow", [P, P], bf16)
                    p_h = ps("dg_ph", [P, 512])
                    s_oh, s_hm = sem("dg_oh"), sem("dg_hm")

                @block.sync
                def _(sp):
                    def load(c, b, width=T):
                        sp.dma_start(idx[b][:, 0:width], src_v[:, ds(c * T, width)]).then_inc(s_idx[b], 16)

                    def store(c, b, width=T):
                        sp.wait_ge(s_o, c + 1)
                        sp.dma_start(edges(scan_out)[:, ds(c * T, width), :], o[b][:, 0:width, :]).then_inc(s_out[b], 16)
                    load(0, 0)
                    load(1, 1)
                    with nc.Fori(0, PAIRS - 1, engines=[nc.sync.engine]) as i:
                        for b in range(2):
                            store(i * 2 + b, b)
                            load(i * 2 + b + 2, b)
                    store(2 * PAIRS - 2, 0)
                    load(2 * PAIRS, 0, TAIL)
                    store(2 * PAIRS - 1, 1)
                    store(2 * PAIRS, 0, TAIL)
                    sp.wait_ge(s_out[0], 16 * (PAIRS + 1))
                    sp.wait_ge(s_out[1], 16 * PAIRS)

                @block.gpsimd
                def _(pool):
                    pool_gathers(pool, table, idx, rows, s_idx, s_free, s_rows, s_turn)

                @block.vector
                def _(dve):
                    st = Steps(dve, s_v)
                    st.step(nc.vector.memset(o[1][:, T - 1, :], none))
                    if degrees:
                        st.step(nc.vector.memset(zrow[:], 0.0))
                    st.wait()
                    setup = st.n
                    dve.sem_inc(s_open, 1)
                    dve.sem_inc(s_free[0], 1)
                    dve.sem_inc(s_free[1], 1)
                    K = 6 if degrees else 1

                    def chunk(c, i, b, width=T):
                        st = Steps(dve, s_v, c * K + setup)
                        W = slice(0, width)
                        if degrees:
                            dve.wait_ge(s_idx[b], i * 16 + 16)
                            st.link(nc.vector.tensor_scalar(hi[:, W], idx[b][:, W], -(J - 1) / 2, 1.0 / J, ALU.add, ALU.mult))
                            st.link(nc.vector.tensor_scalar(hi[:, W], hi[:, W], MAGIC, -MAGIC, ALU.add, ALU.add))
                            st.link(nc.vector.scalar_tensor_tensor(lo[:, W], hi[:, W], -float(J), idx[b][:, W], ALU.mult, ALU.add))
                            dve.wait_ge(s_hm, c + 1)
                            st.step(nc.vector.tensor_tensor(ohi[:, W, :], bc(hi[:, W], 2, P), bc(iota_row[:], 1, width), ALU.is_equal))
                            st.link(nc.vector.tensor_tensor(olo[:, W, :], bc(lo[:, W], 2, J), bc(iota_row[:, 0:J], 1, width), ALU.is_equal))
                            nc.vector.sem_inc(s_oh, 1)
                        dve.wait_ge(s_rows[b], i * (16 * T) + 16 * width)
                        dve.wait_ge(s_out[b], i * 16)
                        for f in range(D):
                            r = nc.vector.tensor_tensor_scan(o[b][:, W, f], gate[:, ds(c * T, width)], rows[b][:, W, f],
                                                             o[1 - b][:, T - 1, f:f + 1], first, op)
                        st.link(r)
                        nc.vector.sem_inc(s_o, 1)
                        nc.vector.sem_inc(s_free[b], 1)
                        assert st.n == K
                    with nc.Fori(0, PAIRS, engines=[nc.vector.engine]) as i:
                        for b in range(2):
                            chunk(i * 2 + b, i, b)
                    chunk(2 * PAIRS, PAIRS, 0, TAIL)
                    base = (2 * PAIRS + 1) * K + setup
                    st = Steps(dve, s_v, base)
                    st.step(nc.vector.tensor_copy(last0[:, 0:D], o[0][:, TAIL - 1, :]))
                    if degrees:
                        dve.wait_ge(s_hm, 2 * PAIRS + 2)
                        st.link(nc.vector.tensor_scalar(nsrc[:], p_h[:, 0:J], 1.0, None, ALU.max))
                        dve.wait_ge(s_hm, 2 * PAIRS + 3)
                        st.link(nc.vector.reciprocal(nsrc[:], nsrc[:]))

                if degrees:
                    @block.tensor
                    def _(pe):
                        pe.wait_ge(s_open, 1)
                        nc.tensor.matmul(p_h[:, 0:J], zrow[:], zrow[:, 0:J], start=True, stop=False).then_inc(s_hm, 1)

                        def count(c, width=T, last=False):
                            pe.wait_ge(s_oh, c + 1)
                            for t in range(width):
                                mm = nc.tensor.matmul(p_h[:, 0:J], ohi[:, t, :], olo[:, t, :], start=False, stop=last and t == width - 1)
                            mm.then_inc(s_hm, 1)
                        with nc.Fori(0, 2 * PAIRS, engines=[nc.tensor.engine]) as c:
                            count(c)
                        count(2 * PAIRS, TAIL, True)

                    @block.scalar
                    def _(act):
                        act.wait_ge(s_v, (2 * PAIRS + 1) * 6 + 2 + 2)
                        nc.scalar.activation(nsrc[:], nsrc[:], ACT.Sqrt).then_inc(s_hm, 1)

        plain_edges("max_edges", nbr1_d, scan_d[1], pen, ALU.max, -BIG, True)
        boundary("max_boundary", last0[:, 0:D], scan_d[1], D, ALU.max, -BIG)
        node_block("max_nodes", 1, scan_d[1], D, x_d[0], own1_d)

        with phase("mlp_edges") as (scope, block):
            sb, ps = maker(scope)
            BLK = 8
            NB = -(-T // BLK)
            EK = BLK * EA
            EK1 = 64 + 1
            idx = [sb(f"ml_idx{b}", [P, T], i32) for b in range(2)]
            own = [sb(f"ml_own{b}", [P, T, D]) for b in range(2)]
            xx = [sb(f"ml_xx{b}", [P, T, 2 * D]) for b in range(2)]
            ea = [sb(f"ml_ea{b}", [P, T * EA]) for b in range(2)]
            eaT = sb("ml_eaT", [EK1, NB, P])
            wxx = sb("ml_wxx", [2 * D, HID])
            wea = sb("ml_wea", [EK1, BLK, HID])
            xT = [sb(f"ml_xT{k}", [P, BLK, P]) for k in range(2)]
            hs = [sb(f"ml_h{b}", [P, T, HID]) for b in range(2)]
            rr = sb("ml_r", [P, T, HID])
            xcarry = sb("ml_xc", [P, D])
            hcarry = sb("ml_hc", [P, HID])
            p_h = [ps(f"ml_ph{k}", [P, 2, 512]) for k in range(2)]
            p_x = ps("ml_px", [P, 2, 512])
            p_e = ps("ml_pe", [P, 2, 512])
            s_idx = [sem(f"ml_idx{b}") for b in range(2)]
            s_rows = [sem(f"ml_rows{b}") for b in range(2)]
            s_free = [sem(f"ml_free{b}") for b in range(2)]
            s_own = [sem(f"ml_own{b}") for b in range(2)]
            s_ea = [sem(f"ml_ea{b}") for b in range(2)]
            s_out = [sem(f"ml_out{b}") for b in range(2)]
            s_v, s_w, s_w2, s_c, s_sp, s_et, s_ev, s_xt, s_xe, s_ph, s_pf, s_er, s_ef, s_o, s_done, s_turn, s_first = (
                sem("ml_" + n) for n in ("v", "w", "w2", "c", "sp", "et", "ev", "xt", "xe", "ph", "pf", "er", "ef", "o", "done", "turn", "first"))

            def blocks(width):
                return [(k, min(BLK, width - k)) for k in range(0, width, BLK)]

            @block.sync
            def _(sp):
                sp.wait_ge(s_w2, 1)
                for t in range(BLK):
                    sp.dma_start(wea[t * EA:(t + 1) * EA, t, :], pw1_in[2 * D:2 * D + EA, :]).then_inc(s_w, 16)
                    sp.dma_start(wea[64:65, t, :], bc(pb1_in, 0, 1)).then_inc(s_w, 16)
                sp.dma_start(wxx[:], pw1_in[0:2 * D, :]).then_inc(s_w, 16)

                def load(c, b, width=T):
                    sp.dma_start(idx[b][:, 0:width], src_v[:, ds(c * T, width)]).then_inc(s_idx[b], 16)
                    sp.dma_start(own[b][:, 0:width, :], edges(start_d)[:, ds(c * T, width), :]).then_inc(s_own[b], 16)
                    sp.dma_start(ea[b][:, 0:width * EA], ea_v[:, ds(c * T, width), :].rearrange("p t a -> p (t a)")).then_inc(s_ea[b], 16)

                def store(c, b, width=T):
                    sp.wait_ge(s_o, c + 1)
                    sp.dma_start(edges(scan_d[2])[:, ds(c * T, width), :], hs[b][:, 0:width, :]).then_inc(s_out[b], 16)
                load(0, 0)
                load(1, 1)
                with nc.Fori(0, PAIRS - 1, engines=[nc.sync.engine]) as i:
                    for b in range(2):
                        sp.wait_ge(s_done, i * 2 + b + 1)
                        load(i * 2 + b + 2, b)
                        store(i * 2 + b, b)
                sp.wait_ge(s_done, 2 * PAIRS - 1)
                load(2 * PAIRS, 0, TAIL)
                store(2 * PAIRS - 2, 0)
                store(2 * PAIRS - 1, 1)
                store(2 * PAIRS, 0, TAIL)
                sp.wait_ge(s_out[0], 16 * (PAIRS + 1))
                sp.wait_ge(s_out[1], 16 * PAIRS)

            @block.gpsimd
            def _(pool):
                nc.gpsimd.indirect_dma_start(xcarry[:], None, x_d[1], bass.IndirectOffsetOnAxis(ap=dfirst[:, 0:1], axis=0)).then_inc(s_c, 16)
                pool_gathers(pool, x_d[1], idx, xx, s_idx, s_free, s_rows, s_turn, D)

            @block.tensor
            def _(pe):
                pe.wait_ge(s_w, 16 * (2 * BLK + 1))

                def chunk(c, i, b, blk0, width=T):
                    bl = blocks(width)

                    def transposes(n):
                        k, w = bl[n]
                        pe.wait_ge(s_xe, blk0 + n)
                        for t in range(w):
                            r = nc.tensor.transpose(p_x[:, t // 4, (t % 4) * P:(t % 4 + 1) * P], xx[b][:, k + t, :], ident[:])
                        r.then_inc(s_xt, 1)
                    pe.wait_ge(s_ea[b], i * 16 + 16)
                    pe.wait_ge(s_ph, blk0)
                    pe.sem_inc(s_turn, 1)
                    for n, (k, w) in enumerate(bl):
                        r = nc.tensor.transpose(p_e[0:w * EA, n // 4, (n % 4) * P:(n % 4 + 1) * P], ea[b][:, k * EA:(k + w) * EA], ident[:])
                    r.then_inc(s_et, 1)
                    pe.wait_ge(s_sp, c + 1)
                    pe.wait_ge(s_rows[b], i * (16 * T) + 16 * width)
                    transposes(0)
                    pe.wait_ge(s_ev, c + 1)
                    for n, (k, w) in enumerate(bl):
                        if n + 1 < len(bl):
                            transposes(n + 1)
                        else:
                            pe.wait_ge(s_xt, blk0 + len(bl))
                            pe.sem_inc(s_done, 1)
                            pe.sem_inc(s_free[b], 1)
                        par = (b * NB + n) % 2
                        ph = p_h[par]
                        pe.wait_ge(s_xe, blk0 + n + 1)
                        pe.wait_ge(s_pf, blk0 + n + 1)
                        for m in range(0, w, 4):
                            ww = min(4, w - m)
                            nc.tensor.matmul(ph[:, m // 4, 0:ww * HID], eaT[:, n, :], wea[:, m:m + ww, :].rearrange("p t f -> p (t f)"), start=True, stop=False)
                            for t in range(m, m + ww):
                                r = nc.tensor.matmul(ph[:, m // 4, (t - m) * HID:(t - m + 1) * HID], xT[par][:, t, :], wxx[:], start=False,
                                                     stop=t == m + ww - 1)
                        r.then_inc(s_ph, 1)
                with nc.Fori(0, PAIRS, engines=[nc.tensor.engine]) as i:
                    for b in range(2):
                        chunk(i * 2 + b, i, b, i * (2 * NB) + b * NB)
                chunk(2 * PAIRS, PAIRS, 0, 2 * PAIRS * NB, TAIL)

            @block.scalar
            def _(act):
                act.sem_inc(s_pf, 2)
                act.sem_inc(s_free[0], 1)
                act.sem_inc(s_free[1], 1)
                act.wait_ge(s_w2, 1)

                def chunk(c, i, b, blk0, width=T):
                    bl = blocks(width)

                    def move_x(n):
                        k, w = bl[n]
                        act.wait_ge(s_xt, blk0 + n + 1)
                        nc.scalar.activation(xT[(b * NB + n) % 2][:, 0:w, :], p_x[:].rearrange("p k n -> p (k n)")[:, 0:w * P].rearrange("p (t n) -> p t n", n=P), ACT.Copy).then_inc(s_xe, 1)
                    act.wait_ge(s_et, c + 1)
                    full = sum(w == BLK for k, w in bl)
                    flat = p_e[:].rearrange("p k n -> p (k n)")
                    r = nc.scalar.activation(eaT[0:EK, 0:full, :], flat[0:EK, 0:full * P].rearrange("p (k n) -> p k n", n=P), ACT.Copy)
                    if full < len(bl):
                        w = bl[-1][1]
                        r = nc.scalar.activation(eaT[0:w * EA, full, :], flat[0:w * EA, full * P:(full + 1) * P], ACT.Copy)
                    r.then_inc(s_ev, 1)
                    move_x(0)
                    act.wait_ge(s_out[b], i * 16)
                    for n, (k, w) in enumerate(bl):
                        par = (b * NB + n) % 2
                        if n + 1 < len(bl):
                            move_x(n + 1)
                        z = p_h[par][:].rearrange("p k n -> p (k n)")[:, 0:w * HID].rearrange("p (t f) -> p t f", f=HID)
                        act.wait_ge(s_ph, blk0 + n + 1)
                        act.wait_ge(s_ef, blk0 + n + 1)
                        nc.scalar.activation(hs[b][:, k:k + w, :], z, ACT.Exp)
                        nc.scalar.activation(rr[:, k:k + w, :], z, ACT.Relu).then_inc(s_pf, 1)
                        act.wait_ge(s_pf, blk0 + n + 3)
                        nc.scalar.activation(rr[:, k:k + w, :], rr[:, k:k + w, :], ACT.Copy, bias=-1.0).then_inc(s_er, 1)
                with nc.Fori(0, PAIRS, engines=[nc.scalar.engine]) as i:
                    for b in range(2):
                        chunk(i * 2 + b, i, b, i * (2 * NB) + b * NB)
                chunk(2 * PAIRS, PAIRS, 0, 2 * PAIRS * NB, TAIL)

            @block.vector
            def _(dve):
                st = Steps(dve, s_v)
                st.step(nc.vector.memset(wea[:], 0.0))
                st.step(nc.vector.memset(eaT[0:64], 0.0))
                st.link(nc.vector.memset(eaT[64:65, :, :], 1.0))
                dve.sem_inc(s_w2, 1)
                st.step(nc.vector.memset(hcarry[:], 0.0))
                dve.sem_inc(s_ef, NB)

                def spread(c, b, lo_f, hi_f, init):
                    for f in range(lo_f, hi_f):
                        r = nc.vector.tensor_tensor_scan(xx[b][:, :, f], keep[:, ds(c * T, T)], own[b][:, :, f], init[:, f:f + 1], ALU.mult, ALU.add)
                    return r

                K = 3
                FB = -(-D // NB)
                dve.wait_ge(s_c, 16)
                dve.wait_ge(s_own[0], 16)
                st.link(spread(0, 0, 0, D, xcarry))
                dve.sem_inc(s_sp, 1)
                setup = st.n

                def chunk(c, i, b, blk0, in_next, width=T):
                    st = Steps(dve, s_v, c * K + setup)
                    bl = blocks(width)
                    if in_next is not None:
                        dve.wait_ge(s_own[1 - b], in_next)
                    for n, (k, w) in enumerate(bl):
                        if in_next is not None and n * FB < D:
                            r = spread(c + 1, 1 - b, n * FB, min(D, (n + 1) * FB), xx[b][:, T - 1, :])
                            if (n + 1) * FB >= D:
                                st.link(r)
                                dve.sem_inc(s_sp, 1)
                        dve.wait_ge(s_er, blk0 + n + 1)
                        nc.vector.scalar_tensor_tensor(hs[b][:, k:k + w, :], hs[b][:, k:k + w, :], 1.0, rr[:, k:k + w, :], ALU.min, ALU.add).then_inc(s_ef, 1)
                    if in_next is None:
                        dve.sem_inc(s_v, 1)
                        st.n += 1
                    dve.wait_ge(s_ef, blk0 + len(bl) + NB)
                    for f in range(HID):
                        r = nc.vector.tensor_tensor_scan(hs[b][:, 0:width, f], keep[:, ds(c * T, width)], hs[b][:, 0:width, f],
                                                         hcarry[:, f:f + 1], ALU.mult, ALU.add)
                    st.link(r)
                    st.link(nc.vector.tensor_copy(hcarry[:], hs[b][:, width - 1, :]))
                    dve.sem_inc(s_o, 1)
                    assert st.n == K, st.n
                with nc.Fori(0, PAIRS, engines=[nc.vector.engine]) as i:
                    chunk(i * 2, i, 0, i * (2 * NB), i * 16 + 16)
                    chunk(i * 2 + 1, i, 1, i * (2 * NB) + NB, i * 16 + 32)
                chunk(2 * PAIRS, PAIRS, 0, 2 * PAIRS * NB, None, TAIL)
                nc.vector.tensor_copy(last0[:], hcarry[:]).then_inc(s_v, 1)

        boundary("mlp_boundary", last0[:], scan_d[2], HID, ALU.add, 0.0)
        node_block("mlp_nodes", 2, scan_d[2], HID, x_d[1])

        plain_edges("gcn_edges", feat_d, scan_d[3], keep, ALU.add, 0.0, False)
        boundary("gcn_boundary", last0[:, 0:D], scan_d[3], D, ALU.add, 0.0)
        node_block("gcn_nodes", 3, scan_d[3], D, x_d[2])


_INS = ['x', 'src', 'dst', 'edge_attr_6', 'L0_gnn_Wq', 'L0_gnn_Wk', 'L0_gnn_Wv', 'L0_gnn_Wo', 'L1_gnn_W', 'L1_gnn_b',
        'L2_gnn_phi_w1', 'L2_gnn_phi_b1', 'L2_gnn_phi_w2', 'L2_gnn_phi_b2', 'L2_gnn_g_w1', 'L2_gnn_g_b1',
        'L2_gnn_g_w2', 'L2_gnn_g_b2', 'L3_gnn_W']


def kernel(**inputs):
    import numpy as _np
    import concourse.bacc as _bacc
    from concourse import mybir as _mybir
    from concourse.bass_utils import run_bass_kernel_spmd as _run

    nc = _bacc.Bacc("TRN2", target_bir_lowering=False, num_devices=1)
    arrays, ap = {}, {}
    for name in _INS:
        a = _np.asarray(inputs[name])
        if name == 'L1_gnn_W':
            a = a.T
        a = _np.ascontiguousarray(a)
        arrays["in_" + name] = a
        ap[name] = nc.dram_tensor("in_" + name, a.shape, _mybir.dt.from_np(a.dtype), kind="ExternalInput").ap()
    out = nc.dram_tensor("out_0", inputs['x'].shape, _mybir.dt.from_np(_np.dtype('float32')), kind="ExternalOutput").ap()
    build(nc, ap['x'], ap['src'], ap['dst'], ap['edge_attr_6'], (ap['L0_gnn_Wk'], ap['L0_gnn_Wv'], ap['L0_gnn_Wq']),
          ap['L0_gnn_Wo'], ap['L1_gnn_W'], ap['L1_gnn_b'], ap['L2_gnn_phi_w1'], ap['L2_gnn_phi_b1'], ap['L2_gnn_phi_w2'],
          ap['L2_gnn_phi_b2'], ap['L2_gnn_g_w1'], ap['L2_gnn_g_b1'], ap['L2_gnn_g_w2'], ap['L2_gnn_g_b2'], ap['L3_gnn_W'], out)
    r = _run(nc, [arrays], core_ids=[0])
    return r.results[0]["out_0"]
```
